# Optimizing a Trainium2 kernel written in Bass

```python
import numpy as np
import jax
import jax.numpy as jnp

def _softmax(x, axis=-1):
    return jax.nn.softmax(x, axis=axis)

def _gelu(x):
    return jax.nn.gelu(x, approximate=True)

def _silu(x):
    return jax.nn.silu(x)

def _sigmoid(x):
    return jax.nn.sigmoid(x)

def _layernorm(x, axis=-1, eps=1e-05):
    m = jnp.mean(x, axis=axis, keepdims=True)
    v = jnp.var(x, axis=axis, keepdims=True)
    return (x - m) / jnp.sqrt(v + eps)

def _scatter_add(tgt, idx, src, axis=0):
    return tgt.at[idx].add(src)

def _segment_sum(src, seg, n):
    return jax.ops.segment_sum(src, seg, n)
kernel_name = 'mk_conv_preact_d4_conv_nhwc768_r4_c496a2'

def setup_inputs(seed: int=0):
    np.random.seed(seed)
    _w = jnp.asarray

    def _rec_inputs():
        import jax
        import jax.numpy as jnp
        _gk = jax.random.key(seed)
        x = 7.572e-06 + 1 * jax.random.normal(jax.random.fold_in(_gk, 1), (16, 14, 14, 192), jnp.float32)
        return x
    x = _rec_inputs()

    def _L0_conv_setup():
        import jax, jax.numpy as jnp
        import numpy as np
        B, H, W, C = (16, 14, 14, 192)
        key = jax.random.key(seed)
        k = jax.random.split(key, 5)
        s = 0.02
        return {'x': jax.random.normal(k[0], (B, H, W, C), dtype=jnp.float32), 'Wx': jax.random.normal(k[1], (3 * C, C), dtype=jnp.float32) * s, 'bx': jnp.zeros((3 * C,), dtype=jnp.float32), 'Wh': jax.random.normal(k[2], (3 * C, C), dtype=jnp.float32) * s, 'bh': jnp.zeros((3 * C,), dtype=jnp.float32), 'Wp': jax.random.normal(k[3], (C, C), dtype=jnp.float32) * s}
    _L0_conv_all = _L0_conv_setup()
    _L0_conv_in = {k: v for k, v in _L0_conv_all.items() if k in ('Wx', 'bx', 'Wh', 'bh', 'Wp')}
    del _L0_conv_all

    def _L1_conv_setup():
        import jax, jax.numpy as jnp
        import numpy as np
        NUM_HEADS = 12

        def _rel_table(size, rel_pos):
            coords = jnp.arange(size)[:, None] - jnp.arange(size)[None, :] + (size - 1)
            return rel_pos[coords]
        key = jax.random.key(seed)
        ks = jax.random.split(key, 7)
        B, H, W, C = (1, 16, 16, 192)
        hd = C // NUM_HEADS
        return {'x': jax.random.normal(ks[0], (B, H, W, C), dtype=jnp.float32), 'qkv_w': jax.random.normal(ks[1], (C, 3 * C), dtype=jnp.float32) * 0.02, 'qkv_b': jax.random.normal(ks[2], (3 * C,), dtype=jnp.float32) * 0.02, 'proj_w': jax.random.normal(ks[3], (C, C), dtype=jnp.float32) * 0.02, 'proj_b': jax.random.normal(ks[4], (C,), dtype=jnp.float32) * 0.02, 'rel_pos_h': jax.random.normal(ks[5], (2 * H - 1, hd), dtype=jnp.float32) * 0.02, 'rel_pos_w': jax.random.normal(ks[6], (2 * W - 1, hd), dtype=jnp.float32) * 0.02}
    _L1_conv_all = _L1_conv_setup()
    _L1_conv_in = {k: v for k, v in _L1_conv_all.items() if k in ('qkv_w', 'qkv_b', 'proj_w', 'proj_b', 'rel_pos_h', 'rel_pos_w')}
    del _L1_conv_all

    def _L2_conv_setup():
        import jax, jax.numpy as jnp
        import numpy as np
        N_EXPERTS = 8
        TOP_K = 2
        HIDDEN = 192
        INTER = 512

        def _gelu(h):
            return jax.nn.gelu(h, approximate=False)
        key = jax.random.key(seed)
        ks = jax.random.split(key, 12)
        s_in = 1.0 / np.sqrt(HIDDEN)
        s_mid = 1.0 / np.sqrt(INTER)
        return {'x': jax.random.normal(ks[0], (4, 16, 16, HIDDEN), dtype=jnp.float32), 'gate_w': jax.random.normal(ks[1], (N_EXPERTS, HIDDEN), dtype=jnp.float32), 'fc1_w': jax.random.uniform(ks[2], (N_EXPERTS, INTER, HIDDEN), jnp.float32, -s_in, s_in), 'fc1_b': jax.random.uniform(ks[3], (N_EXPERTS, INTER), jnp.float32, -s_in, s_in), 'fc2_w': jax.random.uniform(ks[4], (N_EXPERTS, HIDDEN, INTER), jnp.float32, -s_mid, s_mid), 'fc2_b': jax.random.uniform(ks[5], (N_EXPERTS, HIDDEN), jnp.float32, -s_mid, s_mid), 'w1_w': jax.random.uniform(ks[6], (INTER, HIDDEN), jnp.float32, -s_in, s_in), 'w1_b': jax.random.uniform(ks[7], (INTER,), jnp.float32, -s_in, s_in), 'w3_w': jax.random.uniform(ks[8], (INTER, HIDDEN), jnp.float32, -s_in, s_in), 'w3_b': jax.random.uniform(ks[9], (INTER,), jnp.float32, -s_in, s_in), 'w2_w': jax.random.uniform(ks[10], (HIDDEN, INTER), jnp.float32, -s_mid, s_mid), 'w2_b': jax.random.uniform(ks[11], (HIDDEN,), jnp.float32, -s_mid, s_mid)}
    _L2_conv_all = _L2_conv_setup()
    _L2_conv_in = {k: v for k, v in _L2_conv_all.items() if k in ('gate_w', 'fc1_w', 'fc1_b', 'fc2_w', 'fc2_b', 'w1_w', 'w1_b', 'w3_w', 'w3_b', 'w2_w', 'w2_b')}
    del _L2_conv_all

    def _L3_conv_setup():
        import jax, jax.numpy as jnp
        import numpy as np
        B, H, W, C, NH = (100, 14, 14, 192, 12)
        HD = C // NH

        def _get_rel_pos(q_size, k_size, rel_pos):
            coords = jnp.arange(q_size)[:, None] - jnp.arange(k_size)[None, :] + (k_size - 1)
            return rel_pos[coords]
        key = jax.random.key(seed)
        ks = jax.random.split(key, 6)
        s = 0.02
        return {'hidden_states': jax.random.normal(ks[0], (B, H, W, C), jnp.float32), 'qkv_w': jax.random.normal(ks[1], (3 * C, C), jnp.float32) * s, 'qkv_b': jnp.zeros((3 * C,), jnp.float32), 'proj_w': jax.random.normal(ks[2], (C, C), jnp.float32) * s, 'proj_b': jnp.zeros((C,), jnp.float32), 'rel_pos_h': jax.random.normal(ks[3], (2 * H - 1, HD), jnp.float32) * s, 'rel_pos_w': jax.random.normal(ks[4], (2 * W - 1, HD), jnp.float32) * s}
    _L3_conv_all = _L3_conv_setup()
    _L3_conv_in = {k: v for k, v in _L3_conv_all.items() if k in ('qkv_w', 'qkv_b', 'proj_w', 'proj_b', 'rel_pos_h', 'rel_pos_w')}
    del _L3_conv_all
    return {'x': x, 'L0_conv_Wx': _L0_conv_in['Wx'], 'L0_conv_bx': _L0_conv_in['bx'], 'L0_conv_Wh': _L0_conv_in['Wh'], 'L0_conv_bh': _L0_conv_in['bh'], 'L0_conv_Wp': _L0_conv_in['Wp'], 'L1_conv_qkv_w': _L1_conv_in['qkv_w'], 'L1_conv_qkv_b': _L1_conv_in['qkv_b'], 'L1_conv_proj_w': _L1_conv_in['proj_w'], 'L1_conv_proj_b': _L1_conv_in['proj_b'], 'L1_conv_rel_pos_h': _L1_conv_in['rel_pos_h'], 'L1_conv_rel_pos_w': _L1_conv_in['rel_pos_w'], 'L2_conv_gate_w': _L2_conv_in['gate_w'], 'L2_conv_fc1_w': _L2_conv_in['fc1_w'], 'L2_conv_fc1_b': _L2_conv_in['fc1_b'], 'L2_conv_fc2_w': _L2_conv_in['fc2_w'], 'L2_conv_fc2_b': _L2_conv_in['fc2_b'], 'L2_conv_w1_w': _L2_conv_in['w1_w'], 'L2_conv_w1_b': _L2_conv_in['w1_b'], 'L2_conv_w3_w': _L2_conv_in['w3_w'], 'L2_conv_w3_b': _L2_conv_in['w3_b'], 'L2_conv_w2_w': _L2_conv_in['w2_w'], 'L2_conv_w2_b': _L2_conv_in['w2_b'], 'L3_conv_qkv_w': _L3_conv_in['qkv_w'], 'L3_conv_qkv_b': _L3_conv_in['qkv_b'], 'L3_conv_proj_w': _L3_conv_in['proj_w'], 'L3_conv_proj_b': _L3_conv_in['proj_b'], 'L3_conv_rel_pos_h': _L3_conv_in['rel_pos_h'], 'L3_conv_rel_pos_w': _L3_conv_in['rel_pos_w']}

def reference(x, L0_conv_Wx, L0_conv_bx, L0_conv_Wh, L0_conv_bh, L0_conv_Wp, L1_conv_qkv_w, L1_conv_qkv_b, L1_conv_proj_w, L1_conv_proj_b, L1_conv_rel_pos_h, L1_conv_rel_pos_w, L2_conv_gate_w, L2_conv_fc1_w, L2_conv_fc1_b, L2_conv_fc2_w, L2_conv_fc2_b, L2_conv_w1_w, L2_conv_w1_b, L2_conv_w3_w, L2_conv_w3_b, L2_conv_w2_w, L2_conv_w2_b, L3_conv_qkv_w, L3_conv_qkv_b, L3_conv_proj_w, L3_conv_proj_b, L3_conv_rel_pos_h, L3_conv_rel_pos_w):
    import jax
    import jax.numpy as jnp

    def _L0_conv_ref(x, Wx, bx, Wh, bh, Wp):
        import jax, jax.numpy as jnp
        import numpy as np
        B, H, W, C = (16, 14, 14, 192)
        b, h_, w_, c = x.shape
        n = h_ * w_
        seq = x.reshape(b, n, c)
        x_zrn = jnp.einsum('bnc,dc->bnd', seq, Wx) + bx
        x_zrn_t = jnp.transpose(x_zrn, (1, 0, 2))

        def step(h, xz):
            h_zrn = h @ Wh.T + bh
            x_z, x_r, x_n = jnp.split(xz, 3, axis=-1)
            h_z, h_r, h_n = jnp.split(h_zrn, 3, axis=-1)
            z = jax.nn.sigmoid(x_z + h_z)
            r = jax.nn.sigmoid(x_r + h_r)
            ncand = jnp.tanh(x_n + r * h_n)
            h_new = (1.0 - z) * ncand + z * h
            return (h_new, h_new)
        h0 = jnp.zeros((b, c), dtype=x.dtype)
        _, hs = jax.lax.scan(step, h0, x_zrn_t)
        y = jnp.transpose(hs, (1, 0, 2))
        y = jnp.einsum('bnc,dc->bnd', y, Wp)
        return y.reshape(b, h_, w_, c)

    def _L1_conv_ref(x, qkv_w, qkv_b, proj_w, proj_b, rel_pos_h, rel_pos_w):
        import jax, jax.numpy as jnp
        import numpy as np
        NUM_HEADS = 12

        def _rel_table(size, rel_pos):
            coords = jnp.arange(size)[:, None] - jnp.arange(size)[None, :] + (size - 1)
            return rel_pos[coords]
        B, H, W, C = x.shape
        nh = NUM_HEADS
        hd = C // nh
        scale = hd ** (-0.5)
        N = H * W
        qkv = x.reshape(B, N, C) @ qkv_w + qkv_b
        qkv = qkv.reshape(B, N, 3, nh, hd).transpose(2, 0, 3, 1, 4).reshape(3, B * nh, N, hd)
        q, k, v = (qkv[0], qkv[1], qkv[2])
        attn = jnp.einsum('bqd,bkd->bqk', q * scale, k)
        Rh = _rel_table(H, rel_pos_h)
        Rw = _rel_table(W, rel_pos_w)
        qr = q.reshape(B * nh, H, W, hd)
        rel_h = jnp.einsum('bhwc,hkc->bhwk', qr, Rh)
        rel_w = jnp.einsum('bhwc,wkc->bhwk', qr, Rw)
        bias = rel_h[..., :, None] + rel_w[..., None, :]
        attn = attn + bias.reshape(B * nh, N, N)
        attn = jax.nn.softmax(attn, axis=-1)
        out = jnp.einsum('bqk,bkd->bqd', attn, v)
        out = out.reshape(B, nh, H, W, hd).transpose(0, 2, 3, 1, 4).reshape(B, H, W, C)
        return out @ proj_w + proj_b

    def _L2_conv_ref(x, gate_w, fc1_w, fc1_b, fc2_w, fc2_b, w1_w, w1_b, w3_w, w3_b, w2_w, w2_b):
        import jax, jax.numpy as jnp
        import numpy as np
        N_EXPERTS = 8
        TOP_K = 2
        HIDDEN = 192
        INTER = 512

        def _gelu(h):
            return jax.nn.gelu(h, approximate=False)
        B, H, W, C = x.shape
        xf = x.reshape(-1, C)
        scores = jax.nn.softmax(xf @ gate_w.T, axis=-1)
        top_v, top_i = jax.lax.top_k(scores, TOP_K)
        top_v = top_v / jnp.sum(top_v, axis=-1, keepdims=True)
        out = jnp.zeros_like(xf)
        for e in range(N_EXPERTS):
            w_e = jnp.sum(jnp.where(top_i == e, top_v, 0.0), axis=-1)
            h = _gelu(xf @ fc1_w[e].T + fc1_b[e])
            y = h @ fc2_w[e].T + fc2_b[e]
            out = out + w_e[:, None] * y
        shared = _gelu(xf @ w1_w.T + w1_b) * (xf @ w3_w.T + w3_b) @ w2_w.T + w2_b
        return (out + shared).reshape(B, H, W, C)

    def _L3_conv_ref(hidden_states, qkv_w, qkv_b, proj_w, proj_b, rel_pos_h, rel_pos_w):
        import jax, jax.numpy as jnp
        import numpy as np
        B, H, W, C, NH = (100, 14, 14, 192, 12)
        HD = C // NH

        def _get_rel_pos(q_size, k_size, rel_pos):
            coords = jnp.arange(q_size)[:, None] - jnp.arange(k_size)[None, :] + (k_size - 1)
            return rel_pos[coords]
        b, h, w, c = hidden_states.shape
        scale = HD ** (-0.5)
        qkv = hidden_states.reshape(b, h * w, c) @ qkv_w.T + qkv_b
        qkv = qkv.reshape(b, h * w, 3, NH, HD).transpose(2, 0, 3, 1, 4)
        q, k, v = (qkv[0], qkv[1], qkv[2])
        Rh = _get_rel_pos(h, h, rel_pos_h)
        Rw = _get_rel_pos(w, w, rel_pos_w)
        qr = q.reshape(b, NH, h, w, HD)
        rel_h = jnp.einsum('bnhwc,hkc->bnhwk', qr, Rh)
        rel_w = jnp.einsum('bnhwc,wkc->bnhwk', qr, Rw)
        bias = (rel_h[..., :, None] + rel_w[..., None, :]).reshape(b, NH, h * w, h * w)
        attn = jnp.einsum('bnqd,bnkd->bnqk', q, k) * scale + bias
        attn = jax.nn.softmax(attn, axis=-1)
        out = jnp.einsum('bnqk,bnkd->bnqd', attn, v)
        out = out.transpose(0, 2, 1, 3).reshape(b, h, w, c)
        return out @ proj_w.T + proj_b

    def _gn(v, G=32, eps=1e-05):
        B_, H_, W_, C_ = v.shape
        g = v.reshape(B_, H_, W_, G, C_ // G)
        m = jnp.mean(g, axis=(1, 2, 4), keepdims=True)
        s = jnp.var(g, axis=(1, 2, 4), keepdims=True)
        return ((g - m) / jnp.sqrt(s + eps)).reshape(v.shape)

    def _ln_c(v, eps=1e-06):
        m = jnp.mean(v, axis=-1, keepdims=True)
        s = jnp.var(v, axis=-1, keepdims=True)
        return (v - m) / jnp.sqrt(s + eps)

    def _ln_t(v, eps=1e-05):
        m = jnp.mean(v, axis=-1, keepdims=True)
        s = jnp.var(v, axis=-1, keepdims=True)
        return (v - m) / jnp.sqrt(s + eps)

    def _to_tokens(v):
        B_, H_, W_, C_ = v.shape
        return v.reshape(B_, H_ * W_, C_)

    def _from_tokens(t, like):
        return t.reshape(like.shape)
    x = x + _L0_conv_ref(_gn(x), L0_conv_Wx, L0_conv_bx, L0_conv_Wh, L0_conv_bh, L0_conv_Wp)
    x = x + _L1_conv_ref(_gn(x), L1_conv_qkv_w, L1_conv_qkv_b, L1_conv_proj_w, L1_conv_proj_b, L1_conv_rel_pos_h, L1_conv_rel_pos_w)
    x = x + _L2_conv_ref(_gn(x), L2_conv_gate_w, L2_conv_fc1_w, L2_conv_fc1_b, L2_conv_fc2_w, L2_conv_fc2_b, L2_conv_w1_w, L2_conv_w1_b, L2_conv_w3_w, L2_conv_w3_b, L2_conv_w2_w, L2_conv_w2_b)
    x = x + _L3_conv_ref(_gn(x), L3_conv_qkv_w, L3_conv_qkv_b, L3_conv_proj_w, L3_conv_proj_b, L3_conv_rel_pos_h, L3_conv_rel_pos_w)
    return x

_drawn_inputs = setup_inputs


def setup_inputs(seed=0):
    import zlib

    import numpy as np

    out = dict(_drawn_inputs(seed))
    spreads = {'L0_conv_bx': (0.0, 0.276),
     'L0_conv_bh': (0.0, 0.507),
     'L3_conv_qkv_b': (0.0, 0.309),
     'L3_conv_proj_b': (0.0, 0.1)}
    factors = {'L0_conv_Wh': 8.0,
     'L1_conv_qkv_w': 8.0,
     'L1_conv_qkv_b': 8.0,
     'L1_conv_proj_w': 6.111,
     'L1_conv_proj_b': 7.837,
     'L1_conv_rel_pos_h': 8.0,
     'L1_conv_rel_pos_w': 8.0,
     'L2_conv_fc1_b': 4.147,
     'L2_conv_w1_b': 6.812,
     'L2_conv_w3_b': 7.163,
     'L3_conv_qkv_w': 8.0,
     'L3_conv_rel_pos_h': 8.0,
     'L3_conv_rel_pos_w': 8.0,
     'L2_conv_fc2_b': 6.142,
     'L2_conv_w2_b': 5.867}
    for name, (base, spread) in spreads.items():
        noise = np.random.default_rng([zlib.crc32(name.encode()), seed]).standard_normal(out[name].shape)
        drawn = base * np.exp(spread * noise) if base else spread * noise
        out[name] = jnp.asarray(drawn.astype(out[name].dtype))
    for name, factor in factors.items():
        out[name] = (out[name] * factor).astype(out[name].dtype)
    return out
```

```python
import numpy as np
import concourse.bass as bass
from concourse import mybir
from contextlib import ExitStack

f32, f32r = mybir.dt.float32, mybir.dt.float32r
bf16, fp16 = mybir.dt.bfloat16, mybir.dt.float16
ALU = mybir.AluOpType
ACT = mybir.ActivationFunctionType
AXIS = mybir.AxisListType

B, H, W, C = 16, 14, 14, 192
T = H * W
N = B * T
CP, CB = 96, 2
HEADS, HD = 12, 16
PAIRS = HEADS // 2
G, GC = 32, C // 32
E, F = 8, 512
FB = F // 128
TB = 2 * T
NT = N // TB
TH = T // 2
HSCALE = 2048.0
EPS = 1e-5
NEG = -3.0e38


class Scope:

    def __init__(self, nc, tag):
        self.nc, self.tag, self.stack, self.sems = nc, tag, ExitStack(), []

    def __enter__(self):
        self.stack.__enter__()
        return self

    def __exit__(self, *e):
        if self.sems:
            self.nc.clear_and_free_semaphores(self.sems)
            self.nc.all_engine_barrier()
        return self.stack.__exit__(*e)

    def sb(self, name, shape, dt=f32):
        return self.stack.enter_context(self.nc.sbuf_tensor(f"{self.tag}_{name}", shape, dt))

    def ps(self, name, banks=1):
        return self.stack.enter_context(self.nc.psum_tensor(f"{self.tag}_{name}", [128, banks, 512], f32))

    def sem(self, name):
        self.sems.append(self.nc.alloc_semaphore(f"{self.tag}_{name}"))
        return self.sems[-1]


def load_x(nc, tag, x_dram, x_sb):
    with Scope(nc, tag) as s:
        loaded = s.sem("loaded")
        with nc.Block() as block:
            @block.sync
            def _(sp):
                sp.dma_start(x_sb[:, :, :], x_dram).then_inc(loaded, 16)
                sp.wait_ge(loaded, 16)


def norm(nc, tag, x_sb, group_avg, xh, xl):
    with Scope(nc, tag) as s:
        stats = s.sb("stats", [CP, CB, B, 6])
        mv = s.sb("mv", [CP, CB, B, 2])
        dev = s.sb("dev", [CP, CB, B])
        spread = s.sb("spread", [CP, CB, B])
        mean_g = s.sb("mean_g", [CP, CB, B])
        std = s.sb("std", [CP, CB, B])
        rstd = s.sb("rstd", [CP, CB, B])
        shift = s.sb("shift", [CP, CB, B])
        avg = s.sb("avg", [CP, CP])
        eps = s.sb("eps", [CP, 1])
        xn = s.sb("xn", [CP, 4, T])
        ps_mean, ps_var = s.ps("ps_mean"), s.ps("ps_var")
        avg_in, chan, chan2 = s.sem("avg_in"), s.sem("chan"), s.sem("chan2")
        mean_ready, var_ready, mean_copied = s.sem("mean_ready"), s.sem("var_ready"), s.sem("mean_copied")
        dev_ready, dev2, spread_ready = s.sem("dev_ready"), s.sem("dev2"), s.sem("spread_ready")
        std_ready, rstd_ready, shift_ready = s.sem("std_ready"), s.sem("rstd_ready"), s.sem("shift_ready")
        xn_ready, xh_ready, xl_ready = s.sem("xn_ready"), s.sem("xh_ready"), s.sem("xl_ready")
        eps_ready = s.sem("eps_ready")
        with nc.Block() as block:
            @block.sync
            def _(sp):
                sp.dma_start(avg[:, :], group_avg).then_inc(avg_in, 16)

            @block.vector
            def _(dve):
                dve.memset(eps[:, :], EPS).then_inc(eps_ready, 1)
                for k in range(CB):
                    for b in range(B):
                        dve.bn_stats(stats[:, k, b, :], x_sb[:, k, b * T:(b + 1) * T]).then_inc(chan, 1)
                dve.wait_ge(chan, CB * B)
                for k in range(CB):
                    for b in range(B):
                        dve.bn_aggr(mv[:, k, b, :], stats[:, k, b, :]).then_inc(chan2, 1)
                dve.wait_ge(mean_ready, 1)
                dve.tensor_copy(mean_g[:, :, :].rearrange("p k b -> p (k b)"), ps_mean[:CP, 0, :CB * B]).then_inc(mean_copied, 1)
                dve.wait_ge(mean_copied, 1)
                dve.tensor_tensor(dev[:, :, :], mv[:, :, :, 0], mean_g[:, :, :], ALU.subtract).then_inc(dev_ready, 1)
                dve.wait_ge(dev_ready, 1)
                dve.tensor_tensor(spread[:, :, :], dev[:, :, :], dev[:, :, :], ALU.mult).then_inc(dev2, 1)
                dve.wait_ge(dev2, 1)
                dve.tensor_tensor(spread[:, :, :], spread[:, :, :], mv[:, :, :, 1], ALU.add).then_inc(spread_ready, 1)
                dve.wait_ge(std_ready, 1)
                dve.reciprocal(rstd[:, :, :], std[:, :, :]).then_inc(rstd_ready, 1)
                dve.wait_ge(rstd_ready, 1)
                dve.scalar_tensor_tensor(shift[:, :, :].rearrange("p k b -> p (k b)"), mean_g[:, :, :].rearrange("p k b -> p (k b)"), -1.0,
                                         rstd[:, :, :].rearrange("p k b -> p (k b)"), ALU.mult, ALU.mult).then_inc(shift_ready, 1)
                dve.wait_ge(shift_ready, 1)
                tiles = [(k, b) for b in range(B) for k in range(CB)]

                def low(n):
                    k, b = tiles[n]
                    dve.wait_ge(xh_ready, n + 1)
                    dve.wait_ge(xn_ready, n + 1)
                    dve.tensor_tensor(xl[:, k, b * T:(b + 1) * T], xn[:, n % 4, :],
                                      xh[:, k, b * T:(b + 1) * T].bitcast(f32), ALU.subtract).then_inc(xl_ready, 1)

                for n, (k, b) in enumerate(tiles):
                    if n >= 4:
                        dve.wait_ge(xl_ready, n - 3)
                    dve.tensor_scalar(xn[:, n % 4, :], x_sb[:, k, b * T:(b + 1) * T], rstd[:, k, b:b + 1],
                                      shift[:, k, b:b + 1], ALU.mult, ALU.add).then_inc(xn_ready, 1)
                    if n >= 2:
                        low(n - 2)
                low(len(tiles) - 2)
                low(len(tiles) - 1)
                dve.wait_ge(xl_ready, len(tiles))

            @block.tensor
            def _(pe):
                pe.wait_ge(avg_in, 16)
                pe.wait_ge(chan2, CB * B)
                pe.matmul(ps_mean[:CP, 0, :CB * B], avg[:, :], mv[:, :, :, 0], start=True, stop=True).then_inc(mean_ready, 1)
                pe.wait_ge(spread_ready, 1)
                pe.matmul(ps_var[:CP, 0, :CB * B], avg[:, :], spread[:, :, :], start=True, stop=True).then_inc(var_ready, 1)

            @block.scalar
            def _(act):
                act.wait_ge(eps_ready, 1)
                act.wait_ge(var_ready, 1)
                act.activation(std[:, :, :].rearrange("p k b -> p (k b)"), ps_var[:CP, 0, :CB * B], ACT.Sqrt,
                               bias=eps[:, :]).then_inc(std_ready, 1)
                act.wait_ge(shift_ready, 1)
                for b in range(B):
                    for k in range(CB):
                        act.activation(xh[:, k, b * T:(b + 1) * T], x_sb[:, k, b * T:(b + 1) * T], ACT.Identity,
                                       scale=rstd[:, k, b:b + 1], bias=shift[:, k, b:b + 1]).then_inc(xh_ready, 1)
                act.wait_ge(xh_ready, B * CB)


def split(eng, whole, high, low, high_ready, low_ready, count):
    eng.tensor_copy(high, whole).then_inc(high_ready, 1)
    eng.wait_ge(high_ready, count + 1)
    eng.tensor_tensor(low, whole, high.bitcast(f32), ALU.subtract).then_inc(low_ready, 1)


def product3(pe, out, wh, wl, xh, xl, start=True, stop=True, blocks=CB):
    terms = [(w, x, k) for k in range(blocks) for w, x in ((wh, xh), (wl, xh), (wh, xl))]
    for n, (w, x, k) in enumerate(terms):
        last = pe.matmul(out, w(k), x(k), start=start and n == 0, stop=stop and n == len(terms) - 1)
    return last


def gru_inputs(nc, xh, xl, wx_dram, bx_dram, bh_dram, gates_in, cand_in):
    with Scope(nc, "gi") as s:
        w = s.sb("w", [CP, CB, 6, 128])
        wh = s.sb("wh", [CP, CB, 6, 128], f32r)
        wl = s.sb("wl", [CP, CB, 6, 128], f32r)
        bx, bh, bias, bias_s = s.sb("bx", [128, 6]), s.sb("bh", [128, 6]), s.sb("bias", [128, 6]), s.sb("bias_s", [128, 6])
        whole = s.sb("whole", [128, 2, TB])
        rest = s.sb("rest", [128, 2, TB])
        rest2 = s.sb("rest2", [128, 2, TB])
        ps = s.ps("ps", 4)
        loaded, wh_ready, wl_ready = s.sem("loaded"), s.sem("wh_ready"), s.sem("wl_ready")
        bias_ready, biass_ready = s.sem("bias_ready"), s.sem("biass_ready")
        summed, moved, cand_ready = s.sem("summed"), s.sem("moved"), s.sem("cand_ready")
        p0, r1, p1, r2, p2 = s.sem("p0"), s.sem("r1"), s.sem("p1"), s.sem("r2"), s.sem("p2")

        def view(x):
            return x.rearrange("p (b t) -> p t b", b=2)

        with nc.Block() as block:
            @block.sync
            def _(sp):
                sp.dma_start(w[:, :, :, :], wx_dram).then_inc(loaded, 16)
                sp.dma_start(bx[:, :], bx_dram).then_inc(loaded, 16)
                sp.dma_start(bh[:, :], bh_dram).then_inc(loaded, 16)

            @block.tensor
            def _(pe):
                pe.wait_ge(wl_ready, 1)
                for n in range(NT):
                    for j in range(6):
                        i = n * 6 + j
                        if i >= 4:
                            pe.wait_ge(moved, i - 3)
                        product3(pe, ps[:, i % 4, :TB], lambda k: wh[:, k, j, :], lambda k: wl[:, k, j, :],
                                 lambda k: xh[:, k, n * TB:(n + 1) * TB],
                                 lambda k: xl[:, k, n * TB:(n + 1) * TB]).then_inc(summed, 1)

            @block.scalar
            def _(act):
                act.wait_ge(biass_ready, 1)
                for n in range(NT):
                    for j in range(6):
                        i, g = n * 6 + j, n * 4 + j
                        act.wait_ge(summed, i + 1)
                        if j < 4:
                            if g >= 2:
                                act.wait_ge(p2, g - 1)
                            act.activation(whole[:, g % 2, :], ps[:, i % 4, :TB], ACT.Identity, scale=HSCALE,
                                           bias=bias_s[:, j:j + 1]).then_inc(moved, 1)
                        else:
                            act.activation(cand_in[:, :, j - 4, 2 * n:2 * n + 2], view(ps[:, i % 4, :TB]), ACT.Identity,
                                           bias=bias[:, j:j + 1]).then_inc(moved, 1)
                act.wait_ge(moved, 6 * NT)

            @block.vector
            def _(dve):
                dve.wait_ge(loaded, 48)
                split(dve, w[:, :, :, :], wh[:, :, :, :], wl[:, :, :, :], wh_ready, wl_ready, 0)
                dve.tensor_tensor(bias[:, 0:4], bx[:, 0:4], bh[:, 0:4], ALU.add).then_inc(bias_ready, 1)
                dve.tensor_copy(bias[:, 4:6], bx[:, 4:6]).then_inc(bias_ready, 1)
                dve.wait_ge(bias_ready, 2)
                dve.tensor_scalar(bias_s[:, :], bias[:, :], HSCALE, None, ALU.mult).then_inc(biass_ready, 1)
                for n in range(NT):
                    for j in range(4):
                        g = n * 4 + j
                        dst = [gates_in[:, :, p, j, 2 * n:2 * n + 2] for p in range(3)]
                        dve.wait_ge(moved, n * 6 + j + 1)
                        dve.tensor_copy(dst[0], view(whole[:, g % 2, :])).then_inc(p0, 1)
                        dve.wait_ge(p0, g + 1)
                        dve.tensor_tensor(view(rest[:, g % 2, :]), view(whole[:, g % 2, :]), dst[0], ALU.subtract).then_inc(r1, 1)
                        dve.wait_ge(r1, g + 1)
                        dve.tensor_copy(dst[1], view(rest[:, g % 2, :])).then_inc(p1, 1)
                        dve.wait_ge(p1, g + 1)
                        dve.tensor_tensor(dst[2], view(rest[:, g % 2, :]), dst[1], ALU.subtract).then_inc(p2, 1)
                dve.wait_ge(p2, NT * 4)


def gru(nc, gates_in, cand_in, state, wh_dram, bhn_dram, ident_dram):
    STEPS = 14
    with Scope(nc, "gru") as s:
        w = s.sb("w", [128, CB, 3, 2, 128])
        wp = s.sb("wp", [128, 5, 3, 2, 128], bf16)
        wr = s.sb("wr", [128, CB, 3, 2, 128])
        ident32, ident = s.sb("ident32", [128, 128]), s.sb("ident", [128, 128], bf16)
        bhn, bhs = s.sb("bhn", [128, 2]), s.sb("bhs", [128, 2, B])
        bp, br = s.sb("bp", [128, 3, 2, B], bf16), s.sb("br", [128, 2, B])
        hp = s.sb("hp", [128, 2, 2, 2 * B], fp16)
        names = "tr tz zs zc rn cand n keep new".split()
        tr, tz, zs, zc, rn, cand, tn, keep, new = (s.sb(n, [128, 2, 2 * B]) for n in names)
        ps_r, ps_n, ps_z = s.ps("ps_r", 2), s.ps("ps_n", 2), s.ps("ps_z", 2)
        loaded, prep, weights_ready = s.sem("loaded"), s.sem("prep"), s.sem("weights_ready")
        hi_ready, lo_ready, h_ready = s.sem("hi_ready"), s.sem("lo_ready"), s.sem("h_ready")
        r_summed, n_summed, z_summed = s.sem("r_summed"), s.sem("n_summed"), s.sem("z_summed")
        tr_ready, tz_ready, tn_ready = s.sem("tr_ready"), s.sem("tz_ready"), s.sem("tn_ready")
        zs_ready, zc_ready, rn_ready = s.sem("zs_ready"), s.sem("zc_ready"), s.sem("rn_ready")
        cand_ready, keep_ready, new_ready = s.sem("cand_ready"), s.sem("keep_ready"), s.sem("new_ready")

        def two(x):
            return x.rearrange("p (k b) -> p k b", k=2)

        with nc.Block() as block:
            @block.sync
            def _(sp):
                sp.dma_start(w[:, :, :, :, :], wh_dram).then_inc(loaded, 16)
                sp.dma_start(ident32[:, :], ident_dram).then_inc(loaded, 16)
                sp.dma_start(bhn[:, :], bhn_dram).then_inc(loaded, 16)

            @block.vector
            def _(dve):
                step = [0]

                def link(ins):
                    step[0] += 1
                    ins.then_inc(prep, 1)
                    dve.wait_ge(prep, step[0])

                dve.memset(state[:, 0, :, :], 0.0).then_inc(h_ready, 1)
                dve.memset(hp[:, 0, 0, :], 0.0).then_inc(hi_ready, 1)
                dve.memset(hp[:, 0, 1, :], 0.0).then_inc(lo_ready, 1)
                dve.wait_ge(loaded, 48)
                link(dve.tensor_copy(wp[:, 0], w[:, 0]))
                link(dve.tensor_tensor(wr[:, 0], w[:, 0], wp[:, 0], ALU.subtract))
                link(dve.tensor_copy(wp[:, 1], wr[:, 0]))
                link(dve.tensor_tensor(wp[:, 2], wr[:, 0], wp[:, 1], ALU.subtract))
                link(dve.tensor_copy(wp[:, 3], w[:, 1]))
                link(dve.tensor_tensor(wr[:, 1], w[:, 1], wp[:, 3], ALU.subtract))
                link(dve.tensor_copy(wp[:, 4], wr[:, 1]))
                link(dve.tensor_copy(wp[64:128, 3], wp[64:128, 4]))
                link(dve.tensor_tensor(wr[:, 0], wr[:, 1], wp[:, 4], ALU.subtract))
                link(dve.tensor_copy(wp[:, 4], wr[:, 0]))
                link(dve.memset(wp[64:128, 4], 0.0))
                for k in range(2):
                    link(dve.memset(bhs[:, k, :], HSCALE))
                    link(dve.tensor_scalar(bhs[:, k, :], bhs[:, k, :], bhn[:, k:k + 1], None, ALU.mult))
                link(dve.tensor_copy(bp[:, 0], bhs[:, :, :]))
                link(dve.tensor_tensor(br[:, :, :], bhs[:, :, :], bp[:, 0], ALU.subtract))
                link(dve.tensor_copy(bp[:, 1], br[:, :, :]))
                link(dve.tensor_tensor(bp[:, 2], br[:, :, :], bp[:, 1], ALU.subtract))
                dve.tensor_copy(ident[:, :], ident32[:, :]).then_inc(weights_ready, 1)
                with dve.Fori(0, T // STEPS) as it:
                    for u in range(STEPS):
                        t, b = it * STEPS + u, u % 2
                        dve.wait_ge(tr_ready, t + 1)
                        dve.wait_ge(n_summed, t + 1)
                        dve.scalar_tensor_tensor(rn[:, b, :], tr[:, b, :], 1.0, ps_n[:, b, :2 * B], ALU.add, ALU.mult).then_inc(rn_ready, 1)
                        dve.wait_ge(rn_ready, t + 1)
                        dve.scalar_tensor_tensor(two(cand[:, b, :]), two(rn[:, b, :]), 0.5 / HSCALE, cand_in[:, t, :, :],
                                                 ALU.mult, ALU.add).then_inc(cand_ready, 1)
                        dve.wait_ge(tz_ready, t + 1)
                        dve.tensor_scalar(zs[:, b, :], tz[:, b, :], 0.5, 0.5, ALU.mult, ALU.add).then_inc(zs_ready, 1)
                        dve.tensor_scalar(zc[:, b, :], tz[:, b, :], -0.5 * HSCALE, 0.5 * HSCALE, ALU.mult, ALU.add).then_inc(zc_ready, 1)
                        dve.wait_ge(zs_ready, t + 1)
                        dve.wait_ge(h_ready, t + 1)
                        dve.tensor_tensor(two(keep[:, b, :]), two(zs[:, b, :]), state[:, t, :, :], ALU.mult).then_inc(keep_ready, 1)
                        dve.wait_ge(zc_ready, t + 1)
                        dve.wait_ge(tn_ready, t + 1)
                        dve.tensor_tensor(new[:, b, :], zc[:, b, :], tn[:, b, :], ALU.mult).then_inc(new_ready, 1)
                        dve.wait_ge(keep_ready, t + 1)
                        dve.wait_ge(new_ready, t + 1)
                        dve.tensor_tensor(hp[:, 1 - b, 0, :], new[:, b, :], keep[:, b, :], ALU.add).then_inc(hi_ready, 1)
                        dve.tensor_tensor(state[:, t + 1, :, :], two(new[:, b, :]), two(keep[:, b, :]), ALU.add).then_inc(h_ready, 1)
                        dve.wait_ge(hi_ready, t + 2)
                        dve.wait_ge(h_ready, t + 2)
                        dve.tensor_tensor(two(hp[:, 1 - b, 1, :]), state[:, t + 1, :, :], two(hp[:, 1 - b, 0, :]),
                                          ALU.subtract).then_inc(lo_ready, 1)

            @block.tensor
            def _(pe):
                HIGH = [(0, 0), (1, 0), (2, 0), (3, 1), (4, 1)]
                LOW = [(0, 0), (1, 0), (3, 1)]

                def gate(out, g, b, part, terms):
                    for m in range(2):
                        for wi, k in terms:
                            last = pe.matmul(out[:, B * m:B * m + B], wp[:, wi, g, m, :], hp[:, b, part, B * k:B * k + B],
                                             start=False, stop=True, skip_group_check=True)
                    return last

                pe.wait_ge(weights_ready, 1)
                with pe.Fori(0, T // STEPS) as it:
                    for u in range(STEPS):
                        t, b = it * STEPS + u, u % 2
                        for p in range(3):
                            pe.matmul(ps_r[:, b, :2 * B], ident[:, :], gates_in[:, t, p, 2:4, :], start=p == 0, stop=p == 2, skip_group_check=True)
                            pe.matmul(ps_n[:, b, :2 * B], ident[:, :], bp[:, p, :, :], start=p == 0, stop=p == 2, skip_group_check=True)
                            pe.matmul(ps_z[:, b, :2 * B], ident[:, :], gates_in[:, t, p, 0:2, :], start=p == 0, stop=p == 2, skip_group_check=True)
                        pe.wait_ge(hi_ready, t + 1)
                        gate(ps_r[:, b, :], 1, b, 0, HIGH)
                        pe.wait_ge(lo_ready, t + 1)
                        gate(ps_r[:, b, :], 1, b, 1, LOW).then_inc(r_summed, 1)
                        gate(ps_n[:, b, :], 2, b, 0, HIGH)
                        gate(ps_n[:, b, :], 2, b, 1, LOW).then_inc(n_summed, 1)
                        gate(ps_z[:, b, :], 0, b, 0, HIGH)
                        gate(ps_z[:, b, :], 0, b, 1, LOW).then_inc(z_summed, 1)

            @block.scalar
            def _(act):
                with act.Fori(0, T // STEPS) as it:
                    for u in range(STEPS):
                        t, b = it * STEPS + u, u % 2
                        act.wait_ge(r_summed, t + 1)
                        act.activation(tr[:, b, :], ps_r[:, b, :2 * B], ACT.Tanh, scale=0.5 / HSCALE).then_inc(tr_ready, 1)
                        act.wait_ge(z_summed, t + 1)
                        act.activation(tz[:, b, :], ps_z[:, b, :2 * B], ACT.Tanh, scale=0.5 / HSCALE).then_inc(tz_ready, 1)
                        act.wait_ge(cand_ready, t + 1)
                        act.activation(tn[:, b, :], cand[:, b, :], ACT.Tanh).then_inc(tn_ready, 1)


def gru_out(nc, state, wp_dram, x_sb, x_dram):
    with Scope(nc, "go") as s:
        w = s.sb("w", [128, 2, CB, CP])
        ps = s.ps("ps", 4)
        loaded, summed, added, stored = s.sem("loaded"), s.sem("summed"), s.sem("added"), s.sem("stored")
        with nc.Block() as block:
            @block.sync
            def _(sp):
                sp.dma_start(w[:, 0, :, :], wp_dram[0:128]).then_inc(loaded, 16)
                sp.dma_start(w[0:64, 1, :, :], wp_dram[128:192]).then_inc(loaded, 16)
                for n in range(NT):
                    sp.wait_ge(added, 2 * n + 2)
                    sp.dma_start(x_dram[:, :, n * TB:(n + 1) * TB], x_sb[:, :, n * TB:(n + 1) * TB]).then_inc(stored, 16)
                sp.wait_ge(stored, 16 * NT)

            @block.tensor
            def _(pe):
                pe.wait_ge(loaded, 32)
                for n in range(NT):
                    for m in range(CB):
                        i = 2 * n + m
                        if i >= 4:
                            pe.wait_ge(added, i - 3)
                        for k, rows in ((0, 128), (1, 64)):
                            last = pe.matmul(ps[:CP, i % 4, :TB], w[:rows, k, m, :],
                                             state[:rows, 1:T + 1, k, 2 * n:2 * n + 2].rearrange("p t b -> p b t"),
                                             start=k == 0, stop=k == 1)
                        last.then_inc(summed, 1)

            @block.vector
            def _(dve):
                for n in range(NT):
                    for m in range(CB):
                        i = 2 * n + m
                        dve.wait_ge(summed, i + 1)
                        x = x_sb[:, m, n * TB:(n + 1) * TB]
                        dve.scalar_tensor_tensor(x, ps[:CP, i % 4, :TB], 1.0 / HSCALE, x, ALU.mult, ALU.add).then_inc(added, 1)


def gru_layer(nc, ins, x_in, y_out):
    with Scope(nc, "l0") as s:
        x_sb = s.sb("x", [CP, CB, N])
        load_x(nc, "l0x", x_in, x_sb)
        with Scope(nc, "l0g") as s3:
            gates_in = s3.sb("gates_in", [128, T, 3, 4, B], bf16)
            cand_in = s3.sb("cand_in", [128, T, 2, B])
            with Scope(nc, "l0n") as s2:
                xh, xl = s2.sb("xh", [CP, CB, N], f32r), s2.sb("xl", [CP, CB, N], f32r)
                norm(nc, "n0", x_sb, ins["group_avg"], xh, xl)
                gru_inputs(nc, xh, xl, ins["wx"], ins["bx"], ins["bh"], gates_in, cand_in)
            with Scope(nc, "l0s") as s2:
                state = s2.sb("state", [128, T + 1, 2, B])
                gru(nc, gates_in, cand_in, state, ins["wh"], ins["bhn"], ins["ident128"])
                gru_out(nc, state, ins["wp"], x_sb, y_out)


def values(nc, tag, xh, xl, wv_dram, bv_dram, v):
    with Scope(nc, tag) as s:
        w = s.sb("w", [CP, CB, C])
        wh, wl = s.sb("wh", [CP, CB, C], f32r), s.sb("wl", [CP, CB, C], f32r)
        bias = s.sb("bias", [128, C])
        ps = s.ps("ps", 4)
        loaded, wh_ready, wl_ready = s.sem("loaded"), s.sem("wh_ready"), s.sem("wl_ready")
        summed, added = s.sem("summed"), s.sem("added")
        with nc.Block() as block:
            @block.sync
            def _(sp):
                sp.dma_start(w[:, :, :], wv_dram).then_inc(loaded, 16)
                sp.dma_start(bias[:TH, :], bv_dram).then_inc(loaded, 16)

            @block.tensor
            def _(pe):
                pe.wait_ge(wl_ready, 1)
                for i in range(2 * B):
                    if i >= 4:
                        pe.wait_ge(added, i - 3)
                    tok = slice(i * TH, (i + 1) * TH)
                    product3(pe, ps[:TH, i % 4, :C], lambda k: xh[:, k, tok], lambda k: xl[:, k, tok],
                             lambda k: wh[:, k, :], lambda k: wl[:, k, :]).then_inc(summed, 1)

            @block.vector
            def _(dve):
                dve.wait_ge(loaded, 32)
                split(dve, w[:, :, :], wh[:, :, :], wl[:, :, :], wh_ready, wl_ready, 0)
                for i in range(2 * B):
                    dve.wait_ge(summed, i + 1)
                    dve.tensor_tensor(v[:TH, i, :], ps[:TH, i % 4, :C], bias[:TH, :], ALU.add).then_inc(added, 1)
                dve.wait_ge(added, 2 * B)


def attention(nc, tag, xh, xl, v, w_dram, b_dram, signs_dram, rel_dram, sel1_dram, sel2_dram, ident_dram, heads_out):
    with Scope(nc, tag) as s:
        q1 = s.sb("q1", [128, N], f32r)
        q2 = s.sb("q2", [128, N], f32r)
        k1, k2 = s.sb("k1", [128, N], f32r), s.sb("k2", [128, N], f32r)
        rel = s.sb("rel", [128, N], f32r)
        vs = s.sb("vs", [128, 2 * B, 2, 33], f32r)
        w = s.sb("w", [CP, CB, 128])
        wh, wl = s.sb("wh", [CP, CB, 128], f32r), s.sb("wl", [CP, CB, 128], f32r)
        bias, bias2 = s.sb("bias", [128, 1]), s.sb("bias2", [128, 2])
        signs = s.sb("signs", [128, 2])
        rw = s.sb("rw", [128, H + W, 28])
        rh, rl = s.sb("rh", [128, H + W, 28], f32r), s.sb("rl", [128, H + W, 28], f32r)
        ident = s.sb("ident", [128, TH])
        hx, xx = s.sb("hx", [128, 2, TB], f32r), s.sb("xx", [128, 2, TB])
        mx = s.sb("mx", [128, 2, 4])
        mt = s.sb("mt", [128, 2, 128])
        p32, ph, pl = s.sb("p32", [128, 2, 2, TB]), s.sb("ph", [128, 2, 2, TB], f32r), s.sb("pl", [128, 2, TB], f32r)
        o = s.sb("o", [33, 2, 2, T])
        flag = s.sb("flag", [1, 1])
        sel = s.sb("sel", [128, 2, T])
        ps = s.ps("ps", 8)
        S_BANK, X_BANK, T_BANK, O_BANK = 0, 2, 3, 7

        loaded, const_ready, zeroed = s.sem("loaded"), s.sem("const_ready"), s.sem("zeroed")
        rh_ready, rl_ready, w_in, wh_ready, wl_ready = (s.sem(n) for n in ("rh_ready", "rl_ready", "w_in", "wh_ready", "wl_ready"))
        bias_ready, vh_ready, vl_ready, qk_summed = (s.sem(n) for n in ("bias_ready", "vh_ready", "vl_ready", "qk_summed"))
        hx_ready, xx_ready, d_ready, q2_zero, k_moved = (s.sem(n) for n in ("hx_ready", "xx_ready", "d_ready", "q2_zero", "k_moved"))
        rel_summed, rel_high, rel_low, rel_moved = (s.sem(n) for n in ("rel_summed", "rel_high", "rel_low", "rel_moved"))
        s_summed, mx_ready, mh_ready, ml_ready = (s.sem(n) for n in ("s_summed", "mx_ready", "mh_ready", "ml_ready"))
        x_ready, x_copied, t_summed, p_ready = (s.sem(n) for n in ("x_ready", "x_copied", "t_summed", "p_ready"))
        pl_ready, o_summed, o_ready = (s.sem(n) for n in ("pl_ready", "o_summed", "o_ready"))
        o_stored = [s.sem("even_stored"), s.sem("odd_stored")]
        pair_free = s.sem("pair_free")

        def two(x):
            return x.rearrange("p (h k) -> p h k", h=2)

        with nc.Block() as block:
            @block.sync
            def _(sp):
                sp.dma_start(signs[:, :], signs_dram).then_inc(loaded, 16)
                sp.dma_start(rw[:, :, :], rel_dram).then_inc(loaded, 16)
                sp.dma_start(ident[:TH, :], ident_dram).then_inc(loaded, 16)
                sp.dma_start(sel[:, 0, :], sel1_dram).then_inc(loaded, 16)
                sp.dma_start(sel[:, 1, :], sel2_dram).then_inc(loaded, 16)
                sp.wait_ge(const_ready, 2 * B)
                with sp.Fori(0, PAIRS) as p:
                    sp.wait_ge(pair_free, p + 1)
                    sp.dma_start(w[:, :, :], w_dram[bass.ds(p, 1)].rearrange("a p k n -> (a p) k n")).then_inc(w_in, 16)
                    sp.dma_start(bias[:, :], b_dram[bass.ds(p, 1)].rearrange("a p k -> (a p) k")).then_inc(w_in, 16)
                    sp.wait_ge(d_ready, p * NT + NT)
                    sp.wait_ge(q2_zero, p * 2 + 4)
                    for r in (0, 64):
                        for dst, at, src in ((k1, 0, 32), (k1, 16, 32), (k2, 16, 48), (q2, 16, 0)):
                            sp.dma_start(dst[r + at:r + at + 16, :].bitcast(f32),
                                         q1[r + src:r + src + 16, :].bitcast(f32)).then_inc(k_moved, 16)
                    sp.wait_ge(k_moved, p * 128 + 128)
                    sp.wait_ge(rel_low, p * 14 + 14)
                    for r, head in ((0, 0), (64, 14)):
                        for dst, low in ((q1, 0), (q2, 64)):
                            for at, part in ((32, 0), (46, 32)):
                                src = low + part + head
                                sp.dma_start(dst[r + at:r + at + 14, :].bitcast(f32),
                                             rel[src:src + 14, :].bitcast(f32)).then_inc(rel_moved, 16)
                    for b in range(B):
                        sp.wait_ge(o_ready, p * B + b + 1)
                        sp.dma_start(heads_out[bass.ds(p, 1), :, :, b * T:(b + 1) * T].rearrange("a r h n -> (a r) h n"),
                                     o[:, b % 2, :, :]).then_inc(o_stored[b % 2], 16)
                for slot in range(2):
                    sp.wait_ge(o_stored[slot], PAIRS * 8 * B)

            @block.gpsimd
            def _(pool):
                pool.memset(mt[:, :, :], 0.0).then_inc(zeroed, 1)
                pool.memset(vs[:, :, :, 32:33].bitcast(f32), 1.0).then_inc(zeroed, 1)
                pool.memset(q2[:, :].bitcast(f32), 0.0).then_inc(q2_zero, 1)
                pool.memset(flag[:, :], 0.0).then_inc(q2_zero, 1)
                pool.wait_ge(loaded, 80)
                split(pool, rw[:, :, :], rh[:, :, :], rl[:, :, :], rh_ready, rl_ready, 0)
                pool.wait_ge(rl_ready, 1)
                with pool.Fori(0, PAIRS) as p:
                    for t in range(NT):
                        pool.wait_ge(hx_ready, p * NT + t + 1)
                        pool.wait_ge(xx_ready, p * NT + t + 1)
                        pool.tensor_tensor(q1[:, t * TB:(t + 1) * TB], xx[:, t % 2, :], hx[:, t % 2, :].bitcast(f32),
                                           ALU.subtract).then_inc(d_ready, 1)
                    for b in range(B):
                        g = p * B + b
                        pool.wait_ge(p_ready, 2 * g + 2)
                        if b >= 1:
                            pool.wait_ge(o_summed, g)
                        pool.tensor_tensor(pl[:TH, :, :], p32[:TH, b % 2, :, :], ph[:TH, b % 2, :, :].bitcast(f32),
                                           ALU.subtract).then_inc(pl_ready, 1)

            @block.tensor
            def _(pe):
                pe.wait_ge(zeroed, 2)
                pe.wait_ge(rl_ready, 1)
                with pe.Fori(0, PAIRS) as p:
                    pe.wait_ge(pair_free, p + 1)
                    pe.wait_ge(wl_ready, p + 1)
                    for t in range(NT):
                        if t >= 4:
                            pe.wait_ge(xx_ready, p * NT + t - 3)
                        product3(pe, ps[:, t % 4, :TB], lambda k: wh[:, k, :], lambda k: wl[:, k, :],
                                 lambda k: xh[:, k, t * TB:(t + 1) * TB],
                                 lambda k: xl[:, k, t * TB:(t + 1) * TB]).then_inc(qk_summed, 1)
                    pe.wait_ge(d_ready, p * NT + NT)
                    q4 = q1[:, :].rearrange("p (b h w) -> p h w b", b=B, h=H)
                    for j in range(14):
                        if j >= 4:
                            pe.wait_ge(rel_low, p * 14 + j - 3)
                        for u in range(2):
                            n = 2 * j + u
                            qs = q4[:, n, :, :].rearrange("p w b -> p b w") if n < H else q4[:, :, n - H, :].rearrange("p h b -> p b h")
                            out = ps[:28, 4 + j % 4, u * 224:u * 224 + 224]
                            pe.matmul(out, rh[:, n, :], qs, start=True, stop=False)
                            last = pe.matmul(out, rl[:, n, :], qs, start=False, stop=True)
                        last.then_inc(rel_summed, 1)

                    def logits_by_query(b):
                        if b == 0:
                            pe.wait_ge(k_moved, p * 128 + 128)
                            pe.wait_ge(rel_moved, p * 128 + 128)
                            pe.wait_ge(vl_ready, p + 1)
                        else:
                            pe.wait_ge(mx_ready, p * B + b)
                        keys = slice(b * T, (b + 1) * T)
                        for head in range(2):
                            r = slice(64 * head, 64 * head + 64)
                            for half in range(2):
                                out = ps[:TH, S_BANK + head, half * T:half * T + T]
                                q = slice(b * T + half * TH, b * T + (half + 1) * TH)
                                pe.matmul(out, q1[r, q], k1[r, keys], start=True, stop=False)
                                last = pe.matmul(out, q2[r, q], k2[r, keys], start=False, stop=True)
                        last.then_inc(s_summed, 1)

                    def maxima_to_rows(b):
                        pe.wait_ge(ml_ready, p * B + b + 1)
                        if b >= 1:
                            pe.wait_ge(x_copied, 2 * (p * B + b))
                        for half in range(2):
                            last = pe.transpose(ps[:, X_BANK, half * TH:half * TH + TH], mt[:TH, half, :], ident[:TH, :])
                        last.then_inc(x_ready, 1)

                    def logits_by_key(b):
                        pe.wait_ge(x_copied, 2 * (p * B + b) + 2)
                        if b >= 2:
                            pe.wait_ge(p_ready, 2 * (p * B + b) - 2)
                        q = slice(b * T, (b + 1) * T)
                        for head in range(2):
                            r = slice(64 * head, 64 * head + 64)
                            for half in range(2):
                                out = ps[:TH, T_BANK + 2 * (b % 2) + head, half * T:half * T + T]
                                keys = slice(b * T + half * TH, b * T + (half + 1) * TH)
                                pe.matmul(out, k1[r, keys], q1[r, q], start=True, stop=False)
                                last = pe.matmul(out, k2[r, keys], q2[r, q], start=False, stop=True)
                        last.then_inc(t_summed, 1)

                    def weigh_values(b):
                        pe.wait_ge(pl_ready, p * B + b + 1)
                        if b >= 1:
                            pe.wait_ge(o_ready, p * B + b)
                        for head in range(2):
                            for half in range(2):
                                lhs = vs[:TH, 2 * b + half, head, :]
                                out = ps[:33, O_BANK, head * T:head * T + T]
                                pe.matmul(out, lhs, ph[:TH, b % 2, head, half * T:half * T + T], start=half == 0, stop=False)
                                last = pe.matmul(out, lhs, pl[:TH, head, half * T:half * T + T], start=False, stop=half == 1)
                        last.then_inc(o_summed, 1)

                    for i in range(B + 3):
                        if i < B:
                            logits_by_query(i)
                        if i >= 3:
                            weigh_values(i - 3)
                        if 1 <= i <= B:
                            logits_by_key(i - 1)
                        if i < B:
                            maxima_to_rows(i)

            @block.scalar
            def _(act):
                act.wait_ge(loaded, 80)
                with act.Fori(0, PAIRS) as p:
                    act.wait_ge(bias_ready, 2 * p + 2)
                    for t in range(NT):
                        act.wait_ge(qk_summed, p * NT + t + 1)
                        if t >= 2:
                            act.wait_ge(d_ready, p * NT + t - 1)
                        act.activation(hx[:, t % 2, :], ps[:, t % 4, :TB], ACT.Identity, scale=signs[:, 0:1],
                                       bias=bias2[:, 0:1]).then_inc(hx_ready, 1)
                        act.activation(xx[:, t % 2, :], ps[:, t % 4, :TB], ACT.Identity, scale=signs[:, 1:2],
                                       bias=bias2[:, 1:2]).then_inc(xx_ready, 1)
                    for j in range(14):
                        act.wait_ge(rel_summed, p * 14 + j + 1)
                        act.activation(rel_out(rel, j, 0), rel_in(ps, j), ACT.Copy).then_inc(rel_high, 1)
                    for b in range(B + 1):
                        if b < B:
                            act.wait_ge(x_ready, p * B + b + 1)
                            cols = slice(b * T, (b + 1) * T)
                            act.activation(q2[0:2, cols], ps[0:2, X_BANK, :T], ACT.Copy).then_inc(x_copied, 1)
                            act.activation(q2[64:66, cols], ps[64:66, X_BANK, :T], ACT.Copy).then_inc(x_copied, 1)
                        if b >= 1:
                            c = b - 1
                            act.wait_ge(t_summed, p * B + c + 1)
                            if c >= 2:
                                act.wait_ge(o_summed, p * B + c - 1)
                                act.wait_ge(pl_ready, p * B + c - 1)
                            banks = ps[:TH, T_BANK + 2 * (c % 2):T_BANK + 2 * (c % 2) + 2, :TB]
                            act.activation(ph[:TH, c % 2, :, :], banks, ACT.Exp).then_inc(p_ready, 1)
                            act.activation(p32[:TH, c % 2, :, :], banks, ACT.Exp).then_inc(p_ready, 1)

            @block.vector
            def _(dve):
                dve.wait_ge(q2_zero, 2)
                dve.tensor_copy(flag[:, :], flag[:, :]).then_inc(pair_free, 1)
                dve.wait_ge(loaded, 80)
                for b in range(B):
                    for n, k in enumerate((k1, k2)):
                        dve.tensor_copy(k[:, b * T:(b + 1) * T], sel[:, n, :]).then_inc(const_ready, 1)
                dve.wait_ge(zeroed, 2)
                with dve.Fori(0, PAIRS) as p:
                    dve.memset(q2[0:2, :].bitcast(f32), 0.0).then_inc(q2_zero, 1)
                    dve.memset(q2[64:66, :].bitcast(f32), 0.0).then_inc(q2_zero, 1)
                    dve.wait_ge(w_in, 32 * p + 32)
                    dve.tensor_copy(wh[:, :, :], w[:, :, :]).then_inc(wh_ready, 1)
                    for k in range(2):
                        dve.tensor_tensor(bias2[:, k:k + 1], bias[:, :], signs[:, k:k + 1], ALU.mult).then_inc(bias_ready, 1)
                    dve.wait_ge(wh_ready, p + 1)
                    dve.tensor_tensor(wl[:, :, :], w[:, :, :], wh[:, :, :].bitcast(f32), ALU.subtract).then_inc(wl_ready, 1)
                    vp = v[:TH, :, bass.ds(p * 32, 32)].rearrange("t i (h d) -> t i h d", h=2)
                    vhi, vlo = vs[:TH, :, :, 0:HD], vs[:TH, :, :, HD:2 * HD]
                    dve.tensor_copy(vhi, vp).then_inc(vh_ready, 1)
                    dve.wait_ge(vh_ready, p + 1)
                    dve.tensor_tensor(vlo, vp, vhi.bitcast(f32), ALU.subtract).then_inc(vl_ready, 1)
                    for j in range(14):
                        dve.wait_ge(rel_high, p * 14 + j + 1)
                        dve.tensor_tensor(rel_out(rel, j, 64), rel_in(ps, j), rel_out(rel, j, 0).bitcast(f32),
                                          ALU.subtract).then_inc(rel_low, 1)
                    for b in range(B + 3):
                        if b < B:
                            g = p * B + b
                            dve.wait_ge(s_summed, g + 1)
                            dve.tensor_reduce(mx[:TH, b % 2, :], ps[:TH, S_BANK:S_BANK + 2, :TB].rearrange("p c (h k) -> p c h k", h=2),
                                              AXIS.X, ALU.max).then_inc(mx_ready, 1)
                            m = mx[:TH, b % 2, :].rearrange("p (c h) -> p h c", c=2)
                            high, low = mt[:TH, :, 0:65:64], mt[:TH, :, 1:66:64]
                            dve.wait_ge(mx_ready, g + 1)
                            if b >= 1:
                                dve.wait_ge(x_ready, g)
                            dve.tensor_copy(high.bitcast(f32r), m).then_inc(mh_ready, 1)
                            dve.wait_ge(mh_ready, g + 1)
                            dve.tensor_tensor(low, m, high, ALU.subtract).then_inc(ml_ready, 1)
                        if b >= 3:
                            c = b - 3
                            g = p * B + c
                            dve.wait_ge(o_summed, g + 1)
                            if c >= 2:
                                dve.wait_ge(o_stored[c % 2], 8 * B * p + 16 * (c // 2))
                            dve.tensor_copy(o[:, c % 2, :, :], two(ps[:33, O_BANK, :TB])).then_inc(o_ready, 1)
                    for slot in range(2):
                        dve.wait_ge(o_stored[slot], 8 * B * p + 8 * B)
                    dve.tensor_copy(flag[:, :], flag[:, :]).then_inc(pair_free, 1)


def rel_in(ps, j):
    return ps[:28, 4 + j % 4, :448].rearrange("p (u b w) -> p u b w", u=2, b=B)


def rel_out(rel, j, low):
    part = 0 if j < 7 else 32
    n = 2 * (j % 7)
    tile = rel[low + part:low + part + 28, :].rearrange("p (b h w) -> p h b w", b=B, h=H)
    return tile[:, n:n + 2, :, :] if j < 7 else tile.rearrange("p h b w -> p w b h")[:, n:n + 2, :, :]


def project(nc, tag, heads_out, sums, w_dram, b_dram, x_dram, y_dram):
    KC = HEADS * 32 // 128
    with Scope(nc, tag) as s:
        w = s.sb("w", [128, KC, CB, CP])
        bias = s.sb("bias", [CP, CB])
        den, rec = s.sb("den", [128, HEADS * N // 128]), s.sb("rec", [128, HEADS * N // 128])
        hin, rin = s.sb("hin", [128, 2, KC, TB]), s.sb("rin", [128, 2, KC, TB])
        hn = s.sb("hn", [128, 2, KC, TB])
        xin = s.sb("xin", [CP, 2, CB, TB])
        y = s.sb("y", [CP, 2, CB, TB])
        ps = s.ps("ps", 4)
        loaded, den_in, rec_ready, rec_stored = (s.sem(n) for n in ("loaded", "den_in", "rec_ready", "rec_stored"))
        summed, added, scaled = s.sem("summed"), s.sem("added"), s.sem("scaled")
        stored = [s.sem("even_stored"), s.sem("odd_stored")]
        slot_in = [s.sem("even_in"), s.sem("odd_in")]
        LOADS = 2 * HEADS + 1
        with nc.Block() as block:
            @block.sync
            def _(sp):
                for p in range(PAIRS):
                    sp.dma_start(sums[2 * p:2 * p + 2, :], heads_out[p, 32, :, :]).then_inc(den_in, 16)
                sp.wait_ge(den_in, 16 * PAIRS)
                sp.dma_start(den[:, :], sums.rearrange("h n -> (h n)").rearrange("(p f) -> p f", p=128)).then_inc(den_in, 16)
                sp.dma_start(w[:, :, :, :], w_dram).then_inc(loaded, 16)
                sp.dma_start(bias[:, :], b_dram).then_inc(loaded, 16)
                sp.wait_ge(rec_ready, 1)
                sp.dma_start(sums.rearrange("h n -> (h n)").rearrange("(p f) -> p f", p=128), rec[:, :]).then_inc(rec_stored, 16)
                sp.wait_ge(rec_stored, 16)
                for n in range(NT + 1):
                    cols = slice(n * TB, (n + 1) * TB)
                    if n < NT:
                        if n >= 2:
                            sp.wait_ge(added, 2 * n - 2)
                        for h in range(HEADS):
                            rows, k = slice(32 * (h % 4), 32 * (h % 4) + 32), h // 4
                            sp.dma_start(hin[rows, n % 2, k, :], heads_out[h // 2, 0:32, h % 2, cols]).then_inc(slot_in[n % 2], 16)
                            sp.dma_start(rin[rows, n % 2, k, :], sums[h:h + 1, cols].to_broadcast([32, TB])).then_inc(slot_in[n % 2], 16)
                        sp.dma_start(xin[:, n % 2, :, :], x_dram[:, :, cols]).then_inc(slot_in[n % 2], 16)
                    if n >= 1:
                        sp.wait_ge(added, 2 * n)
                        sp.dma_start(y_dram[:, :, (n - 1) * TB:n * TB], y[:, (n - 1) % 2, :, :]).then_inc(stored[(n - 1) % 2], 16)
                for slot in range(2):
                    sp.wait_ge(stored[slot], 8 * NT)

            @block.tensor
            def _(pe):
                pe.wait_ge(loaded, 32)
                for n in range(NT):
                    pe.wait_ge(scaled, n + 1)
                    for m in range(CB):
                        i = 2 * n + m
                        if i >= 4:
                            pe.wait_ge(added, i - 3)
                        for k in range(KC):
                            last = pe.matmul(ps[:CP, i % 4, :TB], w[:, k, m, :], hn[:, n % 2, k, :], start=k == 0, stop=k == KC - 1)
                        last.then_inc(summed, 1)

            @block.gpsimd
            def _(pool):
                for n in range(NT):
                    pool.wait_ge(slot_in[n % 2], 16 * LOADS * (n // 2 + 1))
                    if n >= 2:
                        pool.wait_ge(summed, 2 * n - 2)
                    pool.tensor_tensor(hn[:, n % 2, :, :], hin[:, n % 2, :, :], rin[:, n % 2, :, :], ALU.mult).then_inc(scaled, 1)

            @block.vector
            def _(dve):
                dve.wait_ge(den_in, 16 * PAIRS + 16)
                dve.reciprocal(rec[:, :], den[:, :]).then_inc(rec_ready, 1)
                dve.wait_ge(loaded, 32)
                for n in range(NT):
                    dve.wait_ge(slot_in[n % 2], 16 * LOADS * (n // 2 + 1))
                    if n >= 2:
                        dve.wait_ge(stored[n % 2], 16 * (n // 2))
                    for m in range(CB):
                        i = 2 * n + m
                        dve.wait_ge(summed, i + 1)
                        dve.scalar_tensor_tensor(y[:, n % 2, m, :], ps[:CP, i % 4, :TB], bias[:, m:m + 1], xin[:, n % 2, m, :],
                                                 ALU.add, ALU.add).then_inc(added, 1)


def attention_layer(nc, tag, ins, x_in, y_out, scratch):
    with Scope(nc, tag) as s:
        xh, xl = s.sb("xh", [CP, CB, N], f32r), s.sb("xl", [CP, CB, N], f32r)
        v = s.sb("v", [128, 2 * B, C])
        with Scope(nc, tag + "x") as s2:
            x_sb = s2.sb("x", [CP, CB, N])
            load_x(nc, tag + "ld", x_in, x_sb)
            norm(nc, tag + "n", x_sb, ins["group_avg"], xh, xl)
        values(nc, tag + "v", xh, xl, ins[tag + "_wv"], ins[tag + "_bv"], v)
        attention(nc, tag + "a", xh, xl, v, ins[tag + "_wqk"], ins[tag + "_bqk"], ins["signs"], ins[tag + "_rel"],
                  ins["sel1"], ins["sel2"], ins["ident98"], scratch["heads_out"])
    project(nc, tag + "p", scratch["heads_out"], scratch["sums"], ins[tag + "_wo"], ins[tag + "_bo"], x_in, y_out)


def route(nc, xh, xl, gate_dram, first_dram, ident_dram, w_rows):
    HALVES = 2 * B
    with Scope(nc, "ro") as s:
        g = s.sb("g", [CP, CB, E])
        gh, gl = s.sb("gh", [CP, CB, E], f32r), s.sb("gl", [CP, CB, E], f32r)
        ident = s.sb("ident", [128, TH])
        first = s.sb("first", [128, E])
        by_expert = s.sb("by_expert", [E, N])
        logit, seen = s.sb("logit", [128, HALVES, E]), s.sb("seen", [128, HALVES, E])
        key, pick1, pick2 = s.sb("key", [128, HALVES, E]), s.sb("pick1", [128, HALVES, E]), s.sb("pick2", [128, HALVES, E])
        m1, m2, km, d, e2, den, w1, w2 = (s.sb(n, [128, HALVES]) for n in "m1 m2 km d e2 den w1 w2".split())
        wt = s.sb("wt", [128, HALVES, 2 * E])
        ps = s.ps("ps", 8)
        loaded, gh_ready, gl_ready, summed = (s.sem(n) for n in ("loaded", "gh_ready", "gl_ready", "summed"))
        copied, turned, chain, m_diff, e2_ready = (s.sem(n) for n in ("copied", "turned", "chain", "m_diff", "e2_ready"))
        wt_ready, back_turned, rows_ready = (s.sem(n) for n in ("wt_ready", "back_turned", "rows_ready"))
        with nc.Block() as block:
            @block.sync
            def _(sp):
                sp.dma_start(g[:, :, :], gate_dram).then_inc(loaded, 16)
                sp.dma_start(ident[:TH, :], ident_dram).then_inc(loaded, 16)
                sp.dma_start(first[:TH, :], first_dram).then_inc(loaded, 16)

            @block.tensor
            def _(pe):
                pe.wait_ge(gl_ready, 1)
                for t in range(NT):
                    if t >= 4:
                        pe.wait_ge(copied, t - 3)
                    product3(pe, ps[:E, t % 4, :TB], lambda k: gh[:, k, :], lambda k: gl[:, k, :],
                             lambda k: xh[:, k, t * TB:(t + 1) * TB], lambda k: xl[:, k, t * TB:(t + 1) * TB]).then_inc(summed, 1)
                pe.wait_ge(copied, NT)
                for i in range(HALVES):
                    last = pe.transpose(ps[:TH, 4, i * E:(i + 1) * E], by_expert[:, i * TH:(i + 1) * TH], ident[:E, :E])
                last.then_inc(turned, 1)
                pe.wait_ge(wt_ready, 2)
                for i in range(HALVES):
                    last = pe.transpose(ps[:2 * E, i // 4, (i % 4) * TH:(i % 4 + 1) * TH], wt[:TH, i, :], ident[:TH, :])
                    if i % 4 == 3:
                        last.then_inc(back_turned, 1)

            @block.scalar
            def _(act):
                for t in range(NT):
                    act.wait_ge(summed, t + 1)
                    act.activation(by_expert[:, t * TB:(t + 1) * TB], ps[:E, t % 4, :TB], ACT.Copy).then_inc(copied, 1)
                act.wait_ge(m_diff, 1)
                act.activation(e2[:TH, :], d[:TH, :], ACT.Exp).then_inc(e2_ready, 1)
                for t in range(NT):
                    act.wait_ge(back_turned, t + 1)
                    act.activation(w_rows[:, t * TB:(t + 1) * TB], ps[:2 * E, t, :TB], ACT.Copy).then_inc(rows_ready, 1)
                act.wait_ge(rows_ready, NT)

            @block.vector
            def _(dve):
                dve.wait_ge(loaded, 48)
                split(dve, g[:, :, :], gh[:, :, :], gl[:, :, :], gh_ready, gl_ready, 0)
                done = [0]

                def link(ins):
                    done[0] += 1
                    ins.then_inc(chain, 1)
                    dve.wait_ge(chain, done[0])

                def over(x):
                    return x[:TH, :].rearrange("p (i a) -> p i a", a=1).to_broadcast([TH, HALVES, E])

                rank = first[:TH, :].rearrange("p (a e) -> p a e", a=1).to_broadcast([TH, HALVES, E])

                def largest(values, m, pick):
                    link(dve.tensor_reduce(m[:TH, :], values[:TH, :, :], AXIS.X, ALU.max))
                    link(dve.tensor_tensor(key[:TH, :, :], values[:TH, :, :], over(m), ALU.is_equal))
                    link(dve.tensor_tensor(key[:TH, :, :], key[:TH, :, :], rank, ALU.mult))
                    link(dve.tensor_reduce(km[:TH, :], key[:TH, :, :], AXIS.X, ALU.max))
                    link(dve.tensor_tensor(pick[:TH, :, :], key[:TH, :, :], over(km), ALU.is_equal))

                dve.wait_ge(turned, 1)
                link(dve.tensor_copy(logit[:TH, :, :], ps[:TH, 4, :HALVES * E].rearrange("p (i e) -> p i e", e=E)))
                largest(logit, m1, pick1)
                link(dve.scalar_tensor_tensor(seen[:TH, :, :], pick1[:TH, :, :], NEG, logit[:TH, :, :], ALU.mult, ALU.add))
                largest(seen, m2, pick2)
                dve.tensor_tensor(d[:TH, :], m2[:TH, :], m1[:TH, :], ALU.subtract).then_inc(m_diff, 1)
                dve.wait_ge(e2_ready, 1)
                link(dve.tensor_scalar(den[:TH, :], e2[:TH, :], 1.0, None, ALU.add))
                link(dve.reciprocal(w1[:TH, :], den[:TH, :]))
                link(dve.tensor_tensor(w2[:TH, :], e2[:TH, :], w1[:TH, :], ALU.mult))
                link(dve.tensor_tensor(pick1[:TH, :, :], pick1[:TH, :, :], over(w1), ALU.mult))
                link(dve.tensor_tensor(pick2[:TH, :, :], pick2[:TH, :, :], over(w2), ALU.mult))
                link(dve.tensor_tensor(key[:TH, :, :], pick1[:TH, :, :], pick2[:TH, :, :], ALU.add))
                dve.tensor_copy(wt[:TH, :, :E].bitcast(f32r), key[:TH, :, :]).then_inc(wt_ready, 1)
                dve.wait_ge(wt_ready, 1)
                dve.tensor_tensor(wt[:TH, :, E:].bitcast(f32r), key[:TH, :, :], wt[:TH, :, :E], ALU.subtract).then_inc(wt_ready, 1)


def experts(nc, xh, xl, w_rows, w1_dram, b1_dram, w2_dram, b2_dram, pick_dram, x_sb):
    with Scope(nc, "ex") as s:
        w1, w2 = s.sb("w1", [CP, CB, F]), s.sb("w2", [128, FB, C])
        w1h, w1l = s.sb("w1h", [CP, 2, CB, F], f32r), s.sb("w1l", [CP, 2, CB, F], f32r)
        w2h, w2l = s.sb("w2h", [128, 2, FB, C], f32r), s.sb("w2l", [128, 2, FB, C], f32r)
        b1, b2 = s.sb("b1", [128, 2, FB]), s.sb("b2", [CP, 2, CB])
        pick32 = s.sb("pick32", [2 * E, 2, CP])
        pick = s.sb("pick", [2 * E, 2, CP], f32r)
        hh, hl = s.sb("hh", [128, 2, FB, TB], f32r), s.sb("hl", [128, 2, FB, TB], f32r)
        h32 = s.sb("h32", [128, 2, TB])
        wb = s.sb("wb", [CP, 2, TB])
        y = s.sb("y", [CP, 2, CB, TB])
        ps_u, ps_d, ps_w = s.ps("ps_u", 4), s.ps("ps_d", 2), s.ps("ps_w", 2)
        big_in, small_in = s.sem("big_in"), [s.sem("even_in"), s.sem("odd_in")]
        high_ready, low_ready, pick_ready = s.sem("high_ready"), s.sem("low_ready"), s.sem("pick_ready")
        up_summed, hh_ready, h32_ready, hl_ready = (s.sem(n) for n in ("up_summed", "hh_ready", "h32_ready", "hl_ready"))
        down_summed, wb_summed, wb_ready, y_ready, x_added = (
            s.sem(n) for n in ("down_summed", "wb_summed", "wb_ready", "y_ready", "x_added"))

        def for_all_experts(eng, body):
            body(0, 0, True, False)
            with eng.Fori(0, (E - 2) // 2) as it:
                for u in (1, 0):
                    body(it * 2 + (1 if u else 2), u, False, False)
            body(E - 1, 1, False, True)

        with nc.Block() as block:
            @block.sync
            def _(sp):
                for e in range(E):
                    if e >= 1:
                        sp.wait_ge(low_ready, 2 * e)
                    sp.dma_start(w1[:, :, :], w1_dram[e]).then_inc(big_in, 16)
                    sp.dma_start(w2[:, :, :], w2_dram[e]).then_inc(big_in, 16)
                    if e >= 2:
                        sp.wait_ge(y_ready, 2 * NT * (e - 1))
                    for dst, src in ((b1, b1_dram), (b2, b2_dram), (pick32, pick_dram)):
                        sp.dma_start(dst[:, e % 2, :], src[e]).then_inc(small_in[e % 2], 16)

            @block.tensor
            def _(pe):
                def down(i, t, u):
                    pe.wait_ge(hl_ready, 4 * i + 4)
                    for m in range(CB):
                        if not (isinstance(i, int) and i == 0):
                            pe.wait_ge(y_ready, 2 * i + m - 1)
                        cols = slice(m * CP, (m + 1) * CP)
                        product3(pe, ps_d[:CP, m, :TB], lambda k: w2h[:, u, k, cols], lambda k: w2l[:, u, k, cols],
                                 lambda k: hh[:, t % 2, k, :], lambda k: hl[:, t % 2, k, :], blocks=FB).then_inc(down_summed, 1)

                def body(e, u, first, last):
                    pe.wait_ge(low_ready, 2 * e + 2)
                    pe.wait_ge(pick_ready, e + 1)
                    for t in range(NT):
                        i = e * NT + t
                        tok = slice(t * TB, (t + 1) * TB)
                        for f in range(FB):
                            if not (first and t == 0):
                                pe.wait_ge(h32_ready, 4 * i + f - 3)
                            rows = slice(f * 128, (f + 1) * 128)
                            product3(pe, ps_u[:, f, :TB], lambda k: w1h[:, u, k, rows], lambda k: w1l[:, u, k, rows],
                                     lambda k: xh[:, k, tok], lambda k: xl[:, k, tok]).then_inc(up_summed, 1)
                        if not (first and t < 2):
                            pe.wait_ge(wb_ready, i - 1)
                        pe.matmul(ps_w[:CP, t % 2, :TB], pick[:, u, :], w_rows[:, tok], start=True, stop=True).then_inc(wb_summed, 1)
                        if not (first and t == 0):
                            down(i - 1, (t - 1) % NT, u if t else 1 - u)
                    if last:
                        down(e * NT + NT - 1, NT - 1, u)

                for_all_experts(pe, body)

            @block.scalar
            def _(act):
                def body(e, u, first, last):
                    act.wait_ge(small_in[u], 48 * ((e - u) // 2 + 1) if isinstance(e, int) else 24 * (e - u) + 48)
                    for t in range(NT):
                        i = e * NT + t
                        for f in range(FB):
                            act.wait_ge(up_summed, 4 * i + f + 1)
                            if f == 0 and not (first and t < 2):
                                act.wait_ge(down_summed, 2 * i - 2)
                            act.activation(hh[:, t % 2, f, :], ps_u[:, f, :TB], ACT.Gelu, bias=b1[:, u, f:f + 1]).then_inc(hh_ready, 1)
                            if not (first and t == 0 and f < 2):
                                act.wait_ge(hl_ready, 4 * i + f - 1)
                            act.activation(h32[:, f % 2, :], ps_u[:, f, :TB], ACT.Gelu, bias=b1[:, u, f:f + 1]).then_inc(h32_ready, 1)
                        act.wait_ge(wb_summed, i + 1)
                        if not (first and t < 2):
                            act.wait_ge(y_ready, 2 * i - 2)
                        act.activation(wb[:, t % 2, :], ps_w[:CP, t % 2, :TB], ACT.Copy).then_inc(wb_ready, 1)

                for_all_experts(act, body)

            @block.vector
            def _(dve):
                def prepare(e, u):
                    dve.wait_ge(big_in, 32 * e + 32)
                    dve.tensor_copy(w1h[:, u, :, :], w1[:, :, :]).then_inc(high_ready, 1)
                    dve.tensor_copy(w2h[:, u, :, :], w2[:, :, :]).then_inc(high_ready, 1)
                    dve.wait_ge(small_in[u], 48 * ((e - u) // 2 + 1) if isinstance(e, int) else 24 * (e - u) + 48)
                    dve.tensor_copy(pick[:, u, :], pick32[:, u, :]).then_inc(pick_ready, 1)
                    dve.wait_ge(high_ready, 2 * e + 2)
                    dve.tensor_tensor(w1l[:, u, :, :], w1[:, :, :], w1h[:, u, :, :].bitcast(f32), ALU.subtract).then_inc(low_ready, 1)
                    dve.tensor_tensor(w2l[:, u, :, :], w2[:, :, :], w2h[:, u, :, :].bitcast(f32), ALU.subtract).then_inc(low_ready, 1)

                def weigh(i, t, u):
                    dve.wait_ge(wb_ready, i + 1)
                    for m in range(CB):
                        dve.wait_ge(down_summed, 2 * i + m + 1)
                        if not (isinstance(i, int) and i < 2):
                            dve.wait_ge(x_added, 2 * i + m - 3)
                        dve.scalar_tensor_tensor(y[:, t % 2, m, :], ps_d[:CP, m, :TB], b2[:, u, m:m + 1], wb[:, t % 2, :],
                                                 ALU.add, ALU.mult).then_inc(y_ready, 1)

                def body(e, u, first, last):
                    for t in range(NT):
                        i = e * NT + t
                        for f in range(FB):
                            dve.wait_ge(h32_ready, 4 * i + f + 1)
                            dve.tensor_tensor(hl[:, t % 2, f, :], h32[:, f % 2, :], hh[:, t % 2, f, :].bitcast(f32),
                                              ALU.subtract).then_inc(hl_ready, 1)
                        if not (first and t == 0):
                            weigh(i - 1, (t - 1) % NT, u if t else 1 - u)
                        if t == 3 and not last:
                            prepare(e + 1, 1 - u)
                    if last:
                        weigh(e * NT + NT - 1, NT - 1, u)

                prepare(0, 0)
                for_all_experts(dve, body)

            @block.gpsimd
            def _(pool):
                def body(e, u, first, last):
                    for t in range(NT):
                        for m in range(CB):
                            pool.wait_ge(y_ready, (e * NT + t) * 2 + m + 1)
                            x = x_sb[:, m, t * TB:(t + 1) * TB]
                            pool.tensor_tensor(x, x, y[:, t % 2, m, :], ALU.add).then_inc(x_added, 1)

                for_all_experts(pool, body)
                pool.wait_ge(x_added, 2 * NT * E)


def shared_expert(nc, xh, xl, w13_dram, b13_dram, w2_dram, b2_dram, x_sb, y_dram):
    with Scope(nc, "sh") as s:
        w13 = s.sb("w13", [CP, 2, CB, F])
        wh, wl = s.sb("wh", [CP, 2, CB, F], f32r), s.sb("wl", [CP, 2, CB, F], f32r)
        w2 = s.sb("w2", [128, FB, C])
        w2h, w2l = s.sb("w2h", [128, FB, C], f32r), s.sb("w2l", [128, FB, C], f32r)
        b13, b2 = s.sb("b13", [128, 2, FB]), s.sb("b2", [CP, CB])
        g = s.sb("g", [128, 2, TB])
        h32 = s.sb("h32", [128, 2, TB])
        hh, hl = s.sb("hh", [128, 2, FB, TB], f32r), s.sb("hl", [128, 2, FB, TB], f32r)
        y = s.sb("y", [CP, 2, CB, TB])
        ps_1, ps_3, ps_d = s.ps("ps_1", 2), s.ps("ps_3", 2), s.ps("ps_d", 2)
        loaded, high_ready, low_ready = s.sem("loaded"), s.sem("high_ready"), s.sem("low_ready")
        summed1, summed3, g_ready, h32_ready = (s.sem(n) for n in ("summed1", "summed3", "g_ready", "h32_ready"))
        hh_ready, hl_ready, down_summed, y_ready = (s.sem(n) for n in ("hh_ready", "hl_ready", "down_summed", "y_ready"))
        stored = [s.sem("even_stored"), s.sem("odd_stored")]
        with nc.Block() as block:
            @block.sync
            def _(sp):
                for dst, src in ((w13[:, :, :, :], w13_dram), (w2[:, :, :], w2_dram), (b13[:, :, :], b13_dram), (b2[:, :], b2_dram)):
                    sp.dma_start(dst, src).then_inc(loaded, 16)
                for t in range(NT):
                    sp.wait_ge(y_ready, 2 * t + 2)
                    sp.dma_start(y_dram[:, :, t * TB:(t + 1) * TB], y[:, t % 2, :, :]).then_inc(stored[t % 2], 16)
                for slot in range(2):
                    sp.wait_ge(stored[slot], 8 * NT)

            @block.tensor
            def _(pe):
                def down(t):
                    pe.wait_ge(hh_ready, 4 * t + 4)
                    pe.wait_ge(hl_ready, 4 * t + 4)
                    for m in range(CB):
                        if t >= 1:
                            pe.wait_ge(y_ready, 2 * t + m - 1)
                        cols = slice(m * CP, (m + 1) * CP)
                        product3(pe, ps_d[:CP, m, :TB], lambda k: w2h[:, k, cols], lambda k: w2l[:, k, cols],
                                 lambda k: hh[:, t % 2, k, :], lambda k: hl[:, t % 2, k, :], blocks=FB).then_inc(down_summed, 1)

                pe.wait_ge(low_ready, 2)
                for t in range(NT):
                    tok = slice(t * TB, (t + 1) * TB)
                    for f in range(FB):
                        i = 4 * t + f
                        rows = slice(f * 128, (f + 1) * 128)
                        if i >= 2:
                            pe.wait_ge(h32_ready, i - 1)
                        for a, ps, done in ((0, ps_1, summed1), (1, ps_3, summed3)):
                            product3(pe, ps[:, i % 2, :TB], lambda k: wh[:, a, k, rows], lambda k: wl[:, a, k, rows],
                                     lambda k: xh[:, k, tok], lambda k: xl[:, k, tok]).then_inc(done, 1)
                    if t >= 1:
                        down(t - 1)
                down(NT - 1)

            @block.scalar
            def _(act):
                act.wait_ge(loaded, 64)
                for i in range(4 * NT + 1):
                    if i < 4 * NT:
                        act.wait_ge(summed1, i + 1)
                        if i >= 2:
                            act.wait_ge(h32_ready, i - 1)
                        act.activation(g[:, i % 2, :], ps_1[:, i % 2, :TB], ACT.Gelu, bias=b13[:, 0, i % 4:i % 4 + 1]).then_inc(g_ready, 1)
                    if i >= 1:
                        j = i - 1
                        t, f = j // 4, j % 4
                        act.wait_ge(h32_ready, j + 1)
                        if f == 0 and t >= 2:
                            act.wait_ge(down_summed, 2 * t - 2)
                        act.activation(hh[:, t % 2, f, :], h32[:, j % 2, :], ACT.Copy).then_inc(hh_ready, 1)

            @block.vector
            def _(dve):
                dve.wait_ge(loaded, 64)
                dve.tensor_copy(wh[:, :, :, :], w13[:, :, :, :]).then_inc(high_ready, 1)
                dve.tensor_copy(w2h[:, :, :], w2[:, :, :]).then_inc(high_ready, 1)
                dve.wait_ge(high_ready, 2)
                dve.tensor_tensor(wl[:, :, :, :], w13[:, :, :, :], wh[:, :, :, :].bitcast(f32), ALU.subtract).then_inc(low_ready, 1)
                dve.tensor_tensor(w2l[:, :, :], w2[:, :, :], w2h[:, :, :].bitcast(f32), ALU.subtract).then_inc(low_ready, 1)

                def finish(t):
                    for m in range(CB):
                        dve.wait_ge(down_summed, 2 * t + m + 1)
                        if m == 0 and t >= 2:
                            dve.wait_ge(stored[t % 2], 16 * (t // 2))
                        dve.scalar_tensor_tensor(y[:, t % 2, m, :], ps_d[:CP, m, :TB], b2[:, m:m + 1], x_sb[:, m, t * TB:(t + 1) * TB],
                                                 ALU.add, ALU.add).then_inc(y_ready, 1)

                for i in range(4 * NT + 1):
                    if i < 4 * NT:
                        dve.wait_ge(summed3, i + 1)
                        dve.wait_ge(g_ready, i + 1)
                        if i >= 2:
                            dve.wait_ge(hh_ready, i - 1)
                            dve.wait_ge(hl_ready, i - 1)
                        dve.scalar_tensor_tensor(h32[:, i % 2, :], ps_3[:, i % 2, :TB], b13[:, 1, i % 4:i % 4 + 1], g[:, i % 2, :],
                                                 ALU.add, ALU.mult).then_inc(h32_ready, 1)
                    if i >= 1:
                        j = i - 1
                        t, f = j // 4, j % 4
                        dve.wait_ge(hh_ready, j + 1)
                        dve.tensor_tensor(hl[:, t % 2, f, :], h32[:, j % 2, :], hh[:, t % 2, f, :].bitcast(f32),
                                          ALU.subtract).then_inc(hl_ready, 1)
                        if f == 3 and t >= 1:
                            finish(t - 1)
                finish(NT - 1)


def experts_layer(nc, ins, x_in, y_out):
    with Scope(nc, "l2") as s:
        x_sb = s.sb("x", [CP, CB, N])
        xh, xl = s.sb("xh", [CP, CB, N], f32r), s.sb("xl", [CP, CB, N], f32r)
        w_rows = s.sb("w_rows", [2 * E, N], f32r)
        load_x(nc, "l2ld", x_in, x_sb)
        norm(nc, "l2n", x_sb, ins["group_avg"], xh, xl)
        route(nc, xh, xl, ins["gate"], ins["first"], ins["ident98"], w_rows)
        experts(nc, xh, xl, w_rows, ins["fc1"], ins["fc1_b"], ins["fc2"], ins["fc2_b"], ins["pick"], x_sb)
        shared_expert(nc, xh, xl, ins["w13"], ins["b13"], ins["w2"], ins["w2_b"], x_sb, y_out)


def build(nc, ins, out, stop_after=99, only=None):
    scratch = {n: nc.dram_tensor(n, sh, f32, kind="Internal").ap() for n, sh in
               (("x1", [CP, CB, N]), ("x2", [CP, CB, N]), ("x3", [CP, CB, N]), ("heads_out", [PAIRS, 33, 2, N]), ("sums", [HEADS, N]))}
    if only in (None, 0):
        gru_layer(nc, ins, ins["x"], scratch["x1"] if stop_after > 0 else out)
    if stop_after >= 1 and only in (None, 1):
        attention_layer(nc, "l1", ins, ins["x"] if only else scratch["x1"], scratch["x2"] if stop_after > 1 else out, scratch)
    if stop_after >= 2 and only in (None, 2):
        experts_layer(nc, ins, ins["x"] if only else scratch["x2"], scratch["x3"] if stop_after > 2 else out)
    if stop_after >= 3 and only in (None, 3):
        attention_layer(nc, "l3", ins, ins["x"] if only else scratch["x3"], out, scratch)


def selectors():
    k = np.arange(T)
    one = np.zeros((64, T), np.float32)
    one[32:46] = (k // W)[None] == np.arange(H)[:, None]
    one[46:60] = (k % W)[None] == np.arange(W)[:, None]
    two = one.copy()
    two[0:2] = -1.0
    signs = np.repeat(np.array([[-1, 0], [1, 1], [-HD ** -0.5, 0], [HD ** -0.5, HD ** -0.5]], np.float32), 16, 0)
    return np.tile(one, (2, 1)), np.tile(two, (2, 1)), np.tile(signs, (2, 1))


def lay_out_attention(tag, wqkv, bqkv, wo, bo, rel_h, rel_w):
    o = {}
    rows = wqkv.reshape(C, 3, PAIRS, 2, HD)
    cols = [rows[:, part, :, head] for head in range(2) for part in (0, 0, 1, 1)]
    o["_wqk"] = np.ascontiguousarray(np.stack(cols, 2).reshape(CB, CP, PAIRS, 128).transpose(2, 1, 0, 3))
    b = bqkv.reshape(3, PAIRS, 2, HD)
    o["_bqk"] = np.ascontiguousarray(np.stack([b[part, :, head] for head in range(2) for part in (0, 0, 1, 1)], 1).reshape(PAIRS, 128, 1))
    o["_wv"] = np.ascontiguousarray(wqkv[:, 2 * C:].reshape(CB, CP, C).transpose(1, 0, 2))
    o["_bv"] = np.ascontiguousarray(np.broadcast_to(bqkv[2 * C:], (TH, C)))
    r = np.zeros((2, 4, HD, H + W, 2, H), np.float32)
    for n in range(H):
        for a, table in ((0, rel_h), (H, rel_w)):
            seen = table[n:n + H][::-1].T
            for head in range(2):
                r[head, 0:2, :, a + n, head, :] = seen
    o["_rel"] = r.reshape(128, H + W, 2 * H)
    w = wo.reshape(PAIRS // 2, 2, 2, 1, HD, C)
    o["_wo"] = np.ascontiguousarray(np.broadcast_to(w, (3, 2, 2, 2, HD, C)).reshape(3, 128, CB, CP).transpose(1, 0, 2, 3))
    o["_bo"] = np.ascontiguousarray(bo.reshape(CB, CP).T)
    return {tag + k: v for k, v in o.items()}


def channels(a):
    a = np.asarray(a)
    return np.ascontiguousarray(np.moveaxis(a.reshape(*a.shape[:-1], CB, CP), (-1, -2), (0, 1)))


def twice(a):
    return np.stack([a[..., :128], np.concatenate([a[..., 128:], a[..., 128:]], -1)], -2)


def lay_out(i):
    a = {k: np.asarray(v) for k, v in i.items()}
    o = {}
    o["x"] = channels(a["x"].reshape(N, C))
    o["group_avg"] = np.kron(np.eye(CP // GC), np.full((GC, GC), 1.0 / GC)).astype(np.float32)
    o["ident128"] = np.eye(128, dtype=np.float32)
    o["wx"] = channels(twice(a["L0_conv_Wx"].reshape(3, C, C).transpose(2, 0, 1)).reshape(C, 6, 128).transpose(1, 2, 0))
    o["bx"] = np.ascontiguousarray(twice(a["L0_conv_bx"].reshape(3, C)).reshape(6, 128).T)
    o["bh"] = np.ascontiguousarray(twice(a["L0_conv_bh"].reshape(3, C)).reshape(6, 128).T)
    o["bhn"] = np.ascontiguousarray(twice(a["L0_conv_bh"][2 * C:]).T)
    wh = twice(a["L0_conv_Wh"].reshape(3, C, C).transpose(2, 0, 1))
    o["wh"] = np.ascontiguousarray(np.moveaxis(twice(np.moveaxis(wh, 0, -1)), (-1, -2), (0, 1)))
    o["wp"] = np.ascontiguousarray(a["L0_conv_Wp"].T.reshape(C, CB, CP))
    o["sel1"], o["sel2"], o["signs"] = selectors()
    o["ident98"] = np.eye(TH, dtype=np.float32)
    o.update(lay_out_attention("l1", a["L1_conv_qkv_w"], a["L1_conv_qkv_b"], a["L1_conv_proj_w"], a["L1_conv_proj_b"],
                               a["L1_conv_rel_pos_h"], a["L1_conv_rel_pos_w"]))
    o.update(lay_out_attention("l3", a["L3_conv_qkv_w"].T, a["L3_conv_qkv_b"], a["L3_conv_proj_w"].T, a["L3_conv_proj_b"],
                               a["L3_conv_rel_pos_h"], a["L3_conv_rel_pos_w"]))
    o["gate"] = channels(a["L2_conv_gate_w"])
    o["first"] = np.ascontiguousarray(np.broadcast_to(np.arange(E, 0, -1, dtype=np.float32), (TH, E)))
    o["fc1"] = np.ascontiguousarray(a["L2_conv_fc1_w"].reshape(E, F, CB, CP).transpose(0, 3, 2, 1))
    o["fc1_b"] = np.ascontiguousarray(a["L2_conv_fc1_b"].reshape(E, FB, 128).transpose(0, 2, 1))
    o["fc2"] = np.ascontiguousarray(a["L2_conv_fc2_w"].reshape(E, C, FB, 128).transpose(0, 3, 2, 1))
    o["fc2_b"] = np.ascontiguousarray(a["L2_conv_fc2_b"].reshape(E, CB, CP).transpose(0, 2, 1))
    o["pick"] = np.ascontiguousarray(np.broadcast_to(np.tile(np.eye(E, dtype=np.float32), (1, 2))[:, :, None], (E, 2 * E, CP)))
    o["w13"] = np.ascontiguousarray(np.stack([a["L2_conv_w1_w"], a["L2_conv_w3_w"]]).reshape(2, F, CB, CP).transpose(3, 0, 2, 1))
    o["b13"] = np.ascontiguousarray(np.stack([a["L2_conv_w1_b"], a["L2_conv_w3_b"]]).reshape(2, FB, 128).transpose(2, 0, 1))
    o["w2"] = np.ascontiguousarray(a["L2_conv_w2_w"].reshape(C, FB, 128).transpose(2, 1, 0))
    o["w2_b"] = np.ascontiguousarray(a["L2_conv_w2_b"].reshape(CB, CP).T)
    return o


def back(y):
    return np.ascontiguousarray(y.transpose(2, 1, 0).reshape(B, H, W, C))


_BUILT_OUT = "out_0_dram"


def kernel(**inputs):
    import concourse.bacc as _bacc
    from concourse.bass_utils import run_bass_kernel_spmd as _run

    nc = _bacc.Bacc("TRN2", target_bir_lowering=False, num_devices=1)
    arrays = {f"in_{k}_dram": v for k, v in lay_out(inputs).items()}
    ins = {k[3:-5]: nc.dram_tensor(k, v.shape, mybir.dt.from_np(v.dtype), kind="ExternalInput").ap() for k, v in arrays.items()}
    out = nc.dram_tensor(_BUILT_OUT, [CP, CB, N], f32, kind="ExternalOutput").ap()
    build(nc, ins, out)
    r = _run(nc, [arrays], core_ids=[0])
    return back(r.results[0][_BUILT_OUT])
```

```python
import numpy as np
import concourse.bass as bass
from concourse import mybir
from contextlib import ExitStack

f32, f32r = mybir.dt.float32, mybir.dt.float32r
bf16, fp16 = mybir.dt.bfloat16, mybir.dt.float16
ALU = mybir.AluOpType
ACT = mybir.ActivationFunctionType
AXIS = mybir.AxisListType

B, H, W, C = 16, 14, 14, 192
T = H * W
N = B * T
CP, CB = 96, 2
HEADS, HD = 12, 16
PAIRS = HEADS // 2
G, GC = 32, C // 32
E, F = 8, 512
FB = F // 128
TB = 2 * T
NT = N // TB
TH = T // 2
HSCALE = 2048.0
EPS = 1e-5
NEG = -3.0e38


class Scope:

    def __init__(self, nc, tag):
        self.nc, self.tag, self.stack, self.sems = nc, tag, ExitStack(), []

    def __enter__(self):
        self.stack.__enter__()
        return self

    def __exit__(self, *e):
        if self.sems:
            self.nc.clear_and_free_semaphores(self.sems)
            self.nc.all_engine_barrier()
        return self.stack.__exit__(*e)

    def sb(self, name, shape, dt=f32):
        return self.stack.enter_context(self.nc.sbuf_tensor(f"{self.tag}_{name}", shape, dt))

    def ps(self, name, banks=1):
        return self.stack.enter_context(self.nc.psum_tensor(f"{self.tag}_{name}", [128, banks, 512], f32))

    def sem(self, name):
        self.sems.append(self.nc.alloc_semaphore(f"{self.tag}_{name}"))
        return self.sems[-1]


def load_x(nc, tag, x_dram, x_sb):
    with Scope(nc, tag) as s:
        loaded = s.sem("loaded")
        with nc.Block() as block:
            @block.sync
            def _(sp):
                sp.dma_start(x_sb[:, :, :], x_dram).then_inc(loaded, 16)
                sp.wait_ge(loaded, 16)


def norm(nc, tag, x_sb, group_avg, xh, xl):
    with Scope(nc, tag) as s:
        stats = s.sb("stats", [CP, CB, B, 6])
        mv = s.sb("mv", [CP, CB, B, 2])
        dev = s.sb("dev", [CP, CB, B])
        spread = s.sb("spread", [CP, CB, B])
        mean_g = s.sb("mean_g", [CP, CB, B])
        std = s.sb("std", [CP, CB, B])
        rstd = s.sb("rstd", [CP, CB, B])
        shift = s.sb("shift", [CP, CB, B])
        avg = s.sb("avg", [CP, CP])
        eps = s.sb("eps", [CP, 1])
        xn = s.sb("xn", [CP, 4, T])
        ps_mean, ps_var = s.ps("ps_mean"), s.ps("ps_var")
        avg_in, chan, chan2 = s.sem("avg_in"), s.sem("chan"), s.sem("chan2")
        mean_ready, var_ready, mean_copied = s.sem("mean_ready"), s.sem("var_ready"), s.sem("mean_copied")
        dev_ready, dev2, spreaqk_ready = s.sem("dev_ready"), s.sem("dev2"), s.sem("spreaqk_ready")
        stqk_ready, rstqk_ready, shift_ready = s.sem("stqk_ready"), s.sem("rstqk_ready"), s.sem("shift_ready")
        xn_ready, xh_ready, xl_ready = s.sem("xn_ready"), s.sem("xh_ready"), s.sem("xl_ready")
        eps_ready = s.sem("eps_ready")
        with nc.Block() as block:
            @block.sync
            def _(sp):
                sp.dma_start(avg[:, :], group_avg).then_inc(avg_in, 16)

            @block.vector
            def _(dve):
                dve.memset(eps[:, :], EPS).then_inc(eps_ready, 1)
                for k in range(CB):
                    for b in range(B):
                        dve.bn_stats(stats[:, k, b, :], x_sb[:, k, b * T:(b + 1) * T]).then_inc(chan, 1)
                dve.wait_ge(chan, CB * B)
                for k in range(CB):
                    for b in range(B):
                        dve.bn_aggr(mv[:, k, b, :], stats[:, k, b, :]).then_inc(chan2, 1)
                dve.wait_ge(mean_ready, 1)
                dve.tensor_copy(mean_g[:, :, :].rearrange("p k b -> p (k b)"), ps_mean[:CP, 0, :CB * B]).then_inc(mean_copied, 1)
                dve.wait_ge(mean_copied, 1)
                dve.tensor_tensor(dev[:, :, :], mv[:, :, :, 0], mean_g[:, :, :], ALU.subtract).then_inc(dev_ready, 1)
                dve.wait_ge(dev_ready, 1)
                dve.tensor_tensor(spread[:, :, :], dev[:, :, :], dev[:, :, :], ALU.mult).then_inc(dev2, 1)
                dve.wait_ge(dev2, 1)
                dve.tensor_tensor(spread[:, :, :], spread[:, :, :], mv[:, :, :, 1], ALU.add).then_inc(spreaqk_ready, 1)
                dve.wait_ge(stqk_ready, 1)
                dve.reciprocal(rstd[:, :, :], std[:, :, :]).then_inc(rstqk_ready, 1)
                dve.wait_ge(rstqk_ready, 1)
                dve.scalar_tensor_tensor(shift[:, :, :].rearrange("p k b -> p (k b)"), mean_g[:, :, :].rearrange("p k b -> p (k b)"), -1.0,
                                         rstd[:, :, :].rearrange("p k b -> p (k b)"), ALU.mult, ALU.mult).then_inc(shift_ready, 1)
                dve.wait_ge(shift_ready, 1)
                tiles = [(k, b) for b in range(B) for k in range(CB)]

                def low(n):
                    k, b = tiles[n]
                    dve.wait_ge(xh_ready, n + 1)
                    dve.wait_ge(xn_ready, n + 1)
                    dve.tensor_tensor(xl[:, k, b * T:(b + 1) * T], xn[:, n % 4, :],
                                      xh[:, k, b * T:(b + 1) * T].bitcast(f32), ALU.subtract).then_inc(xl_ready, 1)

                for n, (k, b) in enumerate(tiles):
                    if n >= 4:
                        dve.wait_ge(xl_ready, n - 3)
                    dve.tensor_scalar(xn[:, n % 4, :], x_sb[:, k, b * T:(b + 1) * T], rstd[:, k, b:b + 1],
                                      shift[:, k, b:b + 1], ALU.mult, ALU.add).then_inc(xn_ready, 1)
                    if n >= 2:
                        low(n - 2)
                low(len(tiles) - 2)
                low(len(tiles) - 1)
                dve.wait_ge(xl_ready, len(tiles))

            @block.tensor
            def _(pe):
                pe.wait_ge(avg_in, 16)
                pe.wait_ge(chan2, CB * B)
                pe.matmul(ps_mean[:CP, 0, :CB * B], avg[:, :], mv[:, :, :, 0], start=True, stop=True).then_inc(mean_ready, 1)
                pe.wait_ge(spreaqk_ready, 1)
                pe.matmul(ps_var[:CP, 0, :CB * B], avg[:, :], spread[:, :, :], start=True, stop=True).then_inc(var_ready, 1)

            @block.scalar
            def _(act):
                act.wait_ge(eps_ready, 1)
                act.wait_ge(var_ready, 1)
                act.activation(std[:, :, :].rearrange("p k b -> p (k b)"), ps_var[:CP, 0, :CB * B], ACT.Sqrt,
                               bias=eps[:, :]).then_inc(stqk_ready, 1)
                act.wait_ge(shift_ready, 1)
                for b in range(B):
                    for k in range(CB):
                        act.activation(xh[:, k, b * T:(b + 1) * T], x_sb[:, k, b * T:(b + 1) * T], ACT.Identity,
                                       scale=rstd[:, k, b:b + 1], bias=shift[:, k, b:b + 1]).then_inc(xh_ready, 1)
                act.wait_ge(xh_ready, B * CB)


def split(eng, whole, high, low, high_ready, low_ready, count):
    eng.tensor_copy(high, whole).then_inc(high_ready, 1)
    eng.wait_ge(high_ready, count + 1)
    eng.tensor_tensor(low, whole, high.bitcast(f32), ALU.subtract).then_inc(low_ready, 1)


def product3(pe, out, wh, wl, xh, xl, start=True, stop=True, blocks=CB):
    terms = [(w, x, k) for k in range(blocks) for w, x in ((wh, xh), (wl, xh), (wh, xl))]
    for n, (w, x, k) in enumerate(terms):
        last = pe.matmul(out, w(k), x(k), start=start and n == 0, stop=stop and n == len(terms) - 1)
    return last


def gru_inputs(nc, xh, xl, wx_dram, bx_dram, bh_dram, gates_in, cand_in):
    with Scope(nc, "gi") as s:
        w = s.sb("w", [CP, CB, 6, 128])
        wh = s.sb("wh", [CP, CB, 6, 128], f32r)
        wl = s.sb("wl", [CP, CB, 6, 128], f32r)
        bx, bh, bias, bias_s = s.sb("bx", [128, 6]), s.sb("bh", [128, 6]), s.sb("bias", [128, 6]), s.sb("bias_s", [128, 6])
        whole = s.sb("whole", [128, 2, TB])
        rest = s.sb("rest", [128, 2, TB])
        rest2 = s.sb("rest2", [128, 2, TB])
        ps = s.ps("ps", 4)
        loaded, wh_ready, wl_ready = s.sem("loaded"), s.sem("wh_ready"), s.sem("wl_ready")
        bias_ready, biass_ready = s.sem("bias_ready"), s.sem("biass_ready")
        summed, moved, canqk_ready = s.sem("summed"), s.sem("moved"), s.sem("canqk_ready")
        p0, r1, p1, r2, p2 = s.sem("p0"), s.sem("r1"), s.sem("p1"), s.sem("r2"), s.sem("p2")

        def view(x):
            return x.rearrange("p (b t) -> p t b", b=2)

        with nc.Block() as block:
            @block.sync
            def _(sp):
                sp.dma_start(w[:, :, :, :], wx_dram).then_inc(loaded, 16)
                sp.dma_start(bx[:, :], bx_dram).then_inc(loaded, 16)
                sp.dma_start(bh[:, :], bh_dram).then_inc(loaded, 16)

            @block.tensor
            def _(pe):
                pe.wait_ge(wl_ready, 1)
                for n in range(NT):
                    for j in range(6):
                        i = n * 6 + j
                        if i >= 4:
                            pe.wait_ge(moved, i - 3)
                        product3(pe, ps[:, i % 4, :TB], lambda k: wh[:, k, j, :], lambda k: wl[:, k, j, :],
                                 lambda k: xh[:, k, n * TB:(n + 1) * TB],
                                 lambda k: xl[:, k, n * TB:(n + 1) * TB]).then_inc(summed, 1)

            @block.scalar
            def _(act):
                act.wait_ge(biass_ready, 1)
                for n in range(NT):
                    for j in range(6):
                        i, g = n * 6 + j, n * 4 + j
                        act.wait_ge(summed, i + 1)
                        if j < 4:
                            if g >= 2:
                                act.wait_ge(p2, g - 1)
                            act.activation(whole[:, g % 2, :], ps[:, i % 4, :TB], ACT.Identity, scale=HSCALE,
                                           bias=bias_s[:, j:j + 1]).then_inc(moved, 1)
                        else:
                            act.activation(cand_in[:, :, j - 4, 2 * n:2 * n + 2], view(ps[:, i % 4, :TB]), ACT.Identity,
                                           bias=bias[:, j:j + 1]).then_inc(moved, 1)
                act.wait_ge(moved, 6 * NT)

            @block.vector
            def _(dve):
                dve.wait_ge(loaded, 48)
                split(dve, w[:, :, :, :], wh[:, :, :, :], wl[:, :, :, :], wh_ready, wl_ready, 0)
                dve.tensor_tensor(bias[:, 0:4], bx[:, 0:4], bh[:, 0:4], ALU.add).then_inc(bias_ready, 1)
                dve.tensor_copy(bias[:, 4:6], bx[:, 4:6]).then_inc(bias_ready, 1)
                dve.wait_ge(bias_ready, 2)
                dve.tensor_scalar(bias_s[:, :], bias[:, :], HSCALE, None, ALU.mult).then_inc(biass_ready, 1)
                for n in range(NT):
                    for j in range(4):
                        g = n * 4 + j
                        dst = [gates_in[:, :, p, j, 2 * n:2 * n + 2] for p in range(3)]
                        dve.wait_ge(moved, n * 6 + j + 1)
                        dve.tensor_copy(dst[0], view(whole[:, g % 2, :])).then_inc(p0, 1)
                        dve.wait_ge(p0, g + 1)
                        dve.tensor_tensor(view(rest[:, g % 2, :]), view(whole[:, g % 2, :]), dst[0], ALU.subtract).then_inc(r1, 1)
                        dve.wait_ge(r1, g + 1)
                        dve.tensor_copy(dst[1], view(rest[:, g % 2, :])).then_inc(p1, 1)
                        dve.wait_ge(p1, g + 1)
                        dve.tensor_tensor(dst[2], view(rest[:, g % 2, :]), dst[1], ALU.subtract).then_inc(p2, 1)
                dve.wait_ge(p2, NT * 4)


def gru(nc, gates_in, cand_in, state, wh_dram, bhn_dram, ident_dram):
    STEPS = 14
    with Scope(nc, "gru") as s:
        w = s.sb("w", [128, CB, 3, 2, 128])
        wp = s.sb("wp", [128, 5, 3, 2, 128], bf16)
        wr = s.sb("wr", [128, CB, 3, 2, 128])
        ident32, ident = s.sb("ident32", [128, 128]), s.sb("ident", [128, 128], bf16)
        bhn, bhs = s.sb("bhn", [128, 2]), s.sb("bhs", [128, 2, B])
        bp, br = s.sb("bp", [128, 3, 2, B], bf16), s.sb("br", [128, 2, B])
        hp = s.sb("hp", [128, 2, 2, 2 * B], fp16)
        names = "tr tz zs zc rn cand n keep new".split()
        tr, tz, zs, zc, rn, cand, tn, keep, new = (s.sb(n, [128, 2, 2 * B]) for n in names)
        ps_r, ps_n, ps_z = s.ps("ps_r", 2), s.ps("ps_n", 2), s.ps("ps_z", 2)
        loaded, prep, weights_ready = s.sem("loaded"), s.sem("prep"), s.sem("weights_ready")
        hi_ready, lo_ready, h_ready = s.sem("hi_ready"), s.sem("lo_ready"), s.sem("h_ready")
        r_summed, n_summed, z_summed = s.sem("r_summed"), s.sem("n_summed"), s.sem("z_summed")
        tr_ready, tz_ready, tn_ready = s.sem("tr_ready"), s.sem("tz_ready"), s.sem("tn_ready")
        zs_ready, zc_ready, rn_ready = s.sem("zs_ready"), s.sem("zc_ready"), s.sem("rn_ready")
        canqk_ready, keep_ready, new_ready = s.sem("canqk_ready"), s.sem("keep_ready"), s.sem("new_ready")

        def two(x):
            return x.rearrange("p (k b) -> p k b", k=2)

        with nc.Block() as block:
            @block.sync
            def _(sp):
                sp.dma_start(w[:, :, :, :, :], wh_dram).then_inc(loaded, 16)
                sp.dma_start(ident32[:, :], ident_dram).then_inc(loaded, 16)
                sp.dma_start(bhn[:, :], bhn_dram).then_inc(loaded, 16)

            @block.vector
            def _(dve):
                step = [0]

                def link(ins):
                    step[0] += 1
                    ins.then_inc(prep, 1)
                    dve.wait_ge(prep, step[0])

                dve.memset(state[:, 0, :, :], 0.0).then_inc(h_ready, 1)
                dve.memset(hp[:, 0, 0, :], 0.0).then_inc(hi_ready, 1)
                dve.memset(hp[:, 0, 1, :], 0.0).then_inc(lo_ready, 1)
                dve.wait_ge(loaded, 48)
                link(dve.tensor_copy(wp[:, 0], w[:, 0]))
                link(dve.tensor_tensor(wr[:, 0], w[:, 0], wp[:, 0], ALU.subtract))
                link(dve.tensor_copy(wp[:, 1], wr[:, 0]))
                link(dve.tensor_tensor(wp[:, 2], wr[:, 0], wp[:, 1], ALU.subtract))
                link(dve.tensor_copy(wp[:, 3], w[:, 1]))
                link(dve.tensor_tensor(wr[:, 1], w[:, 1], wp[:, 3], ALU.subtract))
                link(dve.tensor_copy(wp[:, 4], wr[:, 1]))
                link(dve.tensor_copy(wp[64:128, 3], wp[64:128, 4]))
                link(dve.tensor_tensor(wr[:, 0], wr[:, 1], wp[:, 4], ALU.subtract))
                link(dve.tensor_copy(wp[:, 4], wr[:, 0]))
                link(dve.memset(wp[64:128, 4], 0.0))
                for k in range(2):
                    link(dve.memset(bhs[:, k, :], HSCALE))
                    link(dve.tensor_scalar(bhs[:, k, :], bhs[:, k, :], bhn[:, k:k + 1], None, ALU.mult))
                link(dve.tensor_copy(bp[:, 0], bhs[:, :, :]))
                link(dve.tensor_tensor(br[:, :, :], bhs[:, :, :], bp[:, 0], ALU.subtract))
                link(dve.tensor_copy(bp[:, 1], br[:, :, :]))
                link(dve.tensor_tensor(bp[:, 2], br[:, :, :], bp[:, 1], ALU.subtract))
                dve.tensor_copy(ident[:, :], ident32[:, :]).then_inc(weights_ready, 1)
                with dve.Fori(0, T // STEPS) as it:
                    for u in range(STEPS):
                        t, b = it * STEPS + u, u % 2
                        dve.wait_ge(tr_ready, t + 1)
                        dve.wait_ge(n_summed, t + 1)
                        dve.scalar_tensor_tensor(rn[:, b, :], tr[:, b, :], 1.0, ps_n[:, b, :2 * B], ALU.add, ALU.mult).then_inc(rn_ready, 1)
                        dve.wait_ge(rn_ready, t + 1)
                        dve.scalar_tensor_tensor(two(cand[:, b, :]), two(rn[:, b, :]), 0.5 / HSCALE, cand_in[:, t, :, :],
                                                 ALU.mult, ALU.add).then_inc(canqk_ready, 1)
                        dve.wait_ge(tz_ready, t + 1)
                        dve.tensor_scalar(zs[:, b, :], tz[:, b, :], 0.5, 0.5, ALU.mult, ALU.add).then_inc(zs_ready, 1)
                        dve.tensor_scalar(zc[:, b, :], tz[:, b, :], -0.5 * HSCALE, 0.5 * HSCALE, ALU.mult, ALU.add).then_inc(zc_ready, 1)
                        dve.wait_ge(zs_ready, t + 1)
                        dve.wait_ge(h_ready, t + 1)
                        dve.tensor_tensor(two(keep[:, b, :]), two(zs[:, b, :]), state[:, t, :, :], ALU.mult).then_inc(keep_ready, 1)
                        dve.wait_ge(zc_ready, t + 1)
                        dve.wait_ge(tn_ready, t + 1)
                        dve.tensor_tensor(new[:, b, :], zc[:, b, :], tn[:, b, :], ALU.mult).then_inc(new_ready, 1)
                        dve.wait_ge(keep_ready, t + 1)
                        dve.wait_ge(new_ready, t + 1)
                        dve.tensor_tensor(hp[:, 1 - b, 0, :], new[:, b, :], keep[:, b, :], ALU.add).then_inc(hi_ready, 1)
                        dve.tensor_tensor(state[:, t + 1, :, :], two(new[:, b, :]), two(keep[:, b, :]), ALU.add).then_inc(h_ready, 1)
                        dve.wait_ge(hi_ready, t + 2)
                        dve.wait_ge(h_ready, t + 2)
                        dve.tensor_tensor(two(hp[:, 1 - b, 1, :]), state[:, t + 1, :, :], two(hp[:, 1 - b, 0, :]),
                                          ALU.subtract).then_inc(lo_ready, 1)

            @block.tensor
            def _(pe):
                HIGH = [(0, 0), (1, 0), (2, 0), (3, 1), (4, 1)]
                LOW = [(0, 0), (1, 0), (3, 1)]

                def gate(out, g, b, part, terms):
                    for m in range(2):
                        for wi, k in terms:
                            last = pe.matmul(out[:, B * m:B * m + B], wp[:, wi, g, m, :], hp[:, b, part, B * k:B * k + B],
                                             start=False, stop=True, skip_group_check=True)
                    return last

                pe.wait_ge(weights_ready, 1)
                with pe.Fori(0, T // STEPS) as it:
                    for u in range(STEPS):
                        t, b = it * STEPS + u, u % 2
                        for p in range(3):
                            pe.matmul(ps_r[:, b, :2 * B], ident[:, :], gates_in[:, t, p, 2:4, :], start=p == 0, stop=p == 2, skip_group_check=True)
                            pe.matmul(ps_n[:, b, :2 * B], ident[:, :], bp[:, p, :, :], start=p == 0, stop=p == 2, skip_group_check=True)
                            pe.matmul(ps_z[:, b, :2 * B], ident[:, :], gates_in[:, t, p, 0:2, :], start=p == 0, stop=p == 2, skip_group_check=True)
                        pe.wait_ge(hi_ready, t + 1)
                        gate(ps_r[:, b, :], 1, b, 0, HIGH)
                        pe.wait_ge(lo_ready, t + 1)
                        gate(ps_r[:, b, :], 1, b, 1, LOW).then_inc(r_summed, 1)
                        gate(ps_n[:, b, :], 2, b, 0, HIGH)
                        gate(ps_n[:, b, :], 2, b, 1, LOW).then_inc(n_summed, 1)
                        gate(ps_z[:, b, :], 0, b, 0, HIGH)
                        gate(ps_z[:, b, :], 0, b, 1, LOW).then_inc(z_summed, 1)

            @block.scalar
            def _(act):
                with act.Fori(0, T // STEPS) as it:
                    for u in range(STEPS):
                        t, b = it * STEPS + u, u % 2
                        act.wait_ge(r_summed, t + 1)
                        act.activation(tr[:, b, :], ps_r[:, b, :2 * B], ACT.Tanh, scale=0.5 / HSCALE).then_inc(tr_ready, 1)
                        act.wait_ge(z_summed, t + 1)
                        act.activation(tz[:, b, :], ps_z[:, b, :2 * B], ACT.Tanh, scale=0.5 / HSCALE).then_inc(tz_ready, 1)
                        act.wait_ge(canqk_ready, t + 1)
                        act.activation(tn[:, b, :], cand[:, b, :], ACT.Tanh).then_inc(tn_ready, 1)


def gru_out(nc, state, wp_dram, x_sb, x_dram):
    with Scope(nc, "go") as s:
        w = s.sb("w", [128, 2, CB, CP])
        ps = s.ps("ps", 4)
        loaded, summed, added, stored = s.sem("loaded"), s.sem("summed"), s.sem("added"), s.sem("stored")
        with nc.Block() as block:
            @block.sync
            def _(sp):
                sp.dma_start(w[:, 0, :, :], wp_dram[0:128]).then_inc(loaded, 16)
                sp.dma_start(w[0:64, 1, :, :], wp_dram[128:192]).then_inc(loaded, 16)
                for n in range(NT):
                    sp.wait_ge(added, 2 * n + 2)
                    sp.dma_start(x_dram[:, :, n * TB:(n + 1) * TB], x_sb[:, :, n * TB:(n + 1) * TB]).then_inc(stored, 16)
                sp.wait_ge(stored, 16 * NT)

            @block.tensor
            def _(pe):
                pe.wait_ge(loaded, 32)
                for n in range(NT):
                    for m in range(CB):
                        i = 2 * n + m
                        if i >= 4:
                            pe.wait_ge(added, i - 3)
                        for k, rows in ((0, 128), (1, 64)):
                            last = pe.matmul(ps[:CP, i % 4, :TB], w[:rows, k, m, :],
                                             state[:rows, 1:T + 1, k, 2 * n:2 * n + 2].rearrange("p t b -> p b t"),
                                             start=k == 0, stop=k == 1)
                        last.then_inc(summed, 1)

            @block.vector
            def _(dve):
                for n in range(NT):
                    for m in range(CB):
                        i = 2 * n + m
                        dve.wait_ge(summed, i + 1)
                        x = x_sb[:, m, n * TB:(n + 1) * TB]
                        dve.scalar_tensor_tensor(x, ps[:CP, i % 4, :TB], 1.0 / HSCALE, x, ALU.mult, ALU.add).then_inc(added, 1)


def gru_layer(nc, ins, x_in, y_out):
    with Scope(nc, "l0") as s:
        x_sb = s.sb("x", [CP, CB, N])
        load_x(nc, "l0x", x_in, x_sb)
        with Scope(nc, "l0g") as s3:
            gates_in = s3.sb("gates_in", [128, T, 3, 4, B], bf16)
            cand_in = s3.sb("cand_in", [128, T, 2, B])
            with Scope(nc, "l0n") as s2:
                xh, xl = s2.sb("xh", [CP, CB, N], f32r), s2.sb("xl", [CP, CB, N], f32r)
                norm(nc, "n0", x_sb, ins["group_avg"], xh, xl)
                gru_inputs(nc, xh, xl, ins["wx"], ins["bx"], ins["bh"], gates_in, cand_in)
            with Scope(nc, "l0s") as s2:
                state = s2.sb("state", [128, T + 1, 2, B])
                gru(nc, gates_in, cand_in, state, ins["wh"], ins["bhn"], ins["ident128"])
                gru_out(nc, state, ins["wp"], x_sb, y_out)


def values(nc, tag, xh, xl, wv_dram, bv_dram, v):
    with Scope(nc, tag) as s:
        w = s.sb("w", [CP, CB, C])
        wh, wl = s.sb("wh", [CP, CB, C], f32r), s.sb("wl", [CP, CB, C], f32r)
        bias = s.sb("bias", [128, C])
        ps = s.ps("ps", 4)
        loaded, wh_ready, wl_ready = s.sem("loaded"), s.sem("wh_ready"), s.sem("wl_ready")
        summed, added = s.sem("summed"), s.sem("added")
        with nc.Block() as block:
            @block.sync
            def _(sp):
                sp.dma_start(w[:, :, :], wv_dram).then_inc(loaded, 16)
                sp.dma_start(bias[:TH, :], bv_dram).then_inc(loaded, 16)

            @block.tensor
            def _(pe):
                pe.wait_ge(wl_ready, 1)
                for i in range(2 * B):
                    if i >= 4:
                        pe.wait_ge(added, i - 3)
                    tok = slice(i * TH, (i + 1) * TH)
                    product3(pe, ps[:TH, i % 4, :C], lambda k: xh[:, k, tok], lambda k: xl[:, k, tok],
                             lambda k: wh[:, k, :], lambda k: wl[:, k, :]).then_inc(summed, 1)

            @block.vector
            def _(dve):
                dve.wait_ge(loaded, 32)
                split(dve, w[:, :, :], wh[:, :, :], wl[:, :, :], wh_ready, wl_ready, 0)
                for i in range(2 * B):
                    dve.wait_ge(summed, i + 1)
                    dve.tensor_tensor(v[:TH, i, :], ps[:TH, i % 4, :C], bias[:TH, :], ALU.add).then_inc(added, 1)
                dve.wait_ge(added, 2 * B)


def attention(nc, tag, xh, xl, v, w_dram, b_dram, signs_dram, rel_dram, sel_dram, ident_dram,
              products, sums):
    with Scope(nc, tag) as s:
        qk = s.sb("qk", [128, N], f32r)
        q = [s.sb("q_a", [128, N], f32r), s.sb("q_b", [128, N], f32r)]
        k = [s.sb("k_a", [128, N], f32r), s.sb("k_b", [128, N], f32r)]
        rel = s.sb("rel", [128, N], f32r)
        vs = s.sb("vs", [128, 2 * B, 2, 33], f32r)
        w = s.sb("w", [CP, CB, 128])
        wh, wl = s.sb("wh", [CP, CB, 128], f32r), s.sb("wl", [CP, CB, 128], f32r)
        bias, bias2 = s.sb("bias", [128, 1]), s.sb("bias2", [128, 2])
        signs = s.sb("signs", [128, 2])
        rw = s.sb("rw", [128, H + W, 28])
        rh, rl = s.sb("rh", [128, H + W, 28], f32r), s.sb("rl", [128, H + W, 28], f32r)
        ident = s.sb("ident", [128, TH])
        hx, xx = s.sb("hx", [128, 2, TB], f32r), s.sb("xx", [128, 2, TB])
        mx = s.sb("mx", [128, 2, 4])
        mt = s.sb("mt", [128, 2, 128])
        p32, ph, pl = s.sb("p32", [128, 2, 2, TB]), s.sb("ph", [128, 3, 2, TB], f32r), s.sb("pl", [128, 2, 2, TB], f32r)
        o = s.sb("o", [33, 2, 2, TB])
        flag = s.sb("flag", [1, 1])
        sel = s.sb("sel", [128, T])
        ps = s.ps("ps", 8)
        S_BANK, X_BANK, T_BANK, O_BANK = 0, 2, 3, 7

        loaded, const_ready, zeroed = s.sem("loaded"), s.sem("const_ready"), s.sem("zeroed")
        rh_ready, rl_ready, w_in, wh_ready, wl_ready = (s.sem(n) for n in ("rh_ready", "rl_ready", "w_in", "wh_ready", "wl_ready"))
        bias_ready, vh_ready, vl_ready, qk_summed = (s.sem(n) for n in ("bias_ready", "vh_ready", "vl_ready", "qk_summed"))
        hx_ready, xx_ready, qk_ready, q_zero, qk_moved = (s.sem(n) for n in ("hx_ready", "xx_ready", "qk_ready", "q_zero", "qk_moved"))
        rel_summed, rel_high, rel_low, rel_moved = (s.sem(n) for n in ("rel_summed", "rel_high", "rel_low", "rel_moved"))
        s_summed, mx_ready, mh_ready, ml_ready = (s.sem(n) for n in ("s_summed", "mx_ready", "mh_ready", "ml_ready"))
        x_ready, x_copied, t_summed, p_ready = (s.sem(n) for n in ("x_ready", "x_copied", "t_summed", "p_ready"))
        pl_ready, o_summed, o_ready = (s.sem(n) for n in ("pl_ready", "o_summed", "o_ready"))
        o_stored = [s.sem("even_stored"), s.sem("odd_stored")]
        pair_free = s.sem("pair_free")

        def two(x):
            return x.rearrange("p (h k) -> p h k", h=2)

        with nc.Block() as block:
            @block.sync
            def _(sp):
                sp.dma_start(signs[:, :], signs_dram).then_inc(loaded, 16)
                sp.dma_start(rw[:, :, :], rel_dram).then_inc(loaded, 16)
                sp.dma_start(ident[:TH, :], ident_dram).then_inc(loaded, 16)
                sp.dma_start(sel[:, :], sel_dram).then_inc(loaded, 16)
                sp.wait_ge(const_ready, 2 * B)
                sp.wait_ge(q_zero, 3)
                with sp.Fori(0, PAIRS) as p:
                    sp.wait_ge(pair_free, p + 1)
                    sp.dma_start(w[:, :, :], w_dram[bass.ds(p, 1)].rearrange("a p k n -> (a p) k n")).then_inc(w_in, 16)
                    sp.dma_start(bias[:, :], b_dram[bass.ds(p, 1)].rearrange("a p k -> (a p) k")).then_inc(w_in, 16)
                    for head in range(2):
                        sp.dma_start(q[head][64:66, :].bitcast(f32), k[head][60:62, :].bitcast(f32)).then_inc(qk_moved, 16)
                    sp.wait_ge(qk_ready, p * NT + NT)
                    for head in range(2):
                        for dst, at, src, rows in ((q, 0, 0, 32), (q, 80, 0, 16), (k, 0, 32, 16), (k, 16, 32, 16), (k, 80, 48, 16)):
                            src += 64 * head
                            sp.dma_start(dst[head][at:at + rows, :].bitcast(f32),
                                         qk[src:src + rows, :].bitcast(f32)).then_inc(qk_moved, 16)
                    sp.wait_ge(rel_low, p * 14 + 14)
                    for head in range(2):
                        for at, src in ((32, 0), (46, 32), (96, 64), (110, 96)):
                            src += 14 * head
                            sp.dma_start(q[head][at:at + 14, :].bitcast(f32),
                                         rel[src:src + 14, :].bitcast(f32)).then_inc(rel_moved, 16)
                    for j in range(NT):
                        sp.wait_ge(o_ready, p * B + 2 * j + 2)
                        cols = slice(j * TB, (j + 1) * TB)
                        sp.dma_start(products[bass.ds(p * 2, 2), :, cols].rearrange("h r n -> r h n"),
                                     o[0:32, j % 2, :, :]).then_inc(o_stored[j % 2], 16)
                        sp.dma_start(sums[bass.ds(p * 2, 2), cols].rearrange("(a h) n -> a h n", a=1),
                                     o[32:33, j % 2, :, :]).then_inc(o_stored[j % 2], 16)
                for slot in range(2):
                    sp.wait_ge(o_stored[slot], PAIRS * 8 * B)

            @block.gpsimd
            def _(pool):
                pool.memset(mt[:, :, :], 0.0).then_inc(zeroed, 1)
                pool.memset(vs[:, :, :, 32:33].bitcast(f32), 1.0).then_inc(zeroed, 1)
                for head in range(2):
                    pool.memset(q[head][:, :].bitcast(f32), 0.0).then_inc(q_zero, 1)
                pool.memset(flag[:, :], 0.0).then_inc(q_zero, 1)
                pool.wait_ge(loaded, 64)
                split(pool, rw[:, :, :], rh[:, :, :], rl[:, :, :], rh_ready, rl_ready, 0)
                pool.wait_ge(rl_ready, 1)
                with pool.Fori(0, PAIRS) as p:
                    for t in range(NT):
                        pool.wait_ge(hx_ready, p * NT + t + 1)
                        pool.wait_ge(xx_ready, p * NT + t + 1)
                        pool.tensor_tensor(qk[:, t * TB:(t + 1) * TB], xx[:, t % 2, :], hx[:, t % 2, :].bitcast(f32),
                                           ALU.subtract).then_inc(qk_ready, 1)
                    for b in range(B):
                        g = p * B + b
                        pool.wait_ge(p_ready, 2 * g + 2)
                        if b >= 2:
                            pool.wait_ge(o_summed, g - 1)
                        pool.tensor_tensor(pl[:TH, b % 2, :, :], p32[:TH, b % 2, :, :], ph[:TH, b % 3, :, :].bitcast(f32),
                                           ALU.subtract).then_inc(pl_ready, 1)

            @block.tensor
            def _(pe):
                pe.wait_ge(zeroed, 2)
                pe.wait_ge(rl_ready, 1)
                with pe.Fori(0, PAIRS) as p:
                    pe.wait_ge(pair_free, p + 1)
                    pe.wait_ge(wl_ready, p + 1)
                    for t in range(NT):
                        if t >= 4:
                            pe.wait_ge(xx_ready, p * NT + t - 3)
                        product3(pe, ps[:, t % 4, :TB], lambda k: wh[:, k, :], lambda k: wl[:, k, :],
                                 lambda k: xh[:, k, t * TB:(t + 1) * TB],
                                 lambda k: xl[:, k, t * TB:(t + 1) * TB]).then_inc(qk_summed, 1)
                    pe.wait_ge(qk_ready, p * NT + NT)
                    q4 = qk[:, :].rearrange("p (b h w) -> p h w b", b=B, h=H)
                    for j in range(14):
                        if j >= 4:
                            pe.wait_ge(rel_low, p * 14 + j - 3)
                        for u in range(2):
                            n = 2 * j + u
                            qs = q4[:, n, :, :].rearrange("p w b -> p b w") if n < H else q4[:, :, n - H, :].rearrange("p h b -> p b h")
                            out = ps[:28, 4 + j % 4, u * 224:u * 224 + 224]
                            pe.matmul(out, rh[:, n, :], qs, start=True, stop=False)
                            last = pe.matmul(out, rl[:, n, :], qs, start=False, stop=True)
                        last.then_inc(rel_summed, 1)

                    def logits_by_query(b):
                        if b == 0:
                            pe.wait_ge(qk_moved, p * 192 + 192)
                            pe.wait_ge(rel_moved, p * 128 + 128)
                            pe.wait_ge(vl_ready, p + 1)
                        else:
                            pe.wait_ge(mx_ready, p * B + b)
                        keys = slice(b * T, (b + 1) * T)
                        for head in range(2):
                            for half in range(2):
                                queries = slice(b * T + half * TH, b * T + (half + 1) * TH)
                                last = pe.matmul(ps[:TH, S_BANK + head, half * T:half * T + T], q[head][:, queries],
                                                 k[head][:, keys], start=True, stop=True)
                        last.then_inc(s_summed, 1)

                    def maxima_to_rows(b):
                        pe.wait_ge(ml_ready, p * B + b + 1)
                        if b >= 1:
                            pe.wait_ge(x_copied, 2 * (p * B + b))
                        for half in range(2):
                            last = pe.transpose(ps[:, X_BANK, half * TH:half * TH + TH], mt[:TH, half, :], ident[:TH, :])
                        last.then_inc(x_ready, 1)

                    def logits_by_key(b):
                        pe.wait_ge(x_copied, 2 * (p * B + b) + 2)
                        if b >= 2:
                            pe.wait_ge(p_ready, 2 * (p * B + b) - 2)
                        queries = slice(b * T, (b + 1) * T)
                        for head in range(2):
                            for half in range(2):
                                keys = slice(b * T + half * TH, b * T + (half + 1) * TH)
                                last = pe.matmul(ps[:TH, T_BANK + 2 * (b % 2) + head, half * T:half * T + T], k[head][:, keys],
                                                 q[head][:, queries], start=True, stop=True)
                        last.then_inc(t_summed, 1)

                    def weigh_values(b):
                        pe.wait_ge(pl_ready, p * B + b + 1)
                        if b >= 1:
                            pe.wait_ge(o_ready, p * B + b)
                        for head in range(2):
                            for half in range(2):
                                lhs = vs[:TH, 2 * b + half, head, :]
                                out = ps[:33, O_BANK, head * T:head * T + T]
                                pe.matmul(out, lhs, ph[:TH, b % 3, head, half * T:half * T + T], start=half == 0, stop=False)
                                last = pe.matmul(out, lhs, pl[:TH, b % 2, head, half * T:half * T + T], start=False, stop=half == 1)
                        last.then_inc(o_summed, 1)

                    for i in range(B + 4):
                        if i < B:
                            logits_by_query(i)
                        if 1 <= i <= B:
                            maxima_to_rows(i - 1)
                        if i >= 4:
                            weigh_values(i - 4)
                        if 1 <= i <= B:
                            logits_by_key(i - 1)

            @block.scalar
            def _(act):
                act.wait_ge(loaded, 64)
                with act.Fori(0, PAIRS) as p:
                    act.wait_ge(bias_ready, 2 * p + 2)
                    for t in range(NT):
                        act.wait_ge(qk_summed, p * NT + t + 1)
                        if t >= 2:
                            act.wait_ge(qk_ready, p * NT + t - 1)
                        act.activation(hx[:, t % 2, :], ps[:, t % 4, :TB], ACT.Identity, scale=signs[:, 0:1],
                                       bias=bias2[:, 0:1]).then_inc(hx_ready, 1)
                        act.activation(xx[:, t % 2, :], ps[:, t % 4, :TB], ACT.Identity, scale=signs[:, 1:2],
                                       bias=bias2[:, 1:2]).then_inc(xx_ready, 1)
                    for j in range(14):
                        act.wait_ge(rel_summed, p * 14 + j + 1)
                        act.activation(rel_out(rel, j, 0), rel_in(ps, j), ACT.Copy).then_inc(rel_high, 1)
                    for b in range(B + 1):
                        if b < B:
                            act.wait_ge(x_ready, p * B + b + 1)
                            cols = slice(b * T, (b + 1) * T)
                            for head in range(2):
                                r = 64 + 32 * head
                                act.activation(q[head][64:66, cols], ps[r:r + 2, X_BANK, :T], ACT.Copy).then_inc(x_copied, 1)
                        if b >= 1:
                            c = b - 1
                            act.wait_ge(t_summed, p * B + c + 1)
                            if c >= 3:
                                act.wait_ge(o_summed, p * B + c - 2)
                            if c >= 2:
                                act.wait_ge(pl_ready, p * B + c - 1)
                            banks = ps[:TH, T_BANK + 2 * (c % 2):T_BANK + 2 * (c % 2) + 2, :TB]
                            act.activation(ph[:TH, c % 3, :, :], banks, ACT.Exp).then_inc(p_ready, 1)
                            act.activation(p32[:TH, c % 2, :, :], banks, ACT.Exp).then_inc(p_ready, 1)

            @block.vector
            def _(dve):
                dve.wait_ge(q_zero, 3)
                dve.tensor_copy(flag[:, :], flag[:, :]).then_inc(pair_free, 1)
                dve.wait_ge(loaded, 64)
                for b in range(B):
                    for head in range(2):
                        dve.tensor_copy(k[head][:, b * T:(b + 1) * T], sel[:, :]).then_inc(const_ready, 1)
                dve.wait_ge(zeroed, 2)
                with dve.Fori(0, PAIRS) as p:
                    dve.wait_ge(w_in, 32 * p + 32)
                    dve.tensor_copy(wh[:, :, :], w[:, :, :]).then_inc(wh_ready, 1)
                    for n in range(2):
                        dve.tensor_tensor(bias2[:, n:n + 1], bias[:, :], signs[:, n:n + 1], ALU.mult).then_inc(bias_ready, 1)
                    dve.wait_ge(wh_ready, p + 1)
                    dve.tensor_tensor(wl[:, :, :], w[:, :, :], wh[:, :, :].bitcast(f32), ALU.subtract).then_inc(wl_ready, 1)
                    vp = v[:TH, :, bass.ds(p * 32, 32)].rearrange("t i (h d) -> t i h d", h=2)
                    vhi, vlo = vs[:TH, :, :, 0:HD], vs[:TH, :, :, HD:2 * HD]
                    dve.tensor_copy(vhi, vp).then_inc(vh_ready, 1)
                    dve.wait_ge(vh_ready, p + 1)
                    dve.tensor_tensor(vlo, vp, vhi.bitcast(f32), ALU.subtract).then_inc(vl_ready, 1)
                    for j in range(14):
                        dve.wait_ge(rel_high, p * 14 + j + 1)
                        dve.tensor_tensor(rel_out(rel, j, 64), rel_in(ps, j), rel_out(rel, j, 0).bitcast(f32),
                                          ALU.subtract).then_inc(rel_low, 1)
                    for b in range(B + 4):
                        if b < B:
                            g = p * B + b
                            dve.wait_ge(s_summed, g + 1)
                            dve.tensor_reduce(mx[:TH, b % 2, :], ps[:TH, S_BANK:S_BANK + 2, :TB].rearrange("p c (h k) -> p c h k", h=2),
                                              AXIS.X, ALU.max).then_inc(mx_ready, 1)
                            m = mx[:TH, b % 2, :].rearrange("p (c h) -> p h c", c=2)
                            high, low = mt[:TH, :, 64:97:32], mt[:TH, :, 65:98:32]
                            dve.wait_ge(mx_ready, g + 1)
                            if b >= 1:
                                dve.wait_ge(x_ready, g)
                            dve.tensor_copy(high.bitcast(f32r), m).then_inc(mh_ready, 1)
                            dve.wait_ge(mh_ready, g + 1)
                            dve.tensor_tensor(low, m, high, ALU.subtract).then_inc(ml_ready, 1)
                        if b >= 4:
                            c = b - 4
                            g = p * B + c
                            dve.wait_ge(o_summed, g + 1)
                            j = c // 2
                            if c % 2 == 0 and j >= 2:
                                dve.wait_ge(o_stored[j % 2], 8 * B * p + 32 * (j // 2))
                            dve.tensor_copy(o[:, j % 2, :, c % 2 * T:c % 2 * T + T], two(ps[:33, O_BANK, :TB])).then_inc(o_ready, 1)
                    for slot in range(2):
                        dve.wait_ge(o_stored[slot], 8 * B * p + 8 * B)
                    dve.tensor_copy(flag[:, :], flag[:, :]).then_inc(pair_free, 1)


def rel_in(ps, j):
    return ps[:28, 4 + j % 4, :448].rearrange("p (u b w) -> p u b w", u=2, b=B)


def rel_out(rel, j, low):
    part = 0 if j < 7 else 32
    n = 2 * (j % 7)
    tile = rel[low + part:low + part + 28, :].rearrange("p (b h w) -> p h b w", b=B, h=H)
    return tile[:, n:n + 2, :, :] if j < 7 else tile.rearrange("p h b w -> p w b h")[:, n:n + 2, :, :]


def project(nc, tag, products, sums, w_dram, b_dram, x_dram, y_dram):
    KC = HEADS * 32 // 128
    SLOTS = 4
    with Scope(nc, tag) as s:
        w = s.sb("w", [128, KC, CB, CP])
        bias = s.sb("bias", [CP, CB])
        den, rec = s.sb("den", [128, HEADS * N // 128]), s.sb("rec", [128, HEADS * N // 128])
        hin, rin = s.sb("hin", [128, SLOTS, KC, TB]), s.sb("rin", [128, SLOTS, KC, TB])
        hn = s.sb("hn", [128, 2, KC, TB])
        xin = s.sb("xin", [CP, SLOTS, CB, TB])
        y = s.sb("y", [CP, 2, CB, TB])
        ps = s.ps("ps", 4)
        loaded, den_in, rec_ready, rec_stored = (s.sem(n) for n in ("loaded", "den_in", "rec_ready", "rec_stored"))
        summed, added, scaled = s.sem("summed"), s.sem("added"), s.sem("scaled")
        stored = [s.sem("even_stored"), s.sem("odd_stored")]
        slot_in = [s.sem(f"slot{n}_in") for n in range(SLOTS)]
        LOADS = 6
        with nc.Block() as block:
            @block.sync
            def _(sp):
                sp.dma_start(den[:, :], sums.rearrange("h n -> (h n)").rearrange("(p f) -> p f", p=128)).then_inc(den_in, 16)
                sp.dma_start(w[:, :, :, :], w_dram).then_inc(loaded, 16)
                sp.dma_start(bias[:, :], b_dram).then_inc(loaded, 16)
                for n in range(NT):
                    cols = slice(n * TB, (n + 1) * TB)
                    if n >= SLOTS:
                        sp.wait_ge(added, 2 * (n - SLOTS) + 2)
                    sp.dma_start(hin[:, n % SLOTS, :, :], products[:, :, cols].rearrange("(k h) r n -> (h r) k n", k=KC)).then_inc(slot_in[n % SLOTS], 16)
                    sp.dma_start(xin[:, n % SLOTS, :, :], x_dram[:, :, cols]).then_inc(slot_in[n % SLOTS], 16)
                    if n == 0:
                        sp.wait_ge(rec_stored, 16)
                    for h in range(4):
                        sp.dma_start(rin[32 * h:32 * h + 32, n % SLOTS, :, :],
                                     sums.rearrange("(a k h) n -> h a k n", a=1, h=4)[h, :, :, cols].to_broadcast([32, KC, TB])).then_inc(slot_in[n % SLOTS], 16)
                for slot in range(2):
                    sp.wait_ge(stored[slot], 8 * NT)

            @block.scalar
            def _(act):
                act.wait_ge(rec_ready, 1)
                act.dma_start(sums.rearrange("h n -> (h n)").rearrange("(p f) -> p f", p=128), rec[:, :]).then_inc(rec_stored, 16)
                for n in range(NT):
                    act.wait_ge(added, 2 * n + 2)
                    act.dma_start(y_dram[:, :, n * TB:(n + 1) * TB], y[:, n % 2, :, :]).then_inc(stored[n % 2], 16)

            @block.tensor
            def _(pe):
                pe.wait_ge(loaded, 32)
                for n in range(NT):
                    pe.wait_ge(scaled, n + 1)
                    for m in range(CB):
                        i = 2 * n + m
                        if i >= 4:
                            pe.wait_ge(added, i - 3)
                        for k in range(KC):
                            last = pe.matmul(ps[:CP, i % 4, :TB], w[:, k, m, :], hn[:, n % 2, k, :], start=k == 0, stop=k == KC - 1)
                        last.then_inc(summed, 1)

            @block.gpsimd
            def _(pool):
                for n in range(NT):
                    pool.wait_ge(slot_in[n % SLOTS], 16 * LOADS * (n // SLOTS + 1))
                    if n >= 2:
                        pool.wait_ge(summed, 2 * n - 2)
                    pool.tensor_tensor(hn[:, n % 2, :, :], hin[:, n % SLOTS, :, :], rin[:, n % SLOTS, :, :], ALU.mult).then_inc(scaled, 1)

            @block.vector
            def _(dve):
                dve.wait_ge(den_in, 16)
                dve.reciprocal(rec[:, :], den[:, :]).then_inc(rec_ready, 1)
                dve.wait_ge(loaded, 32)
                for n in range(NT):
                    dve.wait_ge(slot_in[n % SLOTS], 16 * LOADS * (n // SLOTS + 1))
                    if n >= 2:
                        dve.wait_ge(stored[n % 2], 16 * (n // 2))
                    for m in range(CB):
                        i = 2 * n + m
                        dve.wait_ge(summed, i + 1)
                        dve.scalar_tensor_tensor(y[:, n % 2, m, :], ps[:CP, i % 4, :TB], bias[:, m:m + 1], xin[:, n % SLOTS, m, :],
                                                 ALU.add, ALU.add).then_inc(added, 1)


def attention_layer(nc, tag, ins, x_in, y_out, scratch):
    with Scope(nc, tag) as s:
        xh, xl = s.sb("xh", [CP, CB, N], f32r), s.sb("xl", [CP, CB, N], f32r)
        v = s.sb("v", [128, 2 * B, C])
        with Scope(nc, tag + "x") as s2:
            x_sb = s2.sb("x", [CP, CB, N])
            load_x(nc, tag + "ld", x_in, x_sb)
            norm(nc, tag + "n", x_sb, ins["group_avg"], xh, xl)
        values(nc, tag + "v", xh, xl, ins[tag + "_wv"], ins[tag + "_bv"], v)
        attention(nc, tag + "a", xh, xl, v, ins[tag + "_wqk"], ins[tag + "_bqk"], ins["signs"], ins[tag + "_rel"],
                  ins["sel"], ins["ident98"],
                  scratch["products"], scratch["sums"])
    project(nc, tag + "p", scratch["products"], scratch["sums"], ins[tag + "_wo"], ins[tag + "_bo"], x_in, y_out)


def route(nc, xh, xl, gate_dram, first_dram, ident_dram, w_rows):
    HALVES = 2 * B
    with Scope(nc, "ro") as s:
        g = s.sb("g", [CP, CB, E])
        gh, gl = s.sb("gh", [CP, CB, E], f32r), s.sb("gl", [CP, CB, E], f32r)
        ident = s.sb("ident", [128, TH])
        first = s.sb("first", [128, E])
        by_expert = s.sb("by_expert", [E, N])
        logit, seen = s.sb("logit", [128, HALVES, E]), s.sb("seen", [128, HALVES, E])
        key, pick1, pick2 = s.sb("key", [128, HALVES, E]), s.sb("pick1", [128, HALVES, E]), s.sb("pick2", [128, HALVES, E])
        m1, m2, km, d, e2, den, w1, w2 = (s.sb(n, [128, HALVES]) for n in "m1 m2 km d e2 den w1 w2".split())
        wt = s.sb("wt", [128, HALVES, 2 * E])
        ps = s.ps("ps", 8)
        loaded, gh_ready, gl_ready, summed = (s.sem(n) for n in ("loaded", "gh_ready", "gl_ready", "summed"))
        copied, turned, chain, m_diff, e2_ready = (s.sem(n) for n in ("copied", "turned", "chain", "m_diff", "e2_ready"))
        wt_ready, back_turned, rows_ready = (s.sem(n) for n in ("wt_ready", "back_turned", "rows_ready"))
        with nc.Block() as block:
            @block.sync
            def _(sp):
                sp.dma_start(g[:, :, :], gate_dram).then_inc(loaded, 16)
                sp.dma_start(ident[:TH, :], ident_dram).then_inc(loaded, 16)
                sp.dma_start(first[:TH, :], first_dram).then_inc(loaded, 16)

            @block.tensor
            def _(pe):
                pe.wait_ge(gl_ready, 1)
                for t in range(NT):
                    if t >= 4:
                        pe.wait_ge(copied, t - 3)
                    product3(pe, ps[:E, t % 4, :TB], lambda k: gh[:, k, :], lambda k: gl[:, k, :],
                             lambda k: xh[:, k, t * TB:(t + 1) * TB], lambda k: xl[:, k, t * TB:(t + 1) * TB]).then_inc(summed, 1)
                pe.wait_ge(copied, NT)
                for i in range(HALVES):
                    last = pe.transpose(ps[:TH, 4, i * E:(i + 1) * E], by_expert[:, i * TH:(i + 1) * TH], ident[:E, :E])
                last.then_inc(turned, 1)
                pe.wait_ge(wt_ready, 2)
                for i in range(HALVES):
                    last = pe.transpose(ps[:2 * E, i // 4, (i % 4) * TH:(i % 4 + 1) * TH], wt[:TH, i, :], ident[:TH, :])
                    if i % 4 == 3:
                        last.then_inc(back_turned, 1)

            @block.scalar
            def _(act):
                for t in range(NT):
                    act.wait_ge(summed, t + 1)
                    act.activation(by_expert[:, t * TB:(t + 1) * TB], ps[:E, t % 4, :TB], ACT.Copy).then_inc(copied, 1)
                act.wait_ge(m_diff, 1)
                act.activation(e2[:TH, :], d[:TH, :], ACT.Exp).then_inc(e2_ready, 1)
                for t in range(NT):
                    act.wait_ge(back_turned, t + 1)
                    act.activation(w_rows[:, t * TB:(t + 1) * TB], ps[:2 * E, t, :TB], ACT.Copy).then_inc(rows_ready, 1)
                act.wait_ge(rows_ready, NT)

            @block.vector
            def _(dve):
                dve.wait_ge(loaded, 48)
                split(dve, g[:, :, :], gh[:, :, :], gl[:, :, :], gh_ready, gl_ready, 0)
                done = [0]

                def link(ins):
                    done[0] += 1
                    ins.then_inc(chain, 1)
                    dve.wait_ge(chain, done[0])

                def over(x):
                    return x[:TH, :].rearrange("p (i a) -> p i a", a=1).to_broadcast([TH, HALVES, E])

                rank = first[:TH, :].rearrange("p (a e) -> p a e", a=1).to_broadcast([TH, HALVES, E])

                def largest(values, m, pick):
                    link(dve.tensor_reduce(m[:TH, :], values[:TH, :, :], AXIS.X, ALU.max))
                    link(dve.tensor_tensor(key[:TH, :, :], values[:TH, :, :], over(m), ALU.is_equal))
                    link(dve.tensor_tensor(key[:TH, :, :], key[:TH, :, :], rank, ALU.mult))
                    link(dve.tensor_reduce(km[:TH, :], key[:TH, :, :], AXIS.X, ALU.max))
                    link(dve.tensor_tensor(pick[:TH, :, :], key[:TH, :, :], over(km), ALU.is_equal))

                dve.wait_ge(turned, 1)
                link(dve.tensor_copy(logit[:TH, :, :], ps[:TH, 4, :HALVES * E].rearrange("p (i e) -> p i e", e=E)))
                largest(logit, m1, pick1)
                link(dve.scalar_tensor_tensor(seen[:TH, :, :], pick1[:TH, :, :], NEG, logit[:TH, :, :], ALU.mult, ALU.add))
                largest(seen, m2, pick2)
                dve.tensor_tensor(d[:TH, :], m2[:TH, :], m1[:TH, :], ALU.subtract).then_inc(m_diff, 1)
                dve.wait_ge(e2_ready, 1)
                link(dve.tensor_scalar(den[:TH, :], e2[:TH, :], 1.0, None, ALU.add))
                link(dve.reciprocal(w1[:TH, :], den[:TH, :]))
                link(dve.tensor_tensor(w2[:TH, :], e2[:TH, :], w1[:TH, :], ALU.mult))
                link(dve.tensor_tensor(pick1[:TH, :, :], pick1[:TH, :, :], over(w1), ALU.mult))
                link(dve.tensor_tensor(pick2[:TH, :, :], pick2[:TH, :, :], over(w2), ALU.mult))
                link(dve.tensor_tensor(key[:TH, :, :], pick1[:TH, :, :], pick2[:TH, :, :], ALU.add))
                dve.tensor_copy(wt[:TH, :, :E].bitcast(f32r), key[:TH, :, :]).then_inc(wt_ready, 1)
                dve.wait_ge(wt_ready, 1)
                dve.tensor_tensor(wt[:TH, :, E:].bitcast(f32r), key[:TH, :, :], wt[:TH, :, :E], ALU.subtract).then_inc(wt_ready, 1)


def experts(nc, xh, xl, w_rows, w1_dram, b1_dram, w2_dram, b2_dram, pick_dram, x_sb):
    with Scope(nc, "ex") as s:
        w1, w2 = s.sb("w1", [CP, CB, F]), s.sb("w2", [128, FB, C])
        w1h, w1l = s.sb("w1h", [CP, 2, CB, F], f32r), s.sb("w1l", [CP, 2, CB, F], f32r)
        w2h, w2l = s.sb("w2h", [128, 2, FB, C], f32r), s.sb("w2l", [128, 2, FB, C], f32r)
        b1, b2 = s.sb("b1", [128, 2, FB]), s.sb("b2", [CP, 2, CB])
        pick32 = s.sb("pick32", [2 * E, 2, CP])
        pick = s.sb("pick", [2 * E, 2, CP], f32r)
        hh, hl = s.sb("hh", [128, 2, FB, TB], f32r), s.sb("hl", [128, 2, FB, TB], f32r)
        h32 = s.sb("h32", [128, 2, TB])
        wb = s.sb("wb", [CP, 2, TB])
        y = s.sb("y", [CP, 2, CB, TB])
        ps_u, ps_d, ps_w = s.ps("ps_u", 4), s.ps("ps_d", 2), s.ps("ps_w", 2)
        big_in, small_in = s.sem("big_in"), [s.sem("even_in"), s.sem("odd_in")]
        high_ready, low_ready, pick_ready = s.sem("high_ready"), s.sem("low_ready"), s.sem("pick_ready")
        up_summed, hh_ready, h32_ready, hl_ready = (s.sem(n) for n in ("up_summed", "hh_ready", "h32_ready", "hl_ready"))
        down_summed, wb_summed, wb_ready, y_ready, x_added = (
            s.sem(n) for n in ("down_summed", "wb_summed", "wb_ready", "y_ready", "x_added"))

        def for_all_experts(eng, body):
            body(0, 0, True, False)
            with eng.Fori(0, (E - 2) // 2) as it:
                for u in (1, 0):
                    body(it * 2 + (1 if u else 2), u, False, False)
            body(E - 1, 1, False, True)

        with nc.Block() as block:
            @block.sync
            def _(sp):
                for e in range(E):
                    if e >= 1:
                        sp.wait_ge(low_ready, 2 * e)
                    sp.dma_start(w1[:, :, :], w1_dram[e]).then_inc(big_in, 16)
                    sp.dma_start(w2[:, :, :], w2_dram[e]).then_inc(big_in, 16)
                    if e >= 2:
                        sp.wait_ge(y_ready, 2 * NT * (e - 1))
                    for dst, src in ((b1, b1_dram), (b2, b2_dram), (pick32, pick_dram)):
                        sp.dma_start(dst[:, e % 2, :], src[e]).then_inc(small_in[e % 2], 16)

            @block.tensor
            def _(pe):
                def down(i, t, u):
                    pe.wait_ge(hl_ready, 4 * i + 4)
                    for m in range(CB):
                        if not (isinstance(i, int) and i == 0):
                            pe.wait_ge(y_ready, 2 * i + m - 1)
                        cols = slice(m * CP, (m + 1) * CP)
                        product3(pe, ps_d[:CP, m, :TB], lambda k: w2h[:, u, k, cols], lambda k: w2l[:, u, k, cols],
                                 lambda k: hh[:, t % 2, k, :], lambda k: hl[:, t % 2, k, :], blocks=FB).then_inc(down_summed, 1)

                def body(e, u, first, last):
                    pe.wait_ge(low_ready, 2 * e + 2)
                    pe.wait_ge(pick_ready, e + 1)
                    for t in range(NT):
                        i = e * NT + t
                        tok = slice(t * TB, (t + 1) * TB)
                        for f in range(FB):
                            if not (first and t == 0):
                                pe.wait_ge(h32_ready, 4 * i + f - 3)
                            rows = slice(f * 128, (f + 1) * 128)
                            product3(pe, ps_u[:, f, :TB], lambda k: w1h[:, u, k, rows], lambda k: w1l[:, u, k, rows],
                                     lambda k: xh[:, k, tok], lambda k: xl[:, k, tok]).then_inc(up_summed, 1)
                        if not (first and t < 2):
                            pe.wait_ge(wb_ready, i - 1)
                        pe.matmul(ps_w[:CP, t % 2, :TB], pick[:, u, :], w_rows[:, tok], start=True, stop=True).then_inc(wb_summed, 1)
                        if not (first and t == 0):
                            down(i - 1, (t - 1) % NT, u if t else 1 - u)
                    if last:
                        down(e * NT + NT - 1, NT - 1, u)

                for_all_experts(pe, body)

            @block.scalar
            def _(act):
                def body(e, u, first, last):
                    act.wait_ge(small_in[u], 48 * ((e - u) // 2 + 1) if isinstance(e, int) else 24 * (e - u) + 48)
                    for t in range(NT):
                        i = e * NT + t
                        for f in range(FB):
                            act.wait_ge(up_summed, 4 * i + f + 1)
                            if f == 0 and not (first and t < 2):
                                act.wait_ge(down_summed, 2 * i - 2)
                            act.activation(hh[:, t % 2, f, :], ps_u[:, f, :TB], ACT.Gelu, bias=b1[:, u, f:f + 1]).then_inc(hh_ready, 1)
                            if not (first and t == 0 and f < 2):
                                act.wait_ge(hl_ready, 4 * i + f - 1)
                            act.activation(h32[:, f % 2, :], ps_u[:, f, :TB], ACT.Gelu, bias=b1[:, u, f:f + 1]).then_inc(h32_ready, 1)
                        act.wait_ge(wb_summed, i + 1)
                        if not (first and t < 2):
                            act.wait_ge(y_ready, 2 * i - 2)
                        act.activation(wb[:, t % 2, :], ps_w[:CP, t % 2, :TB], ACT.Copy).then_inc(wb_ready, 1)

                for_all_experts(act, body)

            @block.vector
            def _(dve):
                def prepare(e, u):
                    dve.wait_ge(big_in, 32 * e + 32)
                    dve.tensor_copy(w1h[:, u, :, :], w1[:, :, :]).then_inc(high_ready, 1)
                    dve.tensor_copy(w2h[:, u, :, :], w2[:, :, :]).then_inc(high_ready, 1)
                    dve.wait_ge(small_in[u], 48 * ((e - u) // 2 + 1) if isinstance(e, int) else 24 * (e - u) + 48)
                    dve.tensor_copy(pick[:, u, :], pick32[:, u, :]).then_inc(pick_ready, 1)
                    dve.wait_ge(high_ready, 2 * e + 2)
                    dve.tensor_tensor(w1l[:, u, :, :], w1[:, :, :], w1h[:, u, :, :].bitcast(f32), ALU.subtract).then_inc(low_ready, 1)
                    dve.tensor_tensor(w2l[:, u, :, :], w2[:, :, :], w2h[:, u, :, :].bitcast(f32), ALU.subtract).then_inc(low_ready, 1)

                def weigh(i, t, u):
                    dve.wait_ge(wb_ready, i + 1)
                    for m in range(CB):
                        dve.wait_ge(down_summed, 2 * i + m + 1)
                        if not (isinstance(i, int) and i < 2):
                            dve.wait_ge(x_added, 2 * i + m - 3)
                        dve.scalar_tensor_tensor(y[:, t % 2, m, :], ps_d[:CP, m, :TB], b2[:, u, m:m + 1], wb[:, t % 2, :],
                                                 ALU.add, ALU.mult).then_inc(y_ready, 1)

                def body(e, u, first, last):
                    for t in range(NT):
                        i = e * NT + t
                        for f in range(FB):
                            dve.wait_ge(h32_ready, 4 * i + f + 1)
                            dve.tensor_tensor(hl[:, t % 2, f, :], h32[:, f % 2, :], hh[:, t % 2, f, :].bitcast(f32),
                                              ALU.subtract).then_inc(hl_ready, 1)
                        if not (first and t == 0):
                            weigh(i - 1, (t - 1) % NT, u if t else 1 - u)
                        if t == 3 and not last:
                            prepare(e + 1, 1 - u)
                    if last:
                        weigh(e * NT + NT - 1, NT - 1, u)

                prepare(0, 0)
                for_all_experts(dve, body)

            @block.gpsimd
            def _(pool):
                def body(e, u, first, last):
                    for t in range(NT):
                        for m in range(CB):
                            pool.wait_ge(y_ready, (e * NT + t) * 2 + m + 1)
                            x = x_sb[:, m, t * TB:(t + 1) * TB]
                            pool.tensor_tensor(x, x, y[:, t % 2, m, :], ALU.add).then_inc(x_added, 1)

                for_all_experts(pool, body)
                pool.wait_ge(x_added, 2 * NT * E)


def shared_expert(nc, xh, xl, w13_dram, b13_dram, w2_dram, b2_dram, x_sb, y_dram):
    with Scope(nc, "sh") as s:
        w13 = s.sb("w13", [CP, 2, CB, F])
        wh, wl = s.sb("wh", [CP, 2, CB, F], f32r), s.sb("wl", [CP, 2, CB, F], f32r)
        w2 = s.sb("w2", [128, FB, C])
        w2h, w2l = s.sb("w2h", [128, FB, C], f32r), s.sb("w2l", [128, FB, C], f32r)
        b13, b2 = s.sb("b13", [128, 2, FB]), s.sb("b2", [CP, CB])
        g = s.sb("g", [128, 2, TB])
        h32 = s.sb("h32", [128, 2, TB])
        hh, hl = s.sb("hh", [128, 2, FB, TB], f32r), s.sb("hl", [128, 2, FB, TB], f32r)
        y = s.sb("y", [CP, 2, CB, TB])
        ps_1, ps_3, ps_d = s.ps("ps_1", 2), s.ps("ps_3", 2), s.ps("ps_d", 2)
        loaded, high_ready, low_ready = s.sem("loaded"), s.sem("high_ready"), s.sem("low_ready")
        summed1, summed3, g_ready, h32_ready = (s.sem(n) for n in ("summed1", "summed3", "g_ready", "h32_ready"))
        hh_ready, hl_ready, down_summed, y_ready = (s.sem(n) for n in ("hh_ready", "hl_ready", "down_summed", "y_ready"))
        stored = [s.sem("even_stored"), s.sem("odd_stored")]
        with nc.Block() as block:
            @block.sync
            def _(sp):
                for dst, src in ((w13[:, :, :, :], w13_dram), (w2[:, :, :], w2_dram), (b13[:, :, :], b13_dram), (b2[:, :], b2_dram)):
                    sp.dma_start(dst, src).then_inc(loaded, 16)
                for t in range(NT):
                    sp.wait_ge(y_ready, 2 * t + 2)
                    sp.dma_start(y_dram[:, :, t * TB:(t + 1) * TB], y[:, t % 2, :, :]).then_inc(stored[t % 2], 16)
                for slot in range(2):
                    sp.wait_ge(stored[slot], 8 * NT)

            @block.tensor
            def _(pe):
                def down(t):
                    pe.wait_ge(hh_ready, 4 * t + 4)
                    pe.wait_ge(hl_ready, 4 * t + 4)
                    for m in range(CB):
                        if t >= 1:
                            pe.wait_ge(y_ready, 2 * t + m - 1)
                        cols = slice(m * CP, (m + 1) * CP)
                        product3(pe, ps_d[:CP, m, :TB], lambda k: w2h[:, k, cols], lambda k: w2l[:, k, cols],
                                 lambda k: hh[:, t % 2, k, :], lambda k: hl[:, t % 2, k, :], blocks=FB).then_inc(down_summed, 1)

                pe.wait_ge(low_ready, 2)
                for t in range(NT):
                    tok = slice(t * TB, (t + 1) * TB)
                    for f in range(FB):
                        i = 4 * t + f
                        rows = slice(f * 128, (f + 1) * 128)
                        if i >= 2:
                            pe.wait_ge(h32_ready, i - 1)
                        for a, ps, done in ((0, ps_1, summed1), (1, ps_3, summed3)):
                            product3(pe, ps[:, i % 2, :TB], lambda k: wh[:, a, k, rows], lambda k: wl[:, a, k, rows],
                                     lambda k: xh[:, k, tok], lambda k: xl[:, k, tok]).then_inc(done, 1)
                    if t >= 1:
                        down(t - 1)
                down(NT - 1)

            @block.scalar
            def _(act):
                act.wait_ge(loaded, 64)
                for i in range(4 * NT + 1):
                    if i < 4 * NT:
                        act.wait_ge(summed1, i + 1)
                        if i >= 2:
                            act.wait_ge(h32_ready, i - 1)
                        act.activation(g[:, i % 2, :], ps_1[:, i % 2, :TB], ACT.Gelu, bias=b13[:, 0, i % 4:i % 4 + 1]).then_inc(g_ready, 1)
                    if i >= 1:
                        j = i - 1
                        t, f = j // 4, j % 4
                        act.wait_ge(h32_ready, j + 1)
                        if f == 0 and t >= 2:
                            act.wait_ge(down_summed, 2 * t - 2)
                        act.activation(hh[:, t % 2, f, :], h32[:, j % 2, :], ACT.Copy).then_inc(hh_ready, 1)

            @block.vector
            def _(dve):
                dve.wait_ge(loaded, 64)
                dve.tensor_copy(wh[:, :, :, :], w13[:, :, :, :]).then_inc(high_ready, 1)
                dve.tensor_copy(w2h[:, :, :], w2[:, :, :]).then_inc(high_ready, 1)
                dve.wait_ge(high_ready, 2)
                dve.tensor_tensor(wl[:, :, :, :], w13[:, :, :, :], wh[:, :, :, :].bitcast(f32), ALU.subtract).then_inc(low_ready, 1)
                dve.tensor_tensor(w2l[:, :, :], w2[:, :, :], w2h[:, :, :].bitcast(f32), ALU.subtract).then_inc(low_ready, 1)

                def finish(t):
                    for m in range(CB):
                        dve.wait_ge(down_summed, 2 * t + m + 1)
                        if m == 0 and t >= 2:
                            dve.wait_ge(stored[t % 2], 16 * (t // 2))
                        dve.scalar_tensor_tensor(y[:, t % 2, m, :], ps_d[:CP, m, :TB], b2[:, m:m + 1], x_sb[:, m, t * TB:(t + 1) * TB],
                                                 ALU.add, ALU.add).then_inc(y_ready, 1)

                for i in range(4 * NT + 1):
                    if i < 4 * NT:
                        dve.wait_ge(summed3, i + 1)
                        dve.wait_ge(g_ready, i + 1)
                        if i >= 2:
                            dve.wait_ge(hh_ready, i - 1)
                            dve.wait_ge(hl_ready, i - 1)
                        dve.scalar_tensor_tensor(h32[:, i % 2, :], ps_3[:, i % 2, :TB], b13[:, 1, i % 4:i % 4 + 1], g[:, i % 2, :],
                                                 ALU.add, ALU.mult).then_inc(h32_ready, 1)
                    if i >= 1:
                        j = i - 1
                        t, f = j // 4, j % 4
                        dve.wait_ge(hh_ready, j + 1)
                        dve.tensor_tensor(hl[:, t % 2, f, :], h32[:, j % 2, :], hh[:, t % 2, f, :].bitcast(f32),
                                          ALU.subtract).then_inc(hl_ready, 1)
                        if f == 3 and t >= 1:
                            finish(t - 1)
                finish(NT - 1)


def experts_layer(nc, ins, x_in, y_out):
    with Scope(nc, "l2") as s:
        x_sb = s.sb("x", [CP, CB, N])
        xh, xl = s.sb("xh", [CP, CB, N], f32r), s.sb("xl", [CP, CB, N], f32r)
        w_rows = s.sb("w_rows", [2 * E, N], f32r)
        load_x(nc, "l2ld", x_in, x_sb)
        norm(nc, "l2n", x_sb, ins["group_avg"], xh, xl)
        route(nc, xh, xl, ins["gate"], ins["first"], ins["ident98"], w_rows)
        experts(nc, xh, xl, w_rows, ins["fc1"], ins["fc1_b"], ins["fc2"], ins["fc2_b"], ins["pick"], x_sb)
        shared_expert(nc, xh, xl, ins["w13"], ins["b13"], ins["w2"], ins["w2_b"], x_sb, y_out)


def build(nc, ins, out, stop_after=99, only=None):
    scratch = {n: nc.dram_tensor(n, sh, f32, kind="Internal").ap() for n, sh in
               (("x1", [CP, CB, N]), ("x2", [CP, CB, N]), ("x3", [CP, CB, N]), ("products", [HEADS, 32, N]), ("sums", [HEADS, N]))}
    if only in (None, 0):
        gru_layer(nc, ins, ins["x"], scratch["x1"] if stop_after > 0 else out)
    if stop_after >= 1 and only in (None, 1):
        attention_layer(nc, "l1", ins, ins["x"] if only else scratch["x1"], scratch["x2"] if stop_after > 1 else out, scratch)
    if stop_after >= 2 and only in (None, 2):
        experts_layer(nc, ins, ins["x"] if only else scratch["x2"], scratch["x3"] if stop_after > 2 else out)
    if stop_after >= 3 and only in (None, 3):
        attention_layer(nc, "l3", ins, ins["x"] if only else scratch["x3"], out, scratch)


def selectors():
    k = np.arange(T)
    sel = np.zeros((128, T), np.float32)
    for row in (32, 96):
        sel[row:row + H] = (k // W)[None] == np.arange(H)[:, None]
        sel[row + H:row + H + W] = (k % W)[None] == np.arange(W)[:, None]
    sel[64:66] = -1.0
    signs = np.repeat(np.array([[-1, 0], [1, 1], [-HD ** -0.5, 0], [HD ** -0.5, HD ** -0.5]], np.float32), 16, 0)
    return sel, np.tile(signs, (2, 1))


def lay_out_attention(tag, wqkv, bqkv, wo, bo, rel_h, rel_w):
    o = {}
    rows = wqkv.reshape(C, 3, PAIRS, 2, HD)
    cols = [rows[:, part, :, head] for head in range(2) for part in (0, 0, 1, 1)]
    o["_wqk"] = np.ascontiguousarray(np.stack(cols, 2).reshape(CB, CP, PAIRS, 128).transpose(2, 1, 0, 3))
    b = bqkv.reshape(3, PAIRS, 2, HD)
    o["_bqk"] = np.ascontiguousarray(np.stack([b[part, :, head] for head in range(2) for part in (0, 0, 1, 1)], 1).reshape(PAIRS, 128, 1))
    o["_wv"] = np.ascontiguousarray(wqkv[:, 2 * C:].reshape(CB, CP, C).transpose(1, 0, 2))
    o["_bv"] = np.ascontiguousarray(np.broadcast_to(bqkv[2 * C:], (TH, C)))
    r = np.zeros((2, 4, HD, H + W, 2, H), np.float32)
    for n in range(H):
        for a, table in ((0, rel_h), (H, rel_w)):
            seen = table[n:n + H][::-1].T
            for head in range(2):
                r[head, 0:2, :, a + n, head, :] = seen
    o["_rel"] = r.reshape(128, H + W, 2 * H)
    w = wo.reshape(PAIRS // 2, 2, 2, 1, HD, C)
    o["_wo"] = np.ascontiguousarray(np.broadcast_to(w, (3, 2, 2, 2, HD, C)).reshape(3, 128, CB, CP).transpose(1, 0, 2, 3))
    o["_bo"] = np.ascontiguousarray(bo.reshape(CB, CP).T)
    return {tag + k: v for k, v in o.items()}


def channels(a):
    a = np.asarray(a)
    return np.ascontiguousarray(np.moveaxis(a.reshape(*a.shape[:-1], CB, CP), (-1, -2), (0, 1)))


def twice(a):
    return np.stack([a[..., :128], np.concatenate([a[..., 128:], a[..., 128:]], -1)], -2)


def lay_out(i):
    a = {k: np.asarray(v) for k, v in i.items()}
    o = {}
    o["x"] = channels(a["x"].reshape(N, C))
    o["group_avg"] = np.kron(np.eye(CP // GC), np.full((GC, GC), 1.0 / GC)).astype(np.float32)
    o["ident128"] = np.eye(128, dtype=np.float32)
    o["wx"] = channels(twice(a["L0_conv_Wx"].reshape(3, C, C).transpose(2, 0, 1)).reshape(C, 6, 128).transpose(1, 2, 0))
    o["bx"] = np.ascontiguousarray(twice(a["L0_conv_bx"].reshape(3, C)).reshape(6, 128).T)
    o["bh"] = np.ascontiguousarray(twice(a["L0_conv_bh"].reshape(3, C)).reshape(6, 128).T)
    o["bhn"] = np.ascontiguousarray(twice(a["L0_conv_bh"][2 * C:]).T)
    wh = twice(a["L0_conv_Wh"].reshape(3, C, C).transpose(2, 0, 1))
    o["wh"] = np.ascontiguousarray(np.moveaxis(twice(np.moveaxis(wh, 0, -1)), (-1, -2), (0, 1)))
    o["wp"] = np.ascontiguousarray(a["L0_conv_Wp"].T.reshape(C, CB, CP))
    o["sel"], o["signs"] = selectors()
    o["ident98"] = np.eye(TH, dtype=np.float32)
    o.update(lay_out_attention("l1", a["L1_conv_qkv_w"], a["L1_conv_qkv_b"], a["L1_conv_proj_w"], a["L1_conv_proj_b"],
                               a["L1_conv_rel_pos_h"], a["L1_conv_rel_pos_w"]))
    o.update(lay_out_attention("l3", a["L3_conv_qkv_w"].T, a["L3_conv_qkv_b"], a["L3_conv_proj_w"].T, a["L3_conv_proj_b"],
                               a["L3_conv_rel_pos_h"], a["L3_conv_rel_pos_w"]))
    o["gate"] = channels(a["L2_conv_gate_w"])
    o["first"] = np.ascontiguousarray(np.broadcast_to(np.arange(E, 0, -1, dtype=np.float32), (TH, E)))
    o["fc1"] = np.ascontiguousarray(a["L2_conv_fc1_w"].reshape(E, F, CB, CP).transpose(0, 3, 2, 1))
    o["fc1_b"] = np.ascontiguousarray(a["L2_conv_fc1_b"].reshape(E, FB, 128).transpose(0, 2, 1))
    o["fc2"] = np.ascontiguousarray(a["L2_conv_fc2_w"].reshape(E, C, FB, 128).transpose(0, 3, 2, 1))
    o["fc2_b"] = np.ascontiguousarray(a["L2_conv_fc2_b"].reshape(E, CB, CP).transpose(0, 2, 1))
    o["pick"] = np.ascontiguousarray(np.broadcast_to(np.tile(np.eye(E, dtype=np.float32), (1, 2))[:, :, None], (E, 2 * E, CP)))
    o["w13"] = np.ascontiguousarray(np.stack([a["L2_conv_w1_w"], a["L2_conv_w3_w"]]).reshape(2, F, CB, CP).transpose(3, 0, 2, 1))
    o["b13"] = np.ascontiguousarray(np.stack([a["L2_conv_w1_b"], a["L2_conv_w3_b"]]).reshape(2, FB, 128).transpose(2, 0, 1))
    o["w2"] = np.ascontiguousarray(a["L2_conv_w2_w"].reshape(C, FB, 128).transpose(2, 1, 0))
    o["w2_b"] = np.ascontiguousarray(a["L2_conv_w2_b"].reshape(CB, CP).T)
    return o


def back(y):
    return np.ascontiguousarray(y.transpose(2, 1, 0).reshape(B, H, W, C))


_BUILT_OUT = "out_0_dram"


def kernel(**inputs):
    import concourse.bacc as _bacc
    from concourse.bass_utils import run_bass_kernel_spmd as _run

    nc = _bacc.Bacc("TRN2", target_bir_lowering=False, num_devices=1)
    arrays = {f"in_{k}_dram": v for k, v in lay_out(inputs).items()}
    ins = {k[3:-5]: nc.dram_tensor(k, v.shape, mybir.dt.from_np(v.dtype), kind="ExternalInput").ap() for k, v in arrays.items()}
    out = nc.dram_tensor(_BUILT_OUT, [CP, CB, N], f32, kind="ExternalOutput").ap()
    build(nc, ins, out)
    r = _run(nc, [arrays], core_ids=[0])
    return back(r.results[0][_BUILT_OUT])
```

```python
import numpy as np
import concourse.bass as bass
from concourse import mybir
from contextlib import ExitStack

f32, f32r = mybir.dt.float32, mybir.dt.float32r
bf16, fp16 = mybir.dt.bfloat16, mybir.dt.float16
ALU = mybir.AluOpType
ACT = mybir.ActivationFunctionType
AXIS = mybir.AxisListType

B, H, W, C = 16, 14, 14, 192
T = H * W
N = B * T
CP, CB = 96, 2
HEADS, HD = 12, 16
PAIRS = HEADS // 2
G, GC = 32, C // 32
E, F = 8, 512
FB = F // 128
TB = 2 * T
NT = N // TB
TH = T // 2
HSCALE = 2048.0
EPS = 1e-5
NEG = -3.0e38


class Scope:

    def __init__(self, nc, tag):
        self.nc, self.tag, self.stack, self.sems = nc, tag, ExitStack(), []

    def __enter__(self):
        self.stack.__enter__()
        return self

    def __exit__(self, *e):
        if self.sems:
            self.nc.clear_and_free_semaphores(self.sems)
            self.nc.all_engine_barrier()
        return self.stack.__exit__(*e)

    def sb(self, name, shape, dt=f32):
        return self.stack.enter_context(self.nc.sbuf_tensor(f"{self.tag}_{name}", shape, dt))

    def ps(self, name, banks=1):
        return self.stack.enter_context(self.nc.psum_tensor(f"{self.tag}_{name}", [128, banks, 512], f32))

    def sem(self, name):
        self.sems.append(self.nc.alloc_semaphore(f"{self.tag}_{name}"))
        return self.sems[-1]


class GroupNorm:
    CHUNK = 4

    def __init__(self, s, x, xh, xl, one_row=False, place=None):
        self.x, self.xh, self.xl, self.one_row = x, xh, xl, one_row
        shapes = dict(stats=[CP, CB, B, 6], mv=[CP, CB, B, 2], dev=[CP, CB, B], spread=[CP, CB, B], mean_g=[CP, CB, B],
                      std=[CP, CB, B], rstd=[CP, CB, B], shift=[CP, CB, B], avg=[CP, CP], eps=[CP, 1], xn=[CP, CB, 2, T])
        if place is None:
            bufs = {n: s.sb(n, shape) for n, shape in shapes.items()}
        else:
            bufs, at = {}, 0
            for n, shape in shapes.items():
                size = int(np.prod(shape[1:]))
                dims = {f"d{k}": d for k, d in enumerate(shape[1:])}
                names = " ".join(dims)
                bufs[n] = place[:, at:at + size].rearrange(f"p ({names}) -> p {names}", **dims)
                at += size
        self.stats, self.mv, self.dev, self.spread, self.mean_g = (bufs[n] for n in ("stats", "mv", "dev", "spread", "mean_g"))
        self.std, self.rstd, self.shift, self.avg, self.eps, self.xn = (bufs[n] for n in ("std", "rstd", "shift", "avg", "eps", "xn"))
        self.x_in, self.avg_in, self.chan, self.chan2, self.mean_ready, self.var_ready = (
            s.sem(n) for n in ("x_in", "avg_in", "chan", "chan2", "mean_ready", "var_ready"))
        self.mean_copied, self.dev_ready, self.dev2, self.spread_ready, self.std_ready, self.rstd_ready = (
            s.sem(n) for n in ("mean_copied", "dev_ready", "dev2", "spread_ready", "std_ready", "rstd_ready"))
        self.shift_ready, self.xn_ready, self.xh_ready, self.eps_ready, self.row_ready = (
            s.sem(n) for n in ("shift_ready", "xn_ready", "xh_ready", "eps_ready", "row_ready"))
        self.low_ready = [s.sem("low0_ready"), s.sem("low1_ready")]
        self.x_chunk = [s.sem(f"x_chunk{n}") for n in range(B // self.CHUNK)]

    def await_images(self, eng, count):
        for k in range(CB):
            eng.wait_ge(self.low_ready[k], count)

    def load(self, sp, x_dram, group_avg):
        sp.dma_start(self.avg[:, :], group_avg).then_inc(self.avg_in, 16)
        for n, loaded in enumerate(self.x_chunk):
            cols = slice(n * self.CHUNK * T, (n + 1) * self.CHUNK * T)
            for k in range(CB):
                sp.dma_start(self.x(k, cols), x_dram[:, k, cols]).then_inc(loaded, 16)

    def statistics(self, dve, mean_sums):
        dve.memset(self.eps[:, :], EPS).then_inc(self.eps_ready, 1)
        for b in range(B):
            if b % self.CHUNK == 0:
                dve.wait_ge(self.x_chunk[b // self.CHUNK], 16 * CB)
            for k in range(CB):
                dve.bn_stats(self.stats[:, k, b, :], self.x(k, slice(b * T, (b + 1) * T))).then_inc(self.chan, 1)
        dve.wait_ge(self.chan, CB * B)
        for k in range(CB):
            for b in range(B):
                dve.bn_aggr(self.mv[:, k, b, :], self.stats[:, k, b, :]).then_inc(self.chan2, 1)
        dve.wait_ge(self.mean_ready, 1)
        dve.tensor_copy(self.mean_g[:, :, :].rearrange("p k b -> p (k b)"), mean_sums).then_inc(self.mean_copied, 1)
        dve.wait_ge(self.mean_copied, 1)
        dve.tensor_tensor(self.dev[:, :, :], self.mv[:, :, :, 0], self.mean_g[:, :, :], ALU.subtract).then_inc(self.dev_ready, 1)
        dve.wait_ge(self.dev_ready, 1)
        dve.tensor_tensor(self.spread[:, :, :], self.dev[:, :, :], self.dev[:, :, :], ALU.mult).then_inc(self.dev2, 1)
        dve.wait_ge(self.dev2, 1)
        dve.tensor_tensor(self.spread[:, :, :], self.spread[:, :, :], self.mv[:, :, :, 1], ALU.add).then_inc(self.spread_ready, 1)

    def normalize(self, dve):
        dve.wait_ge(self.std_ready, 1)
        dve.reciprocal(self.rstd[:, :, :], self.std[:, :, :]).then_inc(self.rstd_ready, 1)
        dve.wait_ge(self.rstd_ready, 1)
        dve.scalar_tensor_tensor(self.shift[:, :, :].rearrange("p k b -> p (k b)"), self.mean_g[:, :, :].rearrange("p k b -> p (k b)"), -1.0,
                                 self.rstd[:, :, :].rearrange("p k b -> p (k b)"), ALU.mult, ALU.mult).then_inc(self.shift_ready, 1)
        dve.wait_ge(self.shift_ready, 1)
        for b in range(B + 1):
            if b < B:
                if b >= 2:
                    self.await_images(dve, b - 1)
                for k in (1, 0):
                    dve.tensor_scalar(self.xn[:, k, b % 2, :], self.x(k, slice(b * T, (b + 1) * T)), self.rstd[:, k, b:b + 1],
                                      self.shift[:, k, b:b + 1], ALU.mult, ALU.add).then_inc(self.xn_ready, 1)
            if b >= 1:
                self.low(dve, b - 1, 0)

    def low(self, eng, b, k):
        cols = slice(b * T, (b + 1) * T)
        eng.wait_ge(self.xh_ready, CB * b + CB)
        eng.wait_ge(self.xn_ready, CB * b + CB)
        eng.tensor_tensor(self.xl[:CP, k, cols], self.xn[:, k, b % 2, :], self.xh[:CP, k, cols].bitcast(f32),
                          ALU.subtract).then_inc(self.low_ready[k], 1)

    def gpsimd(self, pool):
        if self.one_row:
            pool.memset(self.xh[CP:CP + 1, :, :].bitcast(f32), 1.0).then_inc(self.row_ready, 1)
            pool.wait_ge(self.row_ready, 1)
            pool.memset(self.xl[CP:CP + 1, :, :].bitcast(f32), 0.0).then_inc(self.row_ready, 1)
            pool.wait_ge(self.row_ready, 2)
        for b in range(B):
            self.low(pool, b, 1)

    def tensor(self, pe, mean_sums, var_sums):
        pe.wait_ge(self.avg_in, 16)
        pe.wait_ge(self.chan2, CB * B)
        pe.matmul(mean_sums, self.avg[:, :], self.mv[:, :, :, 0], start=True, stop=True).then_inc(self.mean_ready, 1)
        pe.wait_ge(self.spread_ready, 1)
        pe.matmul(var_sums, self.avg[:, :], self.spread[:, :, :], start=True, stop=True).then_inc(self.var_ready, 1)

    def scalar(self, act, var_sums):
        act.wait_ge(self.eps_ready, 1)
        act.wait_ge(self.var_ready, 1)
        act.activation(self.std[:, :, :].rearrange("p k b -> p (k b)"), var_sums, ACT.Sqrt, bias=self.eps[:, :]).then_inc(self.std_ready, 1)
        act.wait_ge(self.shift_ready, 1)
        for b in range(B):
            for k in range(CB):
                cols = slice(b * T, (b + 1) * T)
                act.activation(self.xh[:CP, k, cols], self.x(k, cols), ACT.Identity, scale=self.rstd[:, k, b:b + 1],
                               bias=self.shift[:, k, b:b + 1]).then_inc(self.xh_ready, 1)


def split(eng, whole, high, low, high_ready, low_ready, count):
    eng.tensor_copy(high, whole).then_inc(high_ready, 1)
    eng.wait_ge(high_ready, count + 1)
    eng.tensor_tensor(low, whole, high.bitcast(f32), ALU.subtract).then_inc(low_ready, 1)


def product3(pe, out, wh, wl, xh, xl, start=True, stop=True, blocks=CB):
    terms = [(w, x, k) for k in range(blocks) for w, x in ((wh, xh), (wl, xh), (wh, xl))]
    for n, (w, x, k) in enumerate(terms):
        last = pe.matmul(out, w(k), x(k), start=start and n == 0, stop=stop and n == len(terms) - 1)
    return last


def gru_inputs(nc, x_in, group_avg, x_sb, xh, xl, wx_dram, bx_dram, bh_dram, gates_in, cand_in, ahead):
    with Scope(nc, "gi") as s:
        w = s.sb("w", [CP, CB, 6, 128])
        wh = s.sb("wh", [CP, CB, 6, 128], f32r)
        wl = s.sb("wl", [CP, CB, 6, 128], f32r)
        bx, bh, bias, bias_s = s.sb("bx", [128, 6]), s.sb("bh", [128, 6]), s.sb("bias", [128, 6]), s.sb("bias_s", [128, 6])
        whole = s.sb("whole", [128, 2, TB])
        rest = s.sb("rest", [128, 2, TB])
        ps = s.ps("ps", 4)
        mean_sums, var_sums = (s.ps(n)[:CP, 0, :CB * B] for n in ("mean_sums", "var_sums"))
        norm = GroupNorm(s, lambda k, cols: x_sb[:, k, cols], xh, xl)
        ahead_in = s.sem("ahead_in")
        loaded, wh_ready, wl_ready = s.sem("loaded"), s.sem("wh_ready"), s.sem("wl_ready")
        bias_ready, biass_ready = s.sem("bias_ready"), s.sem("biass_ready")
        summed, moved = s.sem("summed"), s.sem("moved")
        p0, r1, p1, p2 = s.sem("p0"), s.sem("r1"), s.sem("p1"), s.sem("p2")

        def view(x):
            return x.rearrange("p (b t) -> p t b", b=2)

        with nc.Block() as block:
            @block.sync
            def _(sp):
                norm.load(sp, x_in, group_avg)
                sp.dma_start(w[:, :, :, :], wx_dram).then_inc(loaded, 16)
                sp.dma_start(bx[:, :], bx_dram).then_inc(loaded, 16)
                sp.dma_start(bh[:, :], bh_dram).then_inc(loaded, 16)
                for dst, src in ahead:
                    sp.dma_start(dst, src).then_inc(ahead_in, 16)
                sp.wait_ge(ahead_in, 16 * len(ahead))

            @block.gpsimd
            def _(pool):
                norm.gpsimd(pool)
                for n in range(NT):
                    for j in range(4):
                        g = n * 4 + j
                        dst = [gates_in[:, :, p, j, 2 * n:2 * n + 2] for p in range(3)]
                        pool.wait_ge(p1, g + 1)
                        pool.tensor_tensor(dst[2], view(rest[:, g % 2, :]), dst[1], ALU.subtract).then_inc(p2, 1)

            @block.tensor
            def _(pe):
                norm.tensor(pe, mean_sums, var_sums)
                pe.wait_ge(wl_ready, 1)
                for n in range(NT):
                    norm.await_images(pe, 2 * n + 2)
                    for j in range(6):
                        i = n * 6 + j
                        if i >= 4:
                            pe.wait_ge(moved, i - 3)
                        product3(pe, ps[:, i % 4, :TB], lambda k: wh[:, k, j, :], lambda k: wl[:, k, j, :],
                                 lambda k: xh[:, k, n * TB:(n + 1) * TB],
                                 lambda k: xl[:, k, n * TB:(n + 1) * TB]).then_inc(summed, 1)

            @block.scalar
            def _(act):
                norm.scalar(act, var_sums)
                act.wait_ge(biass_ready, 1)
                for n in range(NT):
                    for j in range(6):
                        i, g = n * 6 + j, n * 4 + j
                        act.wait_ge(summed, i + 1)
                        if j < 4:
                            if g >= 2:
                                act.wait_ge(p2, g - 1)
                            act.activation(whole[:, g % 2, :], ps[:, i % 4, :TB], ACT.Identity, scale=HSCALE,
                                           bias=bias_s[:, j:j + 1]).then_inc(moved, 1)
                        else:
                            act.activation(cand_in[:, :, j - 4, 2 * n:2 * n + 2], view(ps[:, i % 4, :TB]), ACT.Identity,
                                           bias=bias[:, j:j + 1]).then_inc(moved, 1)
                act.wait_ge(moved, 6 * NT)

            @block.vector
            def _(dve):
                norm.statistics(dve, mean_sums)
                dve.wait_ge(loaded, 48)
                split(dve, w[:, :, :, :], wh[:, :, :, :], wl[:, :, :, :], wh_ready, wl_ready, 0)
                dve.tensor_tensor(bias[:, 0:4], bx[:, 0:4], bh[:, 0:4], ALU.add).then_inc(bias_ready, 1)
                dve.tensor_copy(bias[:, 4:6], bx[:, 4:6]).then_inc(bias_ready, 1)
                dve.wait_ge(bias_ready, 2)
                dve.tensor_scalar(bias_s[:, :], bias[:, :], HSCALE, None, ALU.mult).then_inc(biass_ready, 1)
                norm.normalize(dve)
                for n in range(NT):
                    for j in range(4):
                        g = n * 4 + j
                        dst = [gates_in[:, :, p, j, 2 * n:2 * n + 2] for p in range(3)]
                        dve.wait_ge(moved, n * 6 + j + 1)
                        dve.tensor_copy(dst[0], view(whole[:, g % 2, :])).then_inc(p0, 1)
                        dve.wait_ge(p0, g + 1)
                        if g >= 2:
                            dve.wait_ge(p2, g - 1)
                        dve.tensor_tensor(view(rest[:, g % 2, :]), view(whole[:, g % 2, :]), dst[0], ALU.subtract).then_inc(r1, 1)
                        dve.wait_ge(r1, g + 1)
                        dve.tensor_copy(dst[1], view(rest[:, g % 2, :])).then_inc(p1, 1)
                dve.wait_ge(p2, NT * 4)


def gru(nc, gates_in, cand_in, state, w, bhn, ident32):
    STEPS = 14
    with Scope(nc, "gru") as s:
        ws = s.sb("ws", [128, CB, 3, 2, 128])
        wp = s.sb("wp", [128, 4, 3, 2, 128], fp16)
        most, least = s.sb("most", [128, 1]), s.sb("least", [128, 1])
        most_all, ones = s.sb("most_all", [1, 1]), s.sb("ones", [1, 128])
        largest, scale, unscale = s.sb("largest", [128, 1]), s.sb("scale", [128, 1]), s.sb("unscale", [128, 1])
        fits, factor = s.sb("fits", [128, 1]), s.sb("factor", [128, 1])
        ident, bhs = s.sb("ident", [128, 128], bf16), s.sb("bhs", [128, 2, B])
        bp, br = s.sb("bp", [128, 3, 2, B], bf16), s.sb("br", [128, 2, B])
        hp = s.sb("hp", [128, 2, 4, 2 * B], fp16)
        KEPT_HIGH, KEPT_LOW, NEW_HIGH, NEW_LOW = range(4)
        names = "tr tz zc rn cand n kept new half".split()
        tr, tz, zc, rn, cand, tn, kept, new, half = (s.sb(n, [128, 2, 2 * B]) for n in names)
        ps_r, ps_n, ps_z = s.ps("ps_r", 2), s.ps("ps_n", 2), s.ps("ps_z", 2)
        prep, weights_ready = s.sem("prep"), s.sem("weights_ready")
        most_ready, most_turned, all_ready, spread, scale_ready = (
            s.sem(n) for n in ("most_ready", "most_turned", "all_ready", "spread", "scale_ready"))
        kept_high, kept_low, new_high, new_low = (s.sem(n) for n in ("kept_high", "kept_low", "new_high", "new_low"))
        h_ready, half_ready = s.sem("h_ready"), s.sem("half_ready")
        r_summed, n_summed, z_summed = s.sem("r_summed"), s.sem("n_summed"), s.sem("z_summed")
        tr_ready, tz_ready, tn_ready = s.sem("tr_ready"), s.sem("tz_ready"), s.sem("tn_ready")
        zc_ready, rn_ready, cand_ready = s.sem("zc_ready"), s.sem("rn_ready"), s.sem("cand_ready")
        kept_ready, new_ready = s.sem("kept_ready"), s.sem("new_ready")

        def two(x):
            return x.rearrange("p (k b) -> p k b", k=2)

        with nc.Block() as block:
            @block.vector
            def _(dve):
                step = [0]

                def link(ins):
                    step[0] += 1
                    ins.then_inc(prep, 1)
                    dve.wait_ge(prep, step[0])

                dve.memset(state[:, 0, :, :], 0.0).then_inc(h_ready, 1)
                dve.memset(half[:, 0, :], 0.0).then_inc(half_ready, 1)
                for part, ready in ((KEPT_HIGH, kept_high), (KEPT_LOW, kept_low), (NEW_HIGH, new_high), (NEW_LOW, new_low)):
                    dve.memset(hp[:, 0, part, :], 0.0).then_inc(ready, 1)
                def whole(x):
                    return x.rearrange("p c g m n -> p (c g m n)")

                link(dve.memset(ones[:, :], 1.0))
                link(dve.tensor_reduce(most[:, :], whole(w[:, :, :, :, :]), AXIS.X, ALU.max))
                link(dve.tensor_reduce(least[:, :], whole(w[:, :, :, :, :]), AXIS.X, ALU.min))
                link(dve.tensor_scalar(least[:, :], least[:, :], -1.0, None, ALU.mult))
                dve.tensor_tensor(most[:, :], most[:, :], least[:, :], ALU.max).then_inc(most_ready, 1)
                dve.wait_ge(most_turned, 1)
                dve.tensor_reduce(most_all[:, :], ps_r[0:1, 0, :128], AXIS.X, ALU.max).then_inc(all_ready, 1)
                dve.wait_ge(spread, 1)
                link(dve.tensor_copy(largest[:, :], ps_n[:, 0, 0:1]))
                link(dve.memset(scale[:, :], 2.0 ** -100))
                link(dve.tensor_scalar(largest[:, :], largest[:, :], 2.0 ** -100, None, ALU.mult))
                for k in (64, 32, 16, 8, 4, 2, 1):
                    link(dve.tensor_scalar(fits[:, :], largest[:, :], 2.0 ** k, 2.0 ** 14, ALU.mult, ALU.is_le))
                    link(dve.tensor_scalar(factor[:, :], fits[:, :], 2.0 ** k - 1, 1.0, ALU.mult, ALU.add))
                    dve.tensor_tensor(scale[:, :], scale[:, :], factor[:, :], ALU.mult).then_inc(scale_ready, 1)
                    link(dve.tensor_tensor(largest[:, :], largest[:, :], factor[:, :], ALU.mult))
                dve.wait_ge(scale_ready, 7)
                link(dve.reciprocal(unscale[:, :], scale[:, :]))
                link(dve.tensor_scalar(unscale[:, :], unscale[:, :], 0.5 / HSCALE, None, ALU.mult))
                link(dve.tensor_scalar(ws[:, :, :, :, :], w[:, :, :, :, :], scale[:, 0:1], None, ALU.mult))
                link(dve.tensor_copy(wp[:, 0], ws[:, 0]))
                link(dve.tensor_tensor(wp[:, 1], ws[:, 0], wp[:, 0], ALU.subtract))
                link(dve.tensor_copy(wp[:, 2], ws[:, 1]))
                link(dve.tensor_tensor(wp[:, 3], ws[:, 1], wp[:, 2], ALU.subtract))
                link(dve.tensor_copy(wp[64:128, 2], wp[64:128, 3]))
                for k in range(2):
                    link(dve.memset(bhs[:, k, :], HSCALE))
                    link(dve.tensor_scalar(bhs[:, k, :], bhs[:, k, :], bhn[:, k:k + 1], None, ALU.mult))
                link(dve.tensor_copy(bp[:, 0], bhs[:, :, :]))
                link(dve.tensor_tensor(br[:, :, :], bhs[:, :, :], bp[:, 0], ALU.subtract))
                link(dve.tensor_copy(bp[:, 1], br[:, :, :]))
                link(dve.tensor_tensor(bp[:, 2], br[:, :, :], bp[:, 1], ALU.subtract))
                dve.tensor_scalar(ident[:, :], ident32[:, :], scale[:, 0:1], None, ALU.mult).then_inc(weights_ready, 1)
                with dve.Fori(0, T // STEPS) as it:
                    for u in range(STEPS):
                        t, b = it * STEPS + u, u % 2
                        dve.wait_ge(tr_ready, t + 1)
                        dve.wait_ge(n_summed, t + 1)
                        dve.scalar_tensor_tensor(rn[:, b, :], tr[:, b, :], 1.0, ps_n[:, b, :2 * B], ALU.add, ALU.mult).then_inc(rn_ready, 1)
                        dve.wait_ge(rn_ready, t + 1)
                        dve.scalar_tensor_tensor(two(cand[:, b, :]), two(rn[:, b, :]), unscale[:, 0:1], cand_in[:, t, :, :],
                                                 ALU.mult, ALU.add).then_inc(cand_ready, 1)
                        dve.wait_ge(tz_ready, t + 1)
                        dve.wait_ge(half_ready, t + 1)
                        dve.scalar_tensor_tensor(hp[:, 1 - b, KEPT_HIGH, :], tz[:, b, :], 1.0, half[:, b, :], ALU.add, ALU.mult).then_inc(kept_high, 1)
                        dve.scalar_tensor_tensor(kept[:, b, :], tz[:, b, :], 1.0, half[:, b, :], ALU.add, ALU.mult).then_inc(kept_ready, 1)
                        dve.tensor_scalar(zc[:, b, :], tz[:, b, :], -0.5 * HSCALE, 0.5 * HSCALE, ALU.mult, ALU.add).then_inc(zc_ready, 1)
                        dve.wait_ge(zc_ready, t + 1)
                        dve.wait_ge(tn_ready, t + 1)
                        dve.tensor_tensor(hp[:, 1 - b, NEW_HIGH, :], zc[:, b, :], tn[:, b, :], ALU.mult).then_inc(new_high, 1)
                        dve.tensor_tensor(new[:, b, :], zc[:, b, :], tn[:, b, :], ALU.mult).then_inc(new_ready, 1)
                        dve.wait_ge(kept_high, t + 2)
                        dve.wait_ge(kept_ready, t + 1)
                        dve.tensor_tensor(hp[:, 1 - b, KEPT_LOW, :], kept[:, b, :], hp[:, 1 - b, KEPT_HIGH, :], ALU.subtract).then_inc(kept_low, 1)
                        dve.wait_ge(new_high, t + 2)
                        dve.wait_ge(new_ready, t + 1)
                        dve.tensor_tensor(hp[:, 1 - b, NEW_LOW, :], new[:, b, :], hp[:, 1 - b, NEW_HIGH, :], ALU.subtract).then_inc(new_low, 1)
                        dve.tensor_tensor(state[:, t + 1, :, :], two(new[:, b, :]), two(kept[:, b, :]), ALU.add).then_inc(h_ready, 1)
                        dve.wait_ge(h_ready, t + 2)
                        dve.tensor_scalar(two(half[:, 1 - b, :]), state[:, t + 1, :, :], 0.5, None, ALU.mult).then_inc(half_ready, 1)

            @block.tensor
            def _(pe):
                HIGH = [(0, 0), (1, 0), (2, 1)]
                LOW = [(0, 0), (2, 1)]

                def gate(out, g, b, part):
                    for m in range(2):
                        for wi, k in HIGH if part in (KEPT_HIGH, NEW_HIGH) else LOW:
                            last = pe.matmul(out[:, b, B * m:B * m + B], wp[:, wi, g, m, :], hp[:, b, part, B * k:B * k + B],
                                             start=False, stop=True, skip_group_check=True)
                    return last

                pe.wait_ge(most_ready, 1)
                pe.matmul(ps_r[0:1, 0, :128], most[:, :], ident32[:, :], start=True, stop=True).then_inc(most_turned, 1)
                pe.wait_ge(all_ready, 1)
                pe.matmul(ps_n[:, 0, 0:1], ones[:, :], most_all[:, :], start=True, stop=True).then_inc(spread, 1)
                pe.wait_ge(weights_ready, 1)
                with pe.Fori(0, T // STEPS) as it:
                    for u in range(STEPS):
                        t, b = it * STEPS + u, u % 2
                        for p in range(3):
                            pe.matmul(ps_r[:, b, :2 * B], ident[:, :], gates_in[:, t, p, 2:4, :], start=p == 0, stop=p == 2, skip_group_check=True)
                            pe.matmul(ps_n[:, b, :2 * B], ident[:, :], bp[:, p, :, :], start=p == 0, stop=p == 2, skip_group_check=True)
                            pe.matmul(ps_z[:, b, :2 * B], ident[:, :], gates_in[:, t, p, 0:2, :], start=p == 0, stop=p == 2, skip_group_check=True)
                        pe.wait_ge(kept_high, t + 1)
                        gate(ps_r, 1, b, KEPT_HIGH)
                        gate(ps_n, 2, b, KEPT_HIGH)
                        gate(ps_z, 0, b, KEPT_HIGH)
                        pe.wait_ge(new_high, t + 1)
                        gate(ps_r, 1, b, NEW_HIGH)
                        gate(ps_n, 2, b, NEW_HIGH)
                        pe.wait_ge(kept_low, t + 1)
                        gate(ps_r, 1, b, KEPT_LOW)
                        pe.wait_ge(new_low, t + 1)
                        gate(ps_r, 1, b, NEW_LOW).then_inc(r_summed, 1)
                        gate(ps_n, 2, b, KEPT_LOW)
                        gate(ps_n, 2, b, NEW_LOW).then_inc(n_summed, 1)
                        gate(ps_z, 0, b, NEW_HIGH)
                        gate(ps_z, 0, b, KEPT_LOW)
                        gate(ps_z, 0, b, NEW_LOW).then_inc(z_summed, 1)

            @block.scalar
            def _(act):
                with act.Fori(0, T // STEPS) as it:
                    for u in range(STEPS):
                        t, b = it * STEPS + u, u % 2
                        act.wait_ge(r_summed, t + 1)
                        act.activation(tr[:, b, :], ps_r[:, b, :2 * B], ACT.Tanh, scale=unscale[:, 0:1]).then_inc(tr_ready, 1)
                        act.wait_ge(z_summed, t + 1)
                        act.activation(tz[:, b, :], ps_z[:, b, :2 * B], ACT.Tanh, scale=unscale[:, 0:1]).then_inc(tz_ready, 1)
                        act.wait_ge(cand_ready, t + 1)
                        act.activation(tn[:, b, :], cand[:, b, :], ACT.Tanh).then_inc(tn_ready, 1)


def gru_out(nc, state, wp_dram, x_sb, x_dram):
    with Scope(nc, "go") as s:
        w = s.sb("w", [128, 2, CB, CP])
        ps = s.ps("ps", 4)
        loaded, summed, added, stored = s.sem("loaded"), s.sem("summed"), s.sem("added"), s.sem("stored")
        with nc.Block() as block:
            @block.sync
            def _(sp):
                sp.dma_start(w[:, 0, :, :], wp_dram[0:128]).then_inc(loaded, 16)
                sp.dma_start(w[0:64, 1, :, :], wp_dram[128:192]).then_inc(loaded, 16)
                for n in range(NT):
                    sp.wait_ge(added, 2 * n + 2)
                    sp.dma_start(x_dram[:, :, n * TB:(n + 1) * TB], x_sb[:, :, n * TB:(n + 1) * TB]).then_inc(stored, 16)
                sp.wait_ge(stored, 16 * NT)

            @block.tensor
            def _(pe):
                pe.wait_ge(loaded, 32)
                for n in range(NT):
                    for m in range(CB):
                        i = 2 * n + m
                        if i >= 4:
                            pe.wait_ge(added, i - 3)
                        for k, rows in ((0, 128), (1, 64)):
                            last = pe.matmul(ps[:CP, i % 4, :TB], w[:rows, k, m, :],
                                             state[:rows, 1:T + 1, k, 2 * n:2 * n + 2].rearrange("p t b -> p b t"),
                                             start=k == 0, stop=k == 1)
                        last.then_inc(summed, 1)

            @block.vector
            def _(dve):
                for n in range(NT):
                    for m in range(CB):
                        i = 2 * n + m
                        dve.wait_ge(summed, i + 1)
                        x = x_sb[:, m, n * TB:(n + 1) * TB]
                        dve.scalar_tensor_tensor(x, ps[:CP, i % 4, :TB], 1.0 / HSCALE, x, ALU.mult, ALU.add).then_inc(added, 1)


def gru_layer(nc, ins, x_in, y_out):
    with Scope(nc, "l0") as s:
        x_sb = s.sb("x", [CP, CB, N])
        with Scope(nc, "l0g") as s3:
            gates_in = s3.sb("gates_in", [128, T, 3, 4, B], bf16)
            cand_in = s3.sb("cand_in", [128, T, 2, B])
            wh, ident, bhn = s3.sb("wh", [128, CB, 3, 2, 128]), s3.sb("ident", [128, 128]), s3.sb("bhn", [128, 2])
            with Scope(nc, "l0n") as s2:
                xh, xl = s2.sb("xh", [CP, CB, N], f32r), s2.sb("xl", [CP, CB, N], f32r)
                gru_inputs(nc, x_in, ins["group_avg"], x_sb, xh, xl, ins["wx"], ins["bx"], ins["bh"], gates_in, cand_in,
                           [(wh[:, :, :, :, :], ins["wh"]), (ident[:, :], ins["ident128"]), (bhn[:, :], ins["bhn"])])
            with Scope(nc, "l0s") as s2:
                state = s2.sb("state", [128, T + 1, 2, B])
                gru(nc, gates_in, cand_in, state, wh, bhn, ident)
                gru_out(nc, state, ins["wp"], x_sb, y_out)


def attention(nc, tag, x_in, group_avg, xh, xl, v, wv_dram, bv_dram, w_dram, signs_dram, rel_dram, sel_dram, ident_dram, products, sums):
    ITEMS = NT + H
    ITEMS_OF_STEP = [0] + 4 * [1] + 9 * [2] + 2 * [0]
    LAG = 4
    EARLY = 12
    QK_MOVES, REL_MOVES = 12 * 16, 8 * 16
    with Scope(nc, tag) as s:
        qk = s.sb("qk", [128, N], f32r)
        q = [s.sb("q_a", [128, N], f32r), s.sb("q_b", [128, N], f32r)]
        k = [s.sb("k_a", [128, N], f32r), s.sb("k_b", [128, N], f32r)]
        rel = s.sb("rel", [128, N], f32r)
        vs = s.sb("vs", [128, 2 * B, 2, 33], f32r)
        w = s.sb("w", [CP + 1, PAIRS, CB, 128])
        wh, wl = s.sb("wh", [CP + 1, CB, 128], f32r), s.sb("wl", [CP + 1, CB, 128], f32r)
        wvh, wvl = s.sb("wvh", [CP, CB, C], f32r), s.sb("wvl", [CP, CB, C], f32r)
        signs = s.sb("signs", [128, 2])
        rh, rl = s.sb("rh", [128, H + W, 28], f32r), s.sb("rl", [128, H + W, 28], f32r)
        ident = s.sb("ident", [128, TH])
        hx = s.sb("hx", [128, 2, TB], f32r)
        mx = s.sb("mx", [128, 2, 4])
        mt = s.sb("mt", [128, 2, 64])
        p32, ph, pl = s.sb("p32", [128, 2, 2, TB]), s.sb("ph", [128, 4, 2, TB], f32r), s.sb("pl", [128, 2, 2, TB], f32r)
        o = s.sb("o", [33, 2, 2, TB])
        sel = s.sb("sel", [128, T])
        ps = s.ps("ps", 8)
        S_BANK, ITEM_BANK, T_BANK, O_BANK = 0, 2, 3, 7
        FIRST_BANKS, V_BANK = 4, 6

        def item_bank(p, n):
            return ITEM_BANK + n % FIRST_BANKS if isinstance(p, int) and p == 0 else ITEM_BANK

        norm = GroupNorm(s, lambda block, cols: q[block][:CP, cols].bitcast(f32), xh, xl, one_row=True,
                         place=v[:CP, :, :].rearrange("p i c -> p (i c)"))
        wv, bias_v = p32[:CP, 0, :, :C], p32[:TH, 1, 0, :C]
        mean_sums, var_sums = ps[:CP, 0, :CB * B], ps[:CP, 1, :CB * B]
        rw = rel[:, :(H + W) * 28].bitcast(f32).rearrange("p (n c) -> p n c", c=28)

        loaded, sel_in, const_ready, zeroed, q_zero = (s.sem(n) for n in ("loaded", "sel_in", "const_ready", "zeroed", "q_zero"))
        rh_ready, rl_ready, wh_ready, wl_ready = (s.sem(n) for n in ("rh_ready", "rl_ready", "wh_ready", "wl_ready"))
        vh_ready, vl_ready = s.sem("vh_ready"), s.sem("vl_ready")
        wv_in, wvh_ready, wvl_ready, v_summed, v_ready = (s.sem(n) for n in ("wv_in", "wvh_ready", "wvl_ready", "v_summed", "v_ready"))
        item_summed, item_high, item_low = s.sem("item_summed"), s.sem("item_high"), s.sem("item_low")
        qk_moved, rel_moved = ([s.sem(f"{n}_{half}_moved") for half in ("first", "second")] for n in ("qk", "rel"))
        s_summed, mx_ready, mh_ready, ml_ready = (s.sem(n) for n in ("s_summed", "mx_ready", "mh_ready", "ml_ready"))
        x_ready, x_copied, t_summed, p_ready = (s.sem(n) for n in ("x_ready", "x_copied", "t_summed", "p_ready"))
        pl_ready, o_summed, o_ready = (s.sem(n) for n in ("pl_ready", "o_summed", "o_ready"))
        o_free = [s.sem("even_free"), s.sem("odd_free")]

        def two(x):
            return x.rearrange("p (h k) -> p h k", h=2)

        def for_all_pairs(eng, step):
            for i in range(B):
                step(0, i, True, False)
            with eng.Fori(1, PAIRS - 1) as p:
                for i in range(B):
                    step(p, i, False, False)
            for i in range(B + LAG):
                step(PAIRS - 1, i, False, True)

        def image(p, i, lag, first):
            if i - lag >= B or (first and i < lag):
                return None
            return (p, i - lag) if i >= lag else (p - 1, i - lag + B)

        def behind(p, b, n):
            return b >= n or not isinstance(p, int) or p > 0

        def items_of_step(i):
            first = sum(ITEMS_OF_STEP[:i])
            return list(range(first, first + ITEMS_OF_STEP[i])) if i < B else []

        with nc.Block() as block:
            @block.sync
            def _(sp):
                qk_parts = [m for head in range(2) for m in (
                    (q[head], 64, k[head], 60, 2), (q[head], 0, qk, 64 * head, 32), (q[head], 80, qk, 64 * head, 16),
                    (k[head], 0, qk, 64 * head + 32, 16), (k[head], 16, qk, 64 * head + 32, 16), (k[head], 80, qk, 64 * head + 48, 16))]
                rel_h_parts = [(q[head], 32 + low, rel, 14 * head + low, 14) for head in range(2) for low in (0, 64)]
                rel_w_parts = [(q[head], 46 + low, rel, 14 * head + 32 + low, 14) for head in range(2) for low in (0, 64)]
                rel_parts = rel_h_parts + rel_w_parts

                def move(half, parts, moved):
                    cols = slice(half * N // 2, (half + 1) * N // 2)
                    for dst, at, src, first, rows in parts:
                        sp.dma_start(dst[at:at + rows, cols].bitcast(f32),
                                     src[first:first + rows, cols].bitcast(f32)).then_inc(moved[half], 16)

                sp.dma_start(sel[:, :], sel_dram).then_inc(sel_in, 16)
                norm.load(sp, x_in, group_avg)
                sp.dma_start(wv, wv_dram).then_inc(wv_in, 16)
                sp.dma_start(bias_v, bv_dram).then_inc(wv_in, 16)
                sp.dma_start(w[:, :, :, :], w_dram).then_inc(loaded, 16)
                sp.dma_start(rw, rel_dram).then_inc(loaded, 16)
                sp.dma_start(signs[:, :], signs_dram).then_inc(loaded, 16)
                sp.dma_start(ident[:TH, :], ident_dram).then_inc(loaded, 16)
                sp.wait_ge(const_ready, 2)
                sp.wait_ge(q_zero, 2)
                sp.wait_ge(item_low, NT)
                move(0, qk_parts, qk_moved)
                sp.wait_ge(item_low, ITEMS)
                move(0, rel_parts, rel_moved)
                move(1, qk_parts, qk_moved)
                move(1, rel_parts, rel_moved)

                def store(p, j):
                    sp.wait_ge(o_ready, p * B + 2 * j + 2)
                    cols = slice(j * TB, (j + 1) * TB)
                    pair = bass.ds(p * 2, 2)
                    sp.dma_start(products[pair, :, cols].rearrange("h r n -> r h n"), o[0:32, j % 2, :, :]).then_inc(o_free[j % 2], 16)
                    sp.dma_start(sums[pair, cols].rearrange("(a h) n -> a h n", a=1), o[32:33, j % 2, :, :]).then_inc(o_free[j % 2], 16)

                def step(p, i, first, last):
                    if i == 0 and not first:
                        sp.wait_ge(t_summed, p * B)
                        move(1, qk_parts, qk_moved)
                    if i == 2 and not first:
                        move(1, rel_parts, rel_moved)
                    now = image(p, i, LAG, first)
                    if now and now[1] % 2 == 1:
                        store(now[0], now[1] // 2)
                    if last:
                        return
                    if i == 9:
                        sp.wait_ge(t_summed, p * B + B // 2)
                    if i in (9, 11):
                        move(0, qk_parts[6 * (i // 11):6 * (i // 11) + 6], qk_moved)
                    if i == 11:
                        sp.wait_ge(item_low, ITEMS * (p + 1) + NT + H // 2)
                        move(0, rel_h_parts, rel_moved)
                    if i == 13:
                        sp.wait_ge(item_low, ITEMS * (p + 1) + ITEMS)
                        move(0, rel_w_parts, rel_moved)

                for_all_pairs(sp, step)
                for slot in range(2):
                    sp.wait_ge(o_free[slot], 16 + PAIRS * 8 * B)

            @block.gpsimd
            def _(pool):
                def fill_k(head):
                    pool.tensor_copy(k[head][:, :].rearrange("p (b t) -> p b t", b=B),
                                     sel[:, :].rearrange("p (b t) -> p b t", b=1).to_broadcast([128, B, T])).then_inc(const_ready, 1)

                pool.memset(mt[:, :, :], 0.0).then_inc(zeroed, 1)
                pool.memset(vs[:, :, :, 32:33].bitcast(f32), 1.0).then_inc(zeroed, 1)
                pool.wait_ge(sel_in, 16)
                fill_k(0)
                pool.wait_ge(zeroed, 2)
                pool.wait_ge(const_ready, 1)
                norm.gpsimd(pool)
                fill_k(1)
                norm.await_images(pool, B)
                for head in range(2):
                    pool.memset(q[head][:, :].bitcast(f32), 0.0).then_inc(q_zero, 1)

                def step(p, i, first, last):
                    if i >= B:
                        return
                    g = p * B + i
                    pool.wait_ge(p_ready, 2 * g + 2)
                    if behind(p, i, 2):
                        pool.wait_ge(o_summed, g - 1)
                    pool.tensor_tensor(pl[:TH, i % 2, :, :], p32[:TH, i % 2, :, :], ph[:TH, i % 4, :, :].bitcast(f32),
                                       ALU.subtract).then_inc(pl_ready, 1)

                for_all_pairs(pool, step)

            @block.tensor
            def _(pe):
                def item(p, n):
                    if n == 0:
                        pe.wait_ge(wl_ready, p + 1)
                    bank = item_bank(p, n)
                    if not isinstance(p, int) or p or n == NT:
                        pe.wait_ge(item_low, ITEMS * p + n)
                    elif n >= FIRST_BANKS:
                        pe.wait_ge(item_low, n - FIRST_BANKS + 1)
                    if n < NT:
                        cols = slice(n * TB, (n + 1) * TB)
                        product3(pe, ps[:, bank, :TB], lambda c: wh[:, c, :], lambda c: wl[:, c, :],
                                 lambda c: xh[:, c, cols], lambda c: xl[:, c, cols]).then_inc(item_summed, 1)
                        return
                    q4 = qk[:, :].rearrange("p (b h w) -> p h w b", b=B, h=H)
                    for u in range(2):
                        r = 2 * (n - NT) + u
                        qs = q4[:, r, :, :].rearrange("p w b -> p b w") if r < H else q4[:, :, r - H, :].rearrange("p h b -> p b h")
                        out = ps[:28, bank, u * 224:u * 224 + 224]
                        pe.matmul(out, rh[:, r, :], qs, start=True, stop=False)
                        last = pe.matmul(out, rl[:, r, :], qs, start=False, stop=True)
                    last.then_inc(item_summed, 1)

                def logits_by_query(p, b):
                    if b % (B // 2) == 0:
                        pe.wait_ge(qk_moved[b // (B // 2)], QK_MOVES * (p + 1))
                        pe.wait_ge(rel_moved[b // (B // 2)], REL_MOVES * (p + 1))
                    if behind(p, b, 1):
                        pe.wait_ge(mx_ready, p * B + b)
                    keys = slice(b * T, (b + 1) * T)
                    for head in range(2):
                        for half in range(2):
                            queries = slice(b * T + half * TH, b * T + (half + 1) * TH)
                            last = pe.matmul(ps[:TH, S_BANK + head, half * T:half * T + T], q[head][:, queries],
                                             k[head][:, keys], start=True, stop=True)
                    last.then_inc(s_summed, 1)

                def maxima_to_rows(p, b):
                    pe.wait_ge(ml_ready, p * B + b + 1)
                    if behind(p, b, 1):
                        pe.wait_ge(x_copied, 2 * (p * B + b))
                    for half in range(2):
                        last = pe.matmul(ps[64:128, O_BANK, half * TH:half * TH + TH], mt[:TH, half, :], ident[:TH, :], start=True, stop=True)
                    last.then_inc(x_ready, 1)

                def logits_by_key(p, b):
                    pe.wait_ge(x_copied, 2 * (p * B + b) + 2)
                    if behind(p, b, 2):
                        pe.wait_ge(p_ready, 2 * (p * B + b) - 2)
                    queries = slice(b * T, (b + 1) * T)
                    for head in range(2):
                        for half in range(2):
                            keys = slice(b * T + half * TH, b * T + (half + 1) * TH)
                            last = pe.matmul(ps[:TH, T_BANK + 2 * (b % 2) + head, half * T:half * T + T], k[head][:, keys],
                                             q[head][:, queries], start=True, stop=True)
                    last.then_inc(t_summed, 1)

                def weigh_values(p, b):
                    pe.wait_ge(pl_ready, p * B + b + 1)
                    if b in (0, EARLY):
                        pe.wait_ge(vl_ready, 2 * p + (1 if b == 0 else 2))
                    if behind(p, b, 1):
                        pe.wait_ge(o_ready, p * B + b)
                    for head in range(2):
                        for half in range(2):
                            lhs = vs[:TH, 2 * b + half, head, :]
                            out = ps[:33, O_BANK, head * T:head * T + T]
                            pe.matmul(out, lhs, ph[:TH, b % 4, head, half * T:half * T + T], start=half == 0, stop=False)
                            last = pe.matmul(out, lhs, pl[:TH, b % 2, head, half * T:half * T + T], start=False, stop=half == 1)
                    last.then_inc(o_summed, 1)

                def step(p, i, first, last):
                    items = [] if last else items_of_step(i)
                    if i < B:
                        logits_by_query(p, i)
                    now = image(p, i, 1, first)
                    if now:
                        maxima_to_rows(*now)
                    for n in items[:1]:
                        item(p + 1, n)
                    before = image(p, i, LAG, first)
                    if before:
                        weigh_values(*before)
                    if now:
                        logits_by_key(*now)
                    for n in items[1:]:
                        item(p + 1, n)

                norm.tensor(pe, mean_sums, var_sums)
                pe.wait_ge(zeroed, 2)
                pe.wait_ge(rl_ready, 1)
                pe.wait_ge(wvl_ready, 1)
                pe.wait_ge(norm.row_ready, 2)
                for n in range(ITEMS):
                    if n < NT:
                        norm.await_images(pe, 2 * n + 2)
                    item(0, n)
                for i in range(2 * B):
                    if i >= 2:
                        pe.wait_ge(v_ready, i - 1)
                    tok = slice(i * TH, (i + 1) * TH)
                    product3(pe, ps[:TH, V_BANK + i % 2, :C], lambda c: xh[:CP, c, tok], lambda c: xl[:CP, c, tok],
                             lambda c: wvh[:, c, :], lambda c: wvl[:, c, :]).then_inc(v_summed, 1)
                pe.wait_ge(v_ready, 2 * B)
                pe.wait_ge(item_low, ITEMS)
                for_all_pairs(pe, step)

            @block.scalar
            def _(act):
                def item(p, n):
                    act.wait_ge(item_summed, ITEMS * p + n + 1)
                    if n < NT:
                        if isinstance(p, int) and p == 0 and n >= 2:
                            act.wait_ge(item_low, n - 1)
                        act.activation(hx[:, n % 2, :], ps[:, item_bank(p, n), :TB], ACT.Copy, scale=signs[:, 0:1]).then_inc(item_high, 1)
                        return
                    if n == NT and (not isinstance(p, int) or p):
                        for half in range(2):
                            act.wait_ge(rel_moved[half], REL_MOVES * p)
                    act.activation(rel_out(rel, n - NT, 0), rel_in(ps, item_bank(p, n)), ACT.Copy).then_inc(item_high, 1)

                def step(p, i, first, last):
                    items = [] if last else items_of_step(i)
                    now = image(p, i, 1, first)
                    if now:
                        pair, b = now
                        cols = slice(b * T, (b + 1) * T)
                        act.wait_ge(x_ready, pair * B + b + 1)
                        for head in range(2):
                            r = 64 + 32 * head
                            act.activation(q[head][64:66, cols], ps[r:r + 2, O_BANK, :T], ACT.Copy).then_inc(x_copied, 1)
                    for n in items[:1]:
                        item(p + 1, n)
                    now = image(p, i, 2, first)
                    if now:
                        pair, b = now
                        g = pair * B + b
                        act.wait_ge(t_summed, g + 1)
                        if behind(pair, b, 4):
                            act.wait_ge(o_summed, g - 3)
                        if behind(pair, b, 2):
                            act.wait_ge(pl_ready, g - 1)
                        banks = ps[:TH, T_BANK + 2 * (b % 2):T_BANK + 2 * (b % 2) + 2, :TB]
                        act.activation(ph[:TH, b % 4, :, :], banks, ACT.Exp).then_inc(p_ready, 1)
                        act.activation(p32[:TH, b % 2, :, :], banks, ACT.Exp).then_inc(p_ready, 1)
                    for n in items[1:]:
                        item(p + 1, n)

                norm.scalar(act, var_sums)
                act.wait_ge(loaded, 64)
                act.wait_ge(rl_ready, 1)
                for n in range(ITEMS):
                    item(0, n)
                for_all_pairs(act, step)

            @block.vector
            def _(dve):
                def split_w(p):
                    wp = w[:, p] if isinstance(p, int) else w[:, bass.ds(p, 1)].rearrange("c a k n -> c (a k) n")
                    dve.tensor_copy(wh[:, :, :], wp).then_inc(wh_ready, 1)
                    dve.wait_ge(wh_ready, p + 1)
                    dve.tensor_tensor(wl[:, :, :], wp, wh[:, :, :].bitcast(f32), ALU.subtract).then_inc(wl_ready, 1)

                def item(p, n):
                    dve.wait_ge(item_high, ITEMS * p + n + 1)
                    if n < NT:
                        if n % (NT // 2) == 0 and (not isinstance(p, int) or p):
                            dve.wait_ge(qk_moved[n // (NT // 2)], QK_MOVES * p)
                        dve.scalar_tensor_tensor(qk[:, n * TB:(n + 1) * TB], ps[:, item_bank(p, n), :TB], signs[:, 1:2],
                                                 hx[:, n % 2, :].bitcast(f32), ALU.mult, ALU.subtract).then_inc(item_low, 1)
                        return
                    dve.tensor_tensor(rel_out(rel, n - NT, 64), rel_in(ps, item_bank(p, n)), rel_out(rel, n - NT, 0).bitcast(f32),
                                      ALU.subtract).then_inc(item_low, 1)

                def step(p, i, first, last):
                    items = [] if last else items_of_step(i)
                    if i < B:
                        g = p * B + i
                        dve.wait_ge(s_summed, g + 1)
                        dve.tensor_reduce(mx[:TH, i % 2, :], ps[:TH, S_BANK:S_BANK + 2, :TB].rearrange("p c (h k) -> p c h k", h=2),
                                          AXIS.X, ALU.max).then_inc(mx_ready, 1)
                        m = mx[:TH, i % 2, :].rearrange("p (c h) -> p h c", c=2)
                        high, low = mt[:TH, :, 0:33:32], mt[:TH, :, 1:34:32]
                        dve.wait_ge(mx_ready, g + 1)
                        if behind(p, i, 1):
                            dve.wait_ge(x_ready, g)
                        dve.tensor_copy(high.bitcast(f32r), m).then_inc(mh_ready, 1)
                        dve.wait_ge(mh_ready, g + 1)
                        dve.tensor_tensor(low, m, high, ALU.subtract).then_inc(ml_ready, 1)
                    if i == 0 and not last:
                        split_w(p + 1)
                    for n in items[:1]:
                        item(p + 1, n)
                    now = image(p, i, LAG, first)
                    if now:
                        pair, c = now
                        j = c // 2
                        dve.wait_ge(o_summed, pair * B + c + 1)
                        if c % 2 == 0:
                            dve.wait_ge(o_free[j % 2], 8 * B * pair + 32 * (j // 2) + 16)
                        dve.tensor_copy(o[:, j % 2, :, c % 2 * T:c % 2 * T + T], two(ps[:33, O_BANK, :TB])).then_inc(o_ready, 1)
                    if i == 1:
                        split_v(p, slice(0, 2 * EARLY), 2 * p + 1)
                    if i == LAG - 1:
                        split_v(p, slice(2 * EARLY, 2 * B), 2 * p + 2)
                    for n in items[1:]:
                        item(p + 1, n)

                def split_v(p, halves, count):
                    vp = v[:TH, halves, bass.ds(p * 32, 32)].rearrange("t i (h d) -> t i h d", h=2)
                    vhi, vlo = vs[:TH, halves, :, 0:HD], vs[:TH, halves, :, HD:2 * HD]
                    dve.tensor_copy(vhi, vp).then_inc(vh_ready, 1)
                    dve.wait_ge(vh_ready, count)
                    dve.tensor_tensor(vlo, vp, vhi.bitcast(f32), ALU.subtract).then_inc(vl_ready, 1)

                norm.statistics(dve, mean_sums)
                for slot in range(2):
                    dve.memset(o[:, slot, :, :], 0.0).then_inc(o_free[slot], 16)
                dve.wait_ge(wv_in, 32)
                split(dve, wv, wvh[:, :, :], wvl[:, :, :], wvh_ready, wvl_ready, 0)
                dve.wait_ge(loaded, 64)
                split_w(0)
                split(dve, rw, rh[:, :, :], rl[:, :, :], rh_ready, rl_ready, 0)
                norm.normalize(dve)
                norm.await_images(dve, B)
                for n in range(ITEMS):
                    item(0, n)
                for i in range(2 * B):
                    dve.wait_ge(v_summed, i + 1)
                    dve.tensor_tensor(v[:TH, i, :], ps[:TH, V_BANK + i % 2, :C], bias_v, ALU.add).then_inc(v_ready, 1)
                dve.wait_ge(v_ready, 2 * B)
                dve.wait_ge(zeroed, 2)
                for_all_pairs(dve, step)


def rel_in(ps, bank):
    return ps[:28, bank, :448].rearrange("p (u b w) -> p u b w", u=2, b=B)


def rel_out(rel, j, low):
    part = 0 if j < 7 else 32
    n = 2 * (j % 7)
    tile = rel[low + part:low + part + 28, :].rearrange("p (b h w) -> p h b w", b=B, h=H)
    return tile[:, n:n + 2, :, :] if j < 7 else tile.rearrange("p h b w -> p w b h")[:, n:n + 2, :, :]


def project(nc, tag, products, sums, w_dram, b_dram, x_dram, y_dram):
    KC = HEADS * 32 // 128
    SLOTS = 4
    with Scope(nc, tag) as s:
        w = s.sb("w", [128, KC, CB, CP])
        bias = s.sb("bias", [CP, CB])
        den, rec = s.sb("den", [128, HEADS * N // 128]), s.sb("rec", [128, HEADS * N // 128])
        hin, rin = s.sb("hin", [128, SLOTS, KC, TB]), s.sb("rin", [128, SLOTS, KC, TB])
        hn = s.sb("hn", [128, 2, KC, TB])
        xin = s.sb("xin", [CP, SLOTS, CB, TB])
        y = s.sb("y", [CP, 2, CB, TB])
        ps = s.ps("ps", 4)
        loaded, den_in, rec_ready, rec_stored = (s.sem(n) for n in ("loaded", "den_in", "rec_ready", "rec_stored"))
        summed, added, scaled = s.sem("summed"), s.sem("added"), s.sem("scaled")
        stored = [s.sem("even_stored"), s.sem("odd_stored")]
        slot_in = [s.sem(f"slot{n}_in") for n in range(SLOTS)]
        LOADS = 6
        with nc.Block() as block:
            @block.sync
            def _(sp):
                sp.dma_start(den[:, :], sums.rearrange("h n -> (h n)").rearrange("(p f) -> p f", p=128)).then_inc(den_in, 16)
                sp.dma_start(w[:, :, :, :], w_dram).then_inc(loaded, 16)
                sp.dma_start(bias[:, :], b_dram).then_inc(loaded, 16)
                for n in range(NT):
                    cols = slice(n * TB, (n + 1) * TB)
                    if n >= SLOTS:
                        sp.wait_ge(added, 2 * (n - SLOTS) + 2)
                    sp.dma_start(hin[:, n % SLOTS, :, :], products[:, :, cols].rearrange("(k h) r n -> (h r) k n", k=KC)).then_inc(slot_in[n % SLOTS], 16)
                    sp.dma_start(xin[:, n % SLOTS, :, :], x_dram[:, :, cols]).then_inc(slot_in[n % SLOTS], 16)
                    if n == 0:
                        sp.wait_ge(rec_stored, 16)
                    for h in range(4):
                        sp.dma_start(rin[32 * h:32 * h + 32, n % SLOTS, :, :],
                                     sums.rearrange("(a k h) n -> h a k n", a=1, h=4)[h, :, :, cols].to_broadcast([32, KC, TB])).then_inc(slot_in[n % SLOTS], 16)
                for slot in range(2):
                    sp.wait_ge(stored[slot], 8 * NT)

            @block.scalar
            def _(act):
                act.wait_ge(rec_ready, 1)
                act.dma_start(sums.rearrange("h n -> (h n)").rearrange("(p f) -> p f", p=128), rec[:, :]).then_inc(rec_stored, 16)
                for n in range(NT):
                    act.wait_ge(added, 2 * n + 2)
                    act.dma_start(y_dram[:, :, n * TB:(n + 1) * TB], y[:, n % 2, :, :]).then_inc(stored[n % 2], 16)

            @block.tensor
            def _(pe):
                pe.wait_ge(loaded, 32)
                for n in range(NT):
                    pe.wait_ge(scaled, n + 1)
                    for m in range(CB):
                        i = 2 * n + m
                        if i >= 4:
                            pe.wait_ge(added, i - 3)
                        for k in range(KC):
                            last = pe.matmul(ps[:CP, i % 4, :TB], w[:, k, m, :], hn[:, n % 2, k, :], start=k == 0, stop=k == KC - 1)
                        last.then_inc(summed, 1)

            @block.gpsimd
            def _(pool):
                for n in range(NT):
                    pool.wait_ge(slot_in[n % SLOTS], 16 * LOADS * (n // SLOTS + 1))
                    if n >= 2:
                        pool.wait_ge(summed, 2 * n - 2)
                    pool.tensor_tensor(hn[:, n % 2, :, :], hin[:, n % SLOTS, :, :], rin[:, n % SLOTS, :, :], ALU.mult).then_inc(scaled, 1)

            @block.vector
            def _(dve):
                dve.wait_ge(den_in, 16)
                dve.reciprocal(rec[:, :], den[:, :]).then_inc(rec_ready, 1)
                dve.wait_ge(loaded, 32)
                for n in range(NT):
                    dve.wait_ge(slot_in[n % SLOTS], 16 * LOADS * (n // SLOTS + 1))
                    if n >= 2:
                        dve.wait_ge(stored[n % 2], 16 * (n // 2))
                    for m in range(CB):
                        i = 2 * n + m
                        dve.wait_ge(summed, i + 1)
                        dve.scalar_tensor_tensor(y[:, n % 2, m, :], ps[:CP, i % 4, :TB], bias[:, m:m + 1], xin[:, n % SLOTS, m, :],
                                                 ALU.add, ALU.add).then_inc(added, 1)


def attention_layer(nc, tag, ins, x_in, y_out, scratch):
    with Scope(nc, tag) as s:
        xh, xl = s.sb("xh", [CP + 1, CB, N], f32r), s.sb("xl", [CP + 1, CB, N], f32r)
        v = s.sb("v", [128, 2 * B, C])
        attention(nc, tag + "a", x_in, ins["group_avg"], xh, xl, v, ins[tag + "_wv"], ins[tag + "_bv"], ins[tag + "_wqk"], ins["signs"], ins[tag + "_rel"],
                  ins["sel"], ins["ident98"],
                  scratch["products"], scratch["sums"])
    project(nc, tag + "p", scratch["products"], scratch["sums"], ins[tag + "_wo"], ins[tag + "_bo"], x_in, y_out)


def route(nc, x_in, group_avg, x_sb, xh, xl, packed, gate_dram, first_dram, ident_dram, w_rows, ahead):
    HALVES = 2 * B
    with Scope(nc, "ro") as s:
        g = s.sb("g", [CP, CB, E])
        gh, gl = s.sb("gh", [CP, CB, E], f32r), s.sb("gl", [CP, CB, E], f32r)
        ident = s.sb("ident", [128, TH])
        first = s.sb("first", [128, E])
        by_expert = s.sb("by_expert", [E, N])
        logit, seen = s.sb("logit", [128, HALVES, E]), s.sb("seen", [128, HALVES, E])
        key, pick1, pick2 = s.sb("key", [128, HALVES, E]), s.sb("pick1", [128, HALVES, E]), s.sb("pick2", [128, HALVES, E])
        m1, m2, km, d, e2, den, w1, w2 = (s.sb(n, [128, HALVES]) for n in "m1 m2 km d e2 den w1 w2".split())
        wt = s.sb("wt", [128, HALVES, 2 * E])
        ps = s.ps("ps", 8)
        norm = GroupNorm(s, lambda k, cols: x_sb[:, k, cols], xh, xl)
        mean_sums, var_sums = ps[:CP, 5, :CB * B], ps[:CP, 6, :CB * B]
        loaded, gh_ready, gl_ready, summed = (s.sem(n) for n in ("loaded", "gh_ready", "gl_ready", "summed"))
        copied, turned, chain, m_diff, e2_ready = (s.sem(n) for n in ("copied", "turned", "chain", "m_diff", "e2_ready"))
        wt_ready, back_turned, rows_ready = (s.sem(n) for n in ("wt_ready", "back_turned", "rows_ready"))
        packs, ahead_in = s.sem("packs"), s.sem("ahead_in")
        with nc.Block() as block:
            @block.sync
            def _(sp):
                norm.load(sp, x_in, group_avg)
                sp.dma_start(g[:, :, :], gate_dram).then_inc(loaded, 16)
                sp.dma_start(ident[:TH, :], ident_dram).then_inc(loaded, 16)
                sp.dma_start(first[:TH, :], first_dram).then_inc(loaded, 16)
                xa, xb, la, lb = packed
                for half in range(2):
                    cols = slice(half * N // 2, (half + 1) * N // 2)
                    norm.await_images(sp, (half + 1) * B // 2)
                    for dst, at, src, k, rows in ((xa, 0, xh, 0, slice(0, 96)), (xa, 96, xh, 1, slice(0, 32)),
                                                  (xb, 0, xh, 1, slice(32, 96)), (xb, 64, xh, 1, slice(32, 96)),
                                                  (la, 0, xl, 0, slice(0, 96)), (la, 96, xl, 1, slice(0, 32)),
                                                  (lb, 0, xl, 1, slice(32, 96))):
                        sp.dma_start(dst[at:at + rows.stop - rows.start, cols].bitcast(f32),
                                     src[rows, k, cols].bitcast(f32)).then_inc(packs, 16)
                for dst, src in ahead:
                    sp.dma_start(dst, src).then_inc(ahead_in, 16)
                sp.wait_ge(ahead_in, 16 * len(ahead))
                sp.wait_ge(packs, 2 * 7 * 16)

            @block.gpsimd
            def _(pool):
                norm.gpsimd(pool)

            @block.tensor
            def _(pe):
                norm.tensor(pe, mean_sums, var_sums)
                pe.wait_ge(gl_ready, 1)
                for t in range(NT):
                    norm.await_images(pe, 2 * t + 2)
                    if t >= 4:
                        pe.wait_ge(copied, t - 3)
                    product3(pe, ps[:E, t % 4, :TB], lambda k: gh[:, k, :], lambda k: gl[:, k, :],
                             lambda k: xh[:, k, t * TB:(t + 1) * TB], lambda k: xl[:, k, t * TB:(t + 1) * TB]).then_inc(summed, 1)
                pe.wait_ge(copied, NT)
                for i in range(HALVES):
                    last = pe.transpose(ps[:TH, 4, i * E:(i + 1) * E], by_expert[:, i * TH:(i + 1) * TH], ident[:E, :E])
                last.then_inc(turned, 1)
                pe.wait_ge(wt_ready, 2)
                for i in range(HALVES):
                    last = pe.transpose(ps[:2 * E, i // 4, (i % 4) * TH:(i % 4 + 1) * TH], wt[:TH, i, :], ident[:TH, :])
                    if i % 4 == 3:
                        last.then_inc(back_turned, 1)

            @block.scalar
            def _(act):
                norm.scalar(act, var_sums)
                for t in range(NT):
                    act.wait_ge(summed, t + 1)
                    act.activation(by_expert[:, t * TB:(t + 1) * TB], ps[:E, t % 4, :TB], ACT.Copy).then_inc(copied, 1)
                act.wait_ge(m_diff, 1)
                act.activation(e2[:TH, :], d[:TH, :], ACT.Exp).then_inc(e2_ready, 1)
                for t in range(NT):
                    act.wait_ge(back_turned, t + 1)
                    act.activation(w_rows[:, t * TB:(t + 1) * TB], ps[:2 * E, t, :TB], ACT.Copy).then_inc(rows_ready, 1)
                act.wait_ge(rows_ready, NT)

            @block.vector
            def _(dve):
                norm.statistics(dve, mean_sums)
                dve.wait_ge(loaded, 48)
                split(dve, g[:, :, :], gh[:, :, :], gl[:, :, :], gh_ready, gl_ready, 0)
                norm.normalize(dve)
                done = [0]

                def link(ins):
                    done[0] += 1
                    ins.then_inc(chain, 1)
                    dve.wait_ge(chain, done[0])

                def over(x):
                    return x[:TH, :].rearrange("p (i a) -> p i a", a=1).to_broadcast([TH, HALVES, E])

                rank = first[:TH, :].rearrange("p (a e) -> p a e", a=1).to_broadcast([TH, HALVES, E])

                def largest(values, m, pick):
                    link(dve.tensor_reduce(m[:TH, :], values[:TH, :, :], AXIS.X, ALU.max))
                    link(dve.tensor_tensor(key[:TH, :, :], values[:TH, :, :], over(m), ALU.is_equal))
                    link(dve.tensor_tensor(key[:TH, :, :], key[:TH, :, :], rank, ALU.mult))
                    link(dve.tensor_reduce(km[:TH, :], key[:TH, :, :], AXIS.X, ALU.max))
                    link(dve.tensor_tensor(pick[:TH, :, :], key[:TH, :, :], over(km), ALU.is_equal))

                dve.wait_ge(turned, 1)
                link(dve.tensor_copy(logit[:TH, :, :], ps[:TH, 4, :HALVES * E].rearrange("p (i e) -> p i e", e=E)))
                largest(logit, m1, pick1)
                link(dve.scalar_tensor_tensor(seen[:TH, :, :], pick1[:TH, :, :], NEG, logit[:TH, :, :], ALU.mult, ALU.add))
                largest(seen, m2, pick2)
                dve.tensor_tensor(d[:TH, :], m2[:TH, :], m1[:TH, :], ALU.subtract).then_inc(m_diff, 1)
                dve.wait_ge(e2_ready, 1)
                link(dve.tensor_scalar(den[:TH, :], e2[:TH, :], 1.0, None, ALU.add))
                link(dve.reciprocal(w1[:TH, :], den[:TH, :]))
                link(dve.tensor_tensor(w2[:TH, :], e2[:TH, :], w1[:TH, :], ALU.mult))
                link(dve.tensor_tensor(pick1[:TH, :, :], pick1[:TH, :, :], over(w1), ALU.mult))
                link(dve.tensor_tensor(pick2[:TH, :, :], pick2[:TH, :, :], over(w2), ALU.mult))
                link(dve.tensor_tensor(key[:TH, :, :], pick1[:TH, :, :], pick2[:TH, :, :], ALU.add))
                dve.tensor_copy(wt[:TH, :, :E].bitcast(f32r), key[:TH, :, :]).then_inc(wt_ready, 1)
                dve.wait_ge(wt_ready, 1)
                dve.tensor_tensor(wt[:TH, :, E:].bitcast(f32r), key[:TH, :, :], wt[:TH, :, :E], ALU.subtract).then_inc(wt_ready, 1)


def product_packed(pe, out, wh, wl, packed):
    xa, xb, la, lb = packed
    pe.matmul(out, wh(0), xa, start=True, stop=False)
    pe.matmul(out, wl, xa, start=False, stop=False)
    pe.matmul(out, wh(0), la, start=False, stop=False)
    pe.matmul(out, wh(1), xb, start=False, stop=False)
    return pe.matmul(out, wh(1)[:64], lb[:64], start=False, stop=True)


def split_packed(dve, w, wh, wl, high_ready, low_ready, count):
    dve.tensor_copy(wh, w).then_inc(high_ready, 1)
    dve.wait_ge(high_ready, count + 1)
    dve.tensor_tensor(wl, w[:, 0], wh[:, 0].bitcast(f32), ALU.subtract).then_inc(low_ready, 1)
    dve.tensor_tensor(wh[64:128, 1], w[64:128, 1], wh[64:128, 1].bitcast(f32), ALU.subtract).then_inc(low_ready, 1)


def experts(nc, packed, w_rows, w1, w2, w1_dram, b1_dram, w2_dram, b2_dram, pick_dram, x_sb, ahead):
    with Scope(nc, "ex") as s:
        w1h, w1l = s.sb("w1h", [128, 2, 2, F], f32r), s.sb("w1l", [128, 2, F], f32r)
        w2h, w2l = s.sb("w2h", [128, 2, FB, C], f32r), s.sb("w2l", [128, 2, FB, C], f32r)
        b1, b2 = s.sb("b1", [128, 2, FB]), s.sb("b2", [CP, 2, CB])
        pick32 = s.sb("pick32", [2 * E, 2, CP])
        pick = s.sb("pick", [2 * E, 2, CP], f32r)
        hh, hl = s.sb("hh", [128, 2, FB, TB], f32r), s.sb("hl", [128, 2, FB, TB], f32r)
        h32 = s.sb("h32", [128, 2, TB])
        wb = s.sb("wb", [CP, 2, TB])
        y = s.sb("y", [CP, 2, CB, TB])
        ps_u, ps_d, ps_w = s.ps("ps_u", 4), s.ps("ps_d", 2), s.ps("ps_w", 2)
        ahead_in, big_in, small_in = s.sem("ahead_in"), s.sem("big_in"), [s.sem("even_in"), s.sem("odd_in")]
        high_ready, low_ready, pick_ready = s.sem("high_ready"), s.sem("low_ready"), s.sem("pick_ready")
        up_summed, hh_ready, h32_ready, hl_ready = (s.sem(n) for n in ("up_summed", "hh_ready", "h32_ready", "hl_ready"))
        down_summed, wb_summed, wb_ready, y_ready, x_added = (
            s.sem(n) for n in ("down_summed", "wb_summed", "wb_ready", "y_ready", "x_added"))

        def for_all_experts(eng, body):
            body(0, 0, True, False)
            with eng.Fori(0, (E - 2) // 2) as it:
                for u in (1, 0):
                    body(it * 2 + (1 if u else 2), u, False, False)
            body(E - 1, 1, False, True)

        with nc.Block() as block:
            @block.sync
            def _(sp):
                for e in range(E):
                    if e >= 1:
                        sp.wait_ge(low_ready, 3 * e)
                        sp.dma_start(w1[:, :, :], w1_dram[e]).then_inc(big_in, 16)
                        sp.dma_start(w2[:, :, :], w2_dram[e]).then_inc(big_in, 16)
                    if e >= 2:
                        sp.wait_ge(y_ready, 2 * NT * (e - 1))
                    for dst, src in ((b1, b1_dram), (b2, b2_dram), (pick32, pick_dram)):
                        sp.dma_start(dst[:, e % 2, :], src[e]).then_inc(small_in[e % 2], 16)
                for dst, src in ahead:
                    sp.dma_start(dst, src).then_inc(ahead_in, 16)
                sp.wait_ge(ahead_in, 16 * len(ahead))

            @block.tensor
            def _(pe):
                def down(i, t, u):
                    pe.wait_ge(hl_ready, 4 * i + 4)
                    for m in range(CB):
                        if not (isinstance(i, int) and i == 0):
                            pe.wait_ge(y_ready, 2 * i + m - 1)
                        cols = slice(m * CP, (m + 1) * CP)
                        product3(pe, ps_d[:CP, m, :TB], lambda k: w2h[:, u, k, cols], lambda k: w2l[:, u, k, cols],
                                 lambda k: hh[:, t % 2, k, :], lambda k: hl[:, t % 2, k, :], blocks=FB).then_inc(down_summed, 1)

                def body(e, u, first, last):
                    pe.wait_ge(low_ready, 3 * e + 3)
                    pe.wait_ge(pick_ready, e + 1)
                    for t in range(NT):
                        i = e * NT + t
                        tok = slice(t * TB, (t + 1) * TB)
                        for f in range(FB):
                            if not (first and t == 0):
                                pe.wait_ge(h32_ready, 4 * i + f - 3)
                            rows = slice(f * 128, (f + 1) * 128)
                            product_packed(pe, ps_u[:, f, :TB], lambda k: w1h[:, u, k, rows], w1l[:, u, rows],
                                           [x[:, tok] for x in packed]).then_inc(up_summed, 1)
                        if not (first and t < 2):
                            pe.wait_ge(wb_ready, i - 1)
                        pe.matmul(ps_w[:CP, t % 2, :TB], pick[:, u, :], w_rows[:, tok], start=True, stop=True).then_inc(wb_summed, 1)
                        if not (first and t == 0):
                            down(i - 1, (t - 1) % NT, u if t else 1 - u)
                    if last:
                        down(e * NT + NT - 1, NT - 1, u)

                for_all_experts(pe, body)

            @block.scalar
            def _(act):
                def body(e, u, first, last):
                    act.wait_ge(small_in[u], 48 * ((e - u) // 2 + 1) if isinstance(e, int) else 24 * (e - u) + 48)
                    for t in range(NT):
                        i = e * NT + t
                        for f in range(FB):
                            act.wait_ge(up_summed, 4 * i + f + 1)
                            if f == 0 and not (first and t < 2):
                                act.wait_ge(down_summed, 2 * i - 2)
                            act.activation(hh[:, t % 2, f, :], ps_u[:, f, :TB], ACT.Gelu, bias=b1[:, u, f:f + 1]).then_inc(hh_ready, 1)
                            if not (first and t == 0 and f < 2):
                                act.wait_ge(hl_ready, 4 * i + f - 1)
                            act.activation(h32[:, f % 2, :], ps_u[:, f, :TB], ACT.Gelu, bias=b1[:, u, f:f + 1]).then_inc(h32_ready, 1)
                        act.wait_ge(wb_summed, i + 1)
                        if not (first and t < 2):
                            act.wait_ge(y_ready, 2 * i - 2)
                        act.activation(wb[:, t % 2, :], ps_w[:CP, t % 2, :TB], ACT.Copy).then_inc(wb_ready, 1)

                for_all_experts(act, body)

            @block.vector
            def _(dve):
                def prepare(e, u):
                    if not isinstance(e, int) or e > 0:
                        dve.wait_ge(big_in, 32 * e)
                    split_packed(dve, w1[:, :, :], w1h[:, u, :, :], w1l[:, u, :], high_ready, low_ready, 2 * e)
                    dve.tensor_copy(w2h[:, u, :, :], w2[:, :, :]).then_inc(high_ready, 1)
                    dve.wait_ge(small_in[u], 48 * ((e - u) // 2 + 1) if isinstance(e, int) else 24 * (e - u) + 48)
                    dve.tensor_copy(pick[:, u, :], pick32[:, u, :]).then_inc(pick_ready, 1)
                    dve.wait_ge(high_ready, 2 * e + 2)
                    dve.tensor_tensor(w2l[:, u, :, :], w2[:, :, :], w2h[:, u, :, :].bitcast(f32), ALU.subtract).then_inc(low_ready, 1)

                def weigh(i, t, u):
                    dve.wait_ge(wb_ready, i + 1)
                    for m in range(CB):
                        dve.wait_ge(down_summed, 2 * i + m + 1)
                        if not (isinstance(i, int) and i < 2):
                            dve.wait_ge(x_added, 2 * i + m - 3)
                        dve.scalar_tensor_tensor(y[:, t % 2, m, :], ps_d[:CP, m, :TB], b2[:, u, m:m + 1], wb[:, t % 2, :],
                                                 ALU.add, ALU.mult).then_inc(y_ready, 1)

                def body(e, u, first, last):
                    for t in range(NT):
                        i = e * NT + t
                        for f in range(FB):
                            dve.wait_ge(h32_ready, 4 * i + f + 1)
                            dve.tensor_tensor(hl[:, t % 2, f, :], h32[:, f % 2, :], hh[:, t % 2, f, :].bitcast(f32),
                                              ALU.subtract).then_inc(hl_ready, 1)
                        if not (first and t == 0):
                            weigh(i - 1, (t - 1) % NT, u if t else 1 - u)
                        if t == 3 and not last:
                            prepare(e + 1, 1 - u)
                    if last:
                        weigh(e * NT + NT - 1, NT - 1, u)

                prepare(0, 0)
                for_all_experts(dve, body)

            @block.gpsimd
            def _(pool):
                def body(e, u, first, last):
                    for t in range(NT):
                        for m in range(CB):
                            pool.wait_ge(y_ready, (e * NT + t) * 2 + m + 1)
                            x = x_sb[:, m, t * TB:(t + 1) * TB]
                            pool.tensor_tensor(x, x, y[:, t % 2, m, :], ALU.add).then_inc(x_added, 1)

                for_all_experts(pool, body)
                pool.wait_ge(x_added, 2 * NT * E)


def shared_expert(nc, packed, w13, b13, w2, b2, x_sb, y_dram):
    with Scope(nc, "sh") as s:
        wh, wl = s.sb("wh", [128, 2, 2, F], f32r), s.sb("wl", [128, 2, F], f32r)
        w2h, w2l = s.sb("w2h", [128, FB, C], f32r), s.sb("w2l", [128, FB, C], f32r)
        g = s.sb("g", [128, 2, TB])
        h32 = s.sb("h32", [128, 2, TB])
        hh, hl = s.sb("hh", [128, 2, FB, TB], f32r), s.sb("hl", [128, 2, FB, TB], f32r)
        y = s.sb("y", [CP, 2, CB, TB])
        ps_1, ps_3, ps_d = s.ps("ps_1", 2), s.ps("ps_3", 2), s.ps("ps_d", 2)
        high_ready, low_ready = s.sem("high_ready"), s.sem("low_ready")
        summed1, summed3, g_ready, h32_ready = (s.sem(n) for n in ("summed1", "summed3", "g_ready", "h32_ready"))
        hh_ready, hl_ready, down_summed, y_ready = (s.sem(n) for n in ("hh_ready", "hl_ready", "down_summed", "y_ready"))
        stored = [s.sem("even_stored"), s.sem("odd_stored")]
        with nc.Block() as block:
            @block.sync
            def _(sp):
                for t in range(NT):
                    sp.wait_ge(y_ready, 2 * t + 2)
                    sp.dma_start(y_dram[:, :, t * TB:(t + 1) * TB], y[:, t % 2, :, :]).then_inc(stored[t % 2], 16)
                for slot in range(2):
                    sp.wait_ge(stored[slot], 8 * NT)

            @block.tensor
            def _(pe):
                def down(t):
                    pe.wait_ge(hh_ready, 4 * t + 4)
                    pe.wait_ge(hl_ready, 4 * t + 4)
                    for m in range(CB):
                        if t >= 1:
                            pe.wait_ge(y_ready, 2 * t + m - 1)
                        cols = slice(m * CP, (m + 1) * CP)
                        product3(pe, ps_d[:CP, m, :TB], lambda k: w2h[:, k, cols], lambda k: w2l[:, k, cols],
                                 lambda k: hh[:, t % 2, k, :], lambda k: hl[:, t % 2, k, :], blocks=FB).then_inc(down_summed, 1)

                pe.wait_ge(low_ready, 5)
                for t in range(NT):
                    tok = slice(t * TB, (t + 1) * TB)
                    for f in range(FB):
                        i = 4 * t + f
                        rows = slice(f * 128, (f + 1) * 128)
                        if i >= 2:
                            pe.wait_ge(h32_ready, i - 1)
                        for a, ps, done in ((0, ps_1, summed1), (1, ps_3, summed3)):
                            product_packed(pe, ps[:, i % 2, :TB], lambda k: wh[:, a, k, rows], wl[:, a, rows],
                                           [x[:, tok] for x in packed]).then_inc(done, 1)
                    if t >= 1:
                        down(t - 1)
                down(NT - 1)

            @block.scalar
            def _(act):
                for i in range(4 * NT + 1):
                    if i < 4 * NT:
                        act.wait_ge(summed1, i + 1)
                        if i >= 2:
                            act.wait_ge(h32_ready, i - 1)
                        act.activation(g[:, i % 2, :], ps_1[:, i % 2, :TB], ACT.Gelu, bias=b13[:, 0, i % 4:i % 4 + 1]).then_inc(g_ready, 1)
                    if i >= 1:
                        j = i - 1
                        t, f = j // 4, j % 4
                        act.wait_ge(h32_ready, j + 1)
                        if f == 0 and t >= 2:
                            act.wait_ge(down_summed, 2 * t - 2)
                        act.activation(hh[:, t % 2, f, :], h32[:, j % 2, :], ACT.Copy).then_inc(hh_ready, 1)

            @block.vector
            def _(dve):
                for a in range(2):
                    split_packed(dve, w13[:, a, :, :], wh[:, a, :, :], wl[:, a, :], high_ready, low_ready, a)
                dve.tensor_copy(w2h[:, :, :], w2[:, :, :]).then_inc(high_ready, 1)
                dve.wait_ge(high_ready, 3)
                dve.tensor_tensor(w2l[:, :, :], w2[:, :, :], w2h[:, :, :].bitcast(f32), ALU.subtract).then_inc(low_ready, 1)

                def finish(t):
                    for m in range(CB):
                        dve.wait_ge(down_summed, 2 * t + m + 1)
                        if m == 0 and t >= 2:
                            dve.wait_ge(stored[t % 2], 16 * (t // 2))
                        dve.scalar_tensor_tensor(y[:, t % 2, m, :], ps_d[:CP, m, :TB], b2[:, m:m + 1], x_sb[:, m, t * TB:(t + 1) * TB],
                                                 ALU.add, ALU.add).then_inc(y_ready, 1)

                for i in range(4 * NT + 1):
                    if i < 4 * NT:
                        dve.wait_ge(summed3, i + 1)
                        dve.wait_ge(g_ready, i + 1)
                        if i >= 2:
                            dve.wait_ge(hh_ready, i - 1)
                            dve.wait_ge(hl_ready, i - 1)
                        dve.scalar_tensor_tensor(h32[:, i % 2, :], ps_3[:, i % 2, :TB], b13[:, 1, i % 4:i % 4 + 1], g[:, i % 2, :],
                                                 ALU.add, ALU.mult).then_inc(h32_ready, 1)
                    if i >= 1:
                        j = i - 1
                        t, f = j // 4, j % 4
                        dve.wait_ge(hh_ready, j + 1)
                        dve.tensor_tensor(hl[:, t % 2, f, :], h32[:, j % 2, :], hh[:, t % 2, f, :].bitcast(f32),
                                          ALU.subtract).then_inc(hl_ready, 1)
                        if f == 3 and t >= 1:
                            finish(t - 1)
                finish(NT - 1)


def experts_layer(nc, ins, x_in, y_out):
    with Scope(nc, "l2") as s:
        x_sb = s.sb("x", [CP, CB, N])
        packed = [s.sb(n, [128, N], f32r) for n in ("xa", "xb", "la", "lb")]
        w_rows = s.sb("w_rows", [2 * E, N], f32r)
        w1, w2 = s.sb("w1", [128, 2, F]), s.sb("w2", [128, FB, C])
        w13, w2s = s.sb("w13", [128, 2, 2, F]), s.sb("w2s", [128, FB, C])
        b13, b2 = s.sb("b13", [128, 2, FB]), s.sb("b2", [CP, CB])
        with Scope(nc, "l2n") as s2:
            xh, xl = s2.sb("xh", [CP, CB, N], f32r), s2.sb("xl", [CP, CB, N], f32r)
            route(nc, x_in, ins["group_avg"], x_sb, xh, xl, packed, ins["gate"], ins["first"], ins["ident98"], w_rows,
                  [(w1[:, :, :], ins["fc1"][0]), (w2[:, :, :], ins["fc2"][0])])
        experts(nc, packed, w_rows, w1, w2, ins["fc1"], ins["fc1_b"], ins["fc2"], ins["fc2_b"], ins["pick"], x_sb,
                [(w13[:, :, :, :], ins["w13"]), (w2s[:, :, :], ins["w2"]), (b13[:, :, :], ins["b13"]), (b2[:, :], ins["w2_b"])])
        shared_expert(nc, packed, w13, b13, w2s, b2, x_sb, y_out)


def build(nc, ins, out):
    shapes = {"x1": [CP, CB, N], "x2": [CP, CB, N], "x3": [CP, CB, N], "products": [HEADS, 32, N], "sums": [HEADS, N]}
    scratch = {n: nc.dram_tensor(n, shape, f32, kind="Internal").ap() for n, shape in shapes.items()}
    gru_layer(nc, ins, ins["x"], scratch["x1"])
    attention_layer(nc, "l1", ins, scratch["x1"], scratch["x2"], scratch)
    experts_layer(nc, ins, scratch["x2"], scratch["x3"])
    attention_layer(nc, "l3", ins, scratch["x3"], out, scratch)


def selectors():
    k = np.arange(T)
    sel = np.zeros((128, T), np.float32)
    for row in (32, 96):
        sel[row:row + H] = (k // W)[None] == np.arange(H)[:, None]
        sel[row + H:row + H + W] = (k % W)[None] == np.arange(W)[:, None]
    sel[64:66] = -1.0
    signs = np.repeat(np.array([[-1, 0], [1, 1], [-HD ** -0.5, 0], [HD ** -0.5, HD ** -0.5]], np.float32), 16, 0)
    return sel, np.tile(signs, (2, 1))


def lay_out_attention(tag, wqkv, bqkv, wo, bo, rel_h, rel_w):
    o = {}
    rows = wqkv.reshape(C, 3, PAIRS, 2, HD)
    cols = [rows[:, part, :, head] for head in range(2) for part in (0, 0, 1, 1)]
    wqk = np.zeros((CP + 1, PAIRS, CB, 128), np.float32)
    wqk[:CP] = np.stack(cols, 2).reshape(CB, CP, PAIRS, 128).transpose(1, 2, 0, 3)
    b = bqkv.reshape(3, PAIRS, 2, HD)
    wqk[CP, :, 0] = np.stack([b[part, :, head] for head in range(2) for part in (0, 0, 1, 1)], 1).reshape(PAIRS, 128)
    o["_wqk"] = wqk
    o["_wv"] = np.ascontiguousarray(wqkv[:, 2 * C:].reshape(CB, CP, C).transpose(1, 0, 2))
    o["_bv"] = np.ascontiguousarray(np.broadcast_to(bqkv[2 * C:], (TH, C)))
    r = np.zeros((2, 4, HD, H + W, 2, H), np.float32)
    for n in range(H):
        for a, table in ((0, rel_h), (H, rel_w)):
            seen = table[n:n + H][::-1].T
            for head in range(2):
                r[head, 0:2, :, a + n, head, :] = seen
    o["_rel"] = r.reshape(128, H + W, 2 * H)
    w = wo.reshape(PAIRS // 2, 2, 2, 1, HD, C)
    o["_wo"] = np.ascontiguousarray(np.broadcast_to(w, (3, 2, 2, 2, HD, C)).reshape(3, 128, CB, CP).transpose(1, 0, 2, 3))
    o["_bo"] = np.ascontiguousarray(bo.reshape(CB, CP).T)
    return {tag + k: v for k, v in o.items()}


def channels(a):
    a = np.asarray(a)
    return np.ascontiguousarray(np.moveaxis(a.reshape(*a.shape[:-1], CB, CP), (-1, -2), (0, 1)))


def twice(a):
    return np.stack([a[..., :128], np.concatenate([a[..., 128:], a[..., 128:]], -1)], -2)


def lay_out(i):
    a = {k: np.asarray(v) for k, v in i.items()}
    o = {}
    o["x"] = channels(a["x"].reshape(N, C))
    o["group_avg"] = np.kron(np.eye(CP // GC), np.full((GC, GC), 1.0 / GC)).astype(np.float32)
    o["ident128"] = np.eye(128, dtype=np.float32)
    o["wx"] = channels(twice(a["L0_conv_Wx"].reshape(3, C, C).transpose(2, 0, 1)).reshape(C, 6, 128).transpose(1, 2, 0))
    o["bx"] = np.ascontiguousarray(twice(a["L0_conv_bx"].reshape(3, C)).reshape(6, 128).T)
    o["bh"] = np.ascontiguousarray(twice(a["L0_conv_bh"].reshape(3, C)).reshape(6, 128).T)
    o["bhn"] = np.ascontiguousarray(twice(a["L0_conv_bh"][2 * C:]).T)
    wh = twice(a["L0_conv_Wh"].reshape(3, C, C).transpose(2, 0, 1))
    o["wh"] = np.ascontiguousarray(np.moveaxis(twice(np.moveaxis(wh, 0, -1)), (-1, -2), (0, 1)))
    o["wp"] = np.ascontiguousarray(a["L0_conv_Wp"].T.reshape(C, CB, CP))
    o["sel"], o["signs"] = selectors()
    o["ident98"] = np.eye(TH, dtype=np.float32)
    o.update(lay_out_attention("l1", a["L1_conv_qkv_w"], a["L1_conv_qkv_b"], a["L1_conv_proj_w"], a["L1_conv_proj_b"],
                               a["L1_conv_rel_pos_h"], a["L1_conv_rel_pos_w"]))
    o.update(lay_out_attention("l3", a["L3_conv_qkv_w"].T, a["L3_conv_qkv_b"], a["L3_conv_proj_w"].T, a["L3_conv_proj_b"],
                               a["L3_conv_rel_pos_h"], a["L3_conv_rel_pos_w"]))
    o["gate"] = channels(a["L2_conv_gate_w"])
    o["first"] = np.ascontiguousarray(np.broadcast_to(np.arange(E, 0, -1, dtype=np.float32), (TH, E)))
    o["fc1"] = np.ascontiguousarray(twice(a["L2_conv_fc1_w"]).transpose(0, 3, 2, 1))
    o["fc1_b"] = np.ascontiguousarray(a["L2_conv_fc1_b"].reshape(E, FB, 128).transpose(0, 2, 1))
    o["fc2"] = np.ascontiguousarray(a["L2_conv_fc2_w"].reshape(E, C, FB, 128).transpose(0, 3, 2, 1))
    o["fc2_b"] = np.ascontiguousarray(a["L2_conv_fc2_b"].reshape(E, CB, CP).transpose(0, 2, 1))
    o["pick"] = np.ascontiguousarray(np.broadcast_to(np.tile(np.eye(E, dtype=np.float32), (1, 2))[:, :, None], (E, 2 * E, CP)))
    o["w13"] = np.ascontiguousarray(twice(np.stack([a["L2_conv_w1_w"], a["L2_conv_w3_w"]])).transpose(3, 0, 2, 1))
    o["b13"] = np.ascontiguousarray(np.stack([a["L2_conv_w1_b"], a["L2_conv_w3_b"]]).reshape(2, FB, 128).transpose(2, 0, 1))
    o["w2"] = np.ascontiguousarray(a["L2_conv_w2_w"].reshape(C, FB, 128).transpose(2, 1, 0))
    o["w2_b"] = np.ascontiguousarray(a["L2_conv_w2_b"].reshape(CB, CP).T)
    return o


def back(y):
    return np.ascontiguousarray(y.transpose(2, 1, 0).reshape(B, H, W, C))


_BUILT_OUT = "out_0_dram"


def kernel(**inputs):
    import concourse.bacc as _bacc
    from concourse.bass_utils import run_bass_kernel_spmd as _run

    nc = _bacc.Bacc("TRN2", target_bir_lowering=False, num_devices=1)
    arrays = {f"in_{k}_dram": v for k, v in lay_out(inputs).items()}
    ins = {k[3:-5]: nc.dram_tensor(k, v.shape, mybir.dt.from_np(v.dtype), kind="ExternalInput").ap() for k, v in arrays.items()}
    out = nc.dram_tensor(_BUILT_OUT, [CP, CB, N], f32, kind="ExternalOutput").ap()
    build(nc, ins, out)
    r = _run(nc, [arrays], core_ids=[0])
    return back(r.results[0][_BUILT_OUT])
```
